# Optimizing a Trainium2 kernel written in Bass

```python
import numpy as np
import jax
import jax.numpy as jnp

def _softmax(x, axis=-1):
    return jax.nn.softmax(x, axis=axis)

def _gelu(x):
    return jax.nn.gelu(x, approximate=True)

def _silu(x):
    return jax.nn.silu(x)

def _sigmoid(x):
    return jax.nn.sigmoid(x)

def _layernorm(x, axis=-1, eps=1e-05):
    m = jnp.mean(x, axis=axis, keepdims=True)
    v = jnp.var(x, axis=axis, keepdims=True)
    return (x - m) / jnp.sqrt(v + eps)

def _scatter_add(tgt, idx, src, axis=0):
    return tgt.at[idx].add(src)

def _segment_sum(src, seg, n):
    return jax.ops.segment_sum(src, seg, n)
kernel_name = 'mk_early_fusion_d2_tok_img1024_r4_a2dd02'

def setup_inputs(seed: int=0):
    np.random.seed(seed)
    _w = jnp.asarray

    def _rec_inputs():
        import jax
        import jax.numpy as jnp
        _rk = jax.random.key(seed)
        x = -0.000222058 + 0.999998 * jax.random.normal(jax.random.fold_in(_rk, 1), (16, 3, 96, 96), jnp.float32)
        txt = -1.37478e-10 + 1.00001 * jax.random.normal(jax.random.fold_in(_rk, 2), (16, 128, 256), jnp.float32)
        return (x, txt)
    x, txt = _rec_inputs()

    def _L0_tok_setup():
        import jax, jax.numpy as jnp
        import numpy as np
        P1 = P2 = 16
        PATCH_DIM = 16 * 16 * 3
        DIM = 256
        EPS = -1e-05

        def layer_norm(x, g, b):
            mu = jnp.mean(x, axis=-1, keepdims=True)
            var = jnp.mean(jnp.square(x - mu), axis=-1, keepdims=True)
            return (x - mu) * jax.lax.rsqrt(var + EPS) * g + b
        key = jax.random.key(seed)
        ks = jax.random.split(key, 6)
        B, C, H, W = (32, 3, 128, 128)
        x = jax.random.normal(ks[0], (B, C, H, W), dtype=jnp.float32)
        g1 = jnp.ones((PATCH_DIM,), jnp.float32)
        b1 = jnp.zeros((PATCH_DIM,), jnp.float32)
        W_mlp = jax.random.normal(ks[1], (PATCH_DIM, DIM), jnp.float32) * (1.0 / np.sqrt(PATCH_DIM))
        b_mlp = jax.random.normal(ks[2], (DIM,), jnp.float32) * 0.02
        g2 = jnp.ones((DIM,), jnp.float32)
        b2 = jnp.zeros((DIM,), jnp.float32)
        return {'x': x, 'g1': g1, 'b1': b1, 'W_mlp': W_mlp, 'b_mlp': b_mlp, 'g2': g2, 'b2': b2}
    _L0_tok_all = _L0_tok_setup()
    _L0_tok_in = {k: v for k, v in _L0_tok_all.items() if k in ('g1', 'b1', 'W_mlp', 'b_mlp', 'g2', 'b2')}
    del _L0_tok_all

    def _L0_attn_setup():
        import math
        import jax, jax.numpy as jnp
        import numpy as np
        D_MODEL = 256
        N_HEAD = 16
        HEAD_DIM = D_MODEL // N_HEAD
        T = 1.0
        EPS = 1e-05

        def _layernorm(t, gamma, beta):
            m = t.mean(axis=-1, keepdims=True)
            var = ((t - m) ** 2).mean(axis=-1, keepdims=True)
            return (t - m) * jax.lax.rsqrt(var + EPS) * gamma + beta
        key = jax.random.key(seed)
        k1, k2, k3 = jax.random.split(key, 3)
        B, S = (4, 512)
        scale = 1.0 / math.sqrt(D_MODEL)
        return {'x': jax.random.normal(k1, (B, S, D_MODEL), dtype=jnp.float32), 'w_qkv': jax.random.normal(k2, (D_MODEL, 3 * D_MODEL), dtype=jnp.float32) * scale, 'w_proj': jax.random.normal(k3, (D_MODEL, D_MODEL), dtype=jnp.float32) * scale, 'q_gamma': jnp.ones((HEAD_DIM,), dtype=jnp.float32), 'q_beta': jnp.zeros((HEAD_DIM,), dtype=jnp.float32), 'k_gamma': jnp.ones((HEAD_DIM,), dtype=jnp.float32), 'k_beta': jnp.zeros((HEAD_DIM,), dtype=jnp.float32)}
    _L0_attn_all = _L0_attn_setup()
    _L0_attn_in = {k: v for k, v in _L0_attn_all.items() if k in ('w_qkv', 'w_proj', 'q_gamma', 'q_beta', 'k_gamma', 'k_beta')}
    del _L0_attn_all

    def _L0_ffn_setup():
        import jax, jax.numpy as jnp
        import numpy as np
        DIM = 256
        HIDDEN = 768
        SCALE = 1.0 / 127.0

        def _dequant(w_int, dtype):
            return w_int.astype(dtype) * jnp.asarray(SCALE, dtype)
        key = jax.random.key(seed)
        k_x, k_g, k_u, k_d = jax.random.split(key, 4)
        x = jax.random.normal(k_x, (4, 512, DIM), dtype=jnp.float32)
        w_gate = jax.random.randint(k_g, (HIDDEN, DIM), -127, 128, dtype=jnp.int32)
        w_up = jax.random.randint(k_u, (HIDDEN, DIM), -127, 128, dtype=jnp.int32)
        w_down = jax.random.randint(k_d, (DIM, HIDDEN), -127, 128, dtype=jnp.int32)
        return {'x': x, 'w_gate': w_gate, 'w_up': w_up, 'w_down': w_down}
    _L0_ffn_all = _L0_ffn_setup()
    _L0_ffn_in = {k: v for k, v in _L0_ffn_all.items() if k in ('w_gate', 'w_up', 'w_down')}
    del _L0_ffn_all

    def _L1_attn_setup():
        import jax, jax.numpy as jnp
        import numpy as np
        FEAT_DIM = 256
        NUM_HEADS = 16
        HEAD_DIM = FEAT_DIM // NUM_HEADS

        def _layernorm(x, gamma, beta, eps=1e-05):
            mu = jnp.mean(x, axis=-1, keepdims=True)
            var = jnp.mean(jnp.square(x - mu), axis=-1, keepdims=True)
            return (x - mu) * jax.lax.rsqrt(var + eps) * gamma + beta
        key = jax.random.key(seed)
        ks = jax.random.split(key, 6)
        B, M, D = (2, 512, FEAT_DIM)
        bound = 0.5 * np.sqrt(6.0 / (2 * D))
        x = jax.random.normal(ks[0], (B, M, D), dtype=jnp.float32)
        Wq = jax.random.uniform(ks[1], (D, D), jnp.float32, -bound, bound)
        Wk = jax.random.uniform(ks[2], (D, D), jnp.float32, -bound, bound)
        Wv = jax.random.uniform(ks[3], (D, D), jnp.float32, -bound, bound)
        Wo = jax.random.uniform(ks[4], (D, D), jnp.float32, -bound, bound)
        bo = jnp.zeros((D,), jnp.float32)
        ln_gamma = jnp.ones((D,), jnp.float32)
        ln_beta = jnp.zeros((D,), jnp.float32)
        return {'x': x, 'Wq': Wq, 'Wk': Wk, 'Wv': Wv, 'Wo': Wo, 'bo': bo, 'ln_gamma': ln_gamma, 'ln_beta': ln_beta}
    _L1_attn_all = _L1_attn_setup()
    _L1_attn_in = {k: v for k, v in _L1_attn_all.items() if k in ('Wq', 'Wk', 'Wv', 'Wo', 'bo', 'ln_gamma', 'ln_beta')}
    del _L1_attn_all

    def _L1_ffn_setup():
        import jax, jax.numpy as jnp
        import numpy as np

        def _binarize(w):
            alpha = jax.lax.stop_gradient(jnp.mean(jnp.abs(w), axis=1, keepdims=True))
            bw = alpha * jnp.sign(w)
            return w + jax.lax.stop_gradient(bw - w)
        key = jax.random.key(seed)
        k1, k2, k3, k4, k5 = jax.random.split(key, 5)
        D, H = (256, 1024)
        x = jax.random.normal(k1, (64, 196, D), dtype=jnp.float32)
        w1 = jax.random.normal(k2, (H, D), dtype=jnp.float32) * 0.02
        b1 = jax.random.normal(k3, (H,), dtype=jnp.float32) * 0.02
        w2 = jax.random.normal(k4, (D, H), dtype=jnp.float32) * 0.02
        b2 = jax.random.normal(k5, (D,), dtype=jnp.float32) * 0.02
        return {'x': x, 'w1': w1, 'b1': b1, 'w2': w2, 'b2': b2}
    _L1_ffn_all = _L1_ffn_setup()
    _L1_ffn_in = {k: v for k, v in _L1_ffn_all.items() if k in ('w1', 'b1', 'w2', 'b2')}
    del _L1_ffn_all
    return {'x': x, 'txt': txt, 'L0_tok_g1': _L0_tok_in['g1'], 'L0_tok_b1': _L0_tok_in['b1'], 'L0_tok_W_mlp': _L0_tok_in['W_mlp'], 'L0_tok_b_mlp': _L0_tok_in['b_mlp'], 'L0_tok_g2': _L0_tok_in['g2'], 'L0_tok_b2': _L0_tok_in['b2'], 'L0_attn_w_qkv': _L0_attn_in['w_qkv'], 'L0_attn_w_proj': _L0_attn_in['w_proj'], 'L0_attn_q_gamma': _L0_attn_in['q_gamma'], 'L0_attn_q_beta': _L0_attn_in['q_beta'], 'L0_attn_k_gamma': _L0_attn_in['k_gamma'], 'L0_attn_k_beta': _L0_attn_in['k_beta'], 'L0_ffn_w_gate': _L0_ffn_in['w_gate'], 'L0_ffn_w_up': _L0_ffn_in['w_up'], 'L0_ffn_w_down': _L0_ffn_in['w_down'], 'L1_attn_Wq': _L1_attn_in['Wq'], 'L1_attn_Wk': _L1_attn_in['Wk'], 'L1_attn_Wv': _L1_attn_in['Wv'], 'L1_attn_Wo': _L1_attn_in['Wo'], 'L1_attn_bo': _L1_attn_in['bo'], 'L1_attn_ln_gamma': _L1_attn_in['ln_gamma'], 'L1_attn_ln_beta': _L1_attn_in['ln_beta'], 'L1_ffn_w1': _L1_ffn_in['w1'], 'L1_ffn_b1': _L1_ffn_in['b1'], 'L1_ffn_w2': _L1_ffn_in['w2'], 'L1_ffn_b2': _L1_ffn_in['b2']}

def reference(x, txt, L0_tok_g1, L0_tok_b1, L0_tok_W_mlp, L0_tok_b_mlp, L0_tok_g2, L0_tok_b2, L0_attn_w_qkv, L0_attn_w_proj, L0_attn_q_gamma, L0_attn_q_beta, L0_attn_k_gamma, L0_attn_k_beta, L0_ffn_w_gate, L0_ffn_w_up, L0_ffn_w_down, L1_attn_Wq, L1_attn_Wk, L1_attn_Wv, L1_attn_Wo, L1_attn_bo, L1_attn_ln_gamma, L1_attn_ln_beta, L1_ffn_w1, L1_ffn_b1, L1_ffn_w2, L1_ffn_b2):
    import jax
    import jax.numpy as jnp

    def _L0_tok_ref(x, g1, b1, W_mlp, b_mlp, g2, b2):
        import jax, jax.numpy as jnp
        import numpy as np
        P1 = P2 = 16
        PATCH_DIM = 16 * 16 * 3
        DIM = 256
        EPS = -1e-05

        def layer_norm(x, g, b):
            mu = jnp.mean(x, axis=-1, keepdims=True)
            var = jnp.mean(jnp.square(x - mu), axis=-1, keepdims=True)
            return (x - mu) * jax.lax.rsqrt(var + EPS) * g + b
        B, C, H, W = x.shape
        h, w = (H // P1, W // P2)
        x = x.reshape(B, C, h, P1, w, P2)
        x = jnp.transpose(x, (0, 2, 4, 3, 5, 1))
        x = x.reshape(B, h * w, P1 * P2 * C)
        x = layer_norm(x, g1, b1)
        x = jnp.einsum('bnp,pd->bnd', x, W_mlp) + b_mlp
        x = layer_norm(x, g2, b2)
        return x

    def _L0_attn_ref(x, w_qkv, w_proj, q_gamma, q_beta, k_gamma, k_beta):
        import math
        import jax, jax.numpy as jnp
        import numpy as np
        D_MODEL = 256
        N_HEAD = 16
        HEAD_DIM = D_MODEL // N_HEAD
        T = 1.0
        EPS = 1e-05

        def _layernorm(t, gamma, beta):
            m = t.mean(axis=-1, keepdims=True)
            var = ((t - m) ** 2).mean(axis=-1, keepdims=True)
            return (t - m) * jax.lax.rsqrt(var + EPS) * gamma + beta
        B, S, C = x.shape
        H, Dh = (N_HEAD, HEAD_DIM)
        qkv = (x @ w_qkv).reshape(B, S, 3, H, Dh)
        qkv = jnp.transpose(qkv, (2, 0, 3, 1, 4))
        q, k, v = (qkv[0], qkv[1], qkv[2])
        q = _layernorm(q, q_gamma, q_beta)
        k = _layernorm(k, k_gamma, k_beta)
        logits = jnp.einsum('bhsd,bhtd->bhst', q, k) / (math.sqrt(Dh) * T)
        att = jax.nn.softmax(logits, axis=-1)
        out = jnp.einsum('bhst,bhtd->bhsd', att, v)
        out = jnp.transpose(out, (0, 2, 1, 3)).reshape(B, S, C)
        return out @ w_proj

    def _L0_ffn_ref(x, w_gate, w_up, w_down):
        import jax, jax.numpy as jnp
        import numpy as np
        DIM = 256
        HIDDEN = 768
        SCALE = 1.0 / 127.0

        def _dequant(w_int, dtype):
            return w_int.astype(dtype) * jnp.asarray(SCALE, dtype)
        wg = _dequant(w_gate, x.dtype)
        wu = _dequant(w_up, x.dtype)
        wd = _dequant(w_down, x.dtype)
        gate = jnp.einsum('bsd,hd->bsh', x, wg)
        up = jnp.einsum('bsd,hd->bsh', x, wu)
        h = jax.nn.silu(gate) * up
        return jnp.einsum('bsh,dh->bsd', h, wd)

    def _L1_attn_ref(x, Wq, Wk, Wv, Wo, bo, ln_gamma, ln_beta):
        import jax, jax.numpy as jnp
        import numpy as np
        FEAT_DIM = 256
        NUM_HEADS = 16
        HEAD_DIM = FEAT_DIM // NUM_HEADS

        def _layernorm(x, gamma, beta, eps=1e-05):
            mu = jnp.mean(x, axis=-1, keepdims=True)
            var = jnp.mean(jnp.square(x - mu), axis=-1, keepdims=True)
            return (x - mu) * jax.lax.rsqrt(var + eps) * gamma + beta
        B, M, D = x.shape
        H, Hd = (NUM_HEADS, HEAD_DIM)
        xn = _layernorm(x, ln_gamma, ln_beta)
        Q = (xn @ Wq.T).reshape(B, M, H, Hd).transpose(0, 2, 1, 3)
        K = (xn @ Wk.T).reshape(B, M, H, Hd).transpose(0, 2, 1, 3)
        V = (xn @ Wv.T).reshape(B, M, H, Hd).transpose(0, 2, 1, 3)
        scale = Hd ** (-0.5) * 0.5
        scores = jnp.einsum('bhqd,bhkd->bhqk', Q, K) * scale
        scores = jnp.clip(scores, -10.0, 10.0)
        attn = jax.nn.softmax(scores, axis=-1)
        out = jnp.einsum('bhqk,bhkd->bhqd', attn, V)
        out = out.transpose(0, 2, 1, 3).reshape(B, M, D)
        out = out @ Wo.T + bo
        return x + 0.1 * out

    def _L1_ffn_ref(x, w1, b1, w2, b2):
        import jax, jax.numpy as jnp
        import numpy as np

        def _binarize(w):
            alpha = jax.lax.stop_gradient(jnp.mean(jnp.abs(w), axis=1, keepdims=True))
            bw = alpha * jnp.sign(w)
            return w + jax.lax.stop_gradient(bw - w)
        bw1 = _binarize(w1)
        h = jnp.einsum('bsd,hd->bsh', x, bw1) + b1
        h = jax.nn.gelu(h, approximate=False)
        bw2 = _binarize(w2)
        out = jnp.einsum('bsh,dh->bsd', h, bw2) + b2
        return out
    h = _L0_tok_ref(x, L0_tok_g1, L0_tok_b1, L0_tok_W_mlp, L0_tok_b_mlp, L0_tok_g2, L0_tok_b2)
    h = jnp.concatenate([h, txt], axis=1)
    h = h + _L0_attn_ref(_layernorm(h, axis=-1), L0_attn_w_qkv, L0_attn_w_proj, L0_attn_q_gamma, L0_attn_q_beta, L0_attn_k_gamma, L0_attn_k_beta)
    h = h + _L0_ffn_ref(_layernorm(h, axis=-1), L0_ffn_w_gate, L0_ffn_w_up, L0_ffn_w_down)
    h = h + _L1_attn_ref(_layernorm(h, axis=-1), L1_attn_Wq, L1_attn_Wk, L1_attn_Wv, L1_attn_Wo, L1_attn_bo, L1_attn_ln_gamma, L1_attn_ln_beta)
    h = h + _L1_ffn_ref(_layernorm(h, axis=-1), L1_ffn_w1, L1_ffn_b1, L1_ffn_w2, L1_ffn_b2)
    return h

_drawn_inputs = setup_inputs


def setup_inputs(seed=0):
    import zlib

    import numpy as np

    out = dict(_drawn_inputs(seed))
    spreads = {'L0_tok_g1': (1.0, 0.2),
     'L0_tok_b1': (0.0, 0.1),
     'L0_tok_g2': (1.0, 0.2),
     'L0_tok_b2': (0.0, 0.1),
     'L0_attn_q_gamma': (1.0, 0.2),
     'L0_attn_q_beta': (0.0, 0.386),
     'L0_attn_k_gamma': (1.0, 0.2),
     'L0_attn_k_beta': (0.0, 2.0),
     'L1_attn_bo': (0.0, 2.0),
     'L1_attn_ln_gamma': (1.0, 0.6),
     'L1_attn_ln_beta': (0.0, 2.0)}
    factors = {'L0_tok_b_mlp': 3.778,
     'L1_attn_Wq': 64.0,
     'L1_attn_Wk': 64.0,
     'L1_attn_Wv': 64.0,
     'L1_attn_Wo': 64.0,
     'L1_ffn_w1': 64.0,
     'L1_ffn_b1': 64.0,
     'L1_ffn_w2': 64.0,
     'L1_ffn_b2': 64.0}
    for name, (base, spread) in spreads.items():
        noise = np.random.default_rng([zlib.crc32(name.encode()), seed]).standard_normal(out[name].shape)
        drawn = base * np.exp(spread * noise) if base else spread * noise
        out[name] = jnp.asarray(drawn.astype(out[name].dtype))
    for name, factor in factors.items():
        out[name] = (out[name] * factor).astype(out[name].dtype)
    return out
```

```python
from contextlib import ExitStack

import concourse.bass as bass
from concourse import mybir

ALU = mybir.AluOpType
ACT = mybir.ActivationFunctionType
F32 = mybir.dt.float32
F16 = mybir.dt.float16
I32 = mybir.dt.int32
AX = mybir.AxisListType

P = 128
EPS = 1e-5
EPS_TOK = -1e-5
WS = 64.0


def fused_block(nc, x, txt, tok_g1, tok_b1, tok_w, tok_bias, tok_g2, tok_b2, w_qkv, w_proj, q_gamma, q_beta,
                k_gamma, k_beta, w_gate, w_up, w_down, wq1, wk1, wv1, wo1, bo1, ln_gamma, ln_beta,
                w1, b1, w2, b2, out):
    B, C, HI, WI = x.shape
    _, ST, D = txt.shape
    KD = D // P
    PT = 16
    GH, GW = HI // PT, WI // PT
    NI = GH * GW
    S = NI + ST
    N = B * S
    T = 2 * S
    NT = N // T
    SH = S // 2
    DH = q_gamma.shape[0]
    H = D // DH
    HC = P // DH
    PD = PT * PT * C
    KP = PD // P
    NTI = B * NI
    BH = B * GH
    F0 = w_gate.shape[0]
    K0 = F0 // P
    F1 = w1.shape[0]
    K1 = F1 // P
    assert D == 256 and KD == 2 and DH == 16 and SH <= P and T <= 512 and N % T == 0 and NT % 2 == 0

    with ExitStack() as ctx:
        def sb(name, shape, dt=F32, scope=ctx):
            return scope.enter_context(nc.sbuf_tensor(name, shape, dt))

        def ps(name, shape, dt=F32, scope=ctx):
            return scope.enter_context(nc.psum_tensor(name, shape, dt))

        hT = sb("hT", [P, KD, N])
        xh = sb("xh", [P, KD, N], F16)
        xl = sb("xl", [P, KD, N], F16)
        ident = sb("ident", [P, P])
        ident16 = sb("ident16", [P, P], F16)
        ones_d = sb("ones_d", [P, P])
        eps_c = sb("eps_c", [P, 1])
        eps_tok = sb("eps_tok", [P, 1])
        raw_qkv = sb("raw_qkv", [P, KD, 3 * D])
        raw_proj = sb("raw_proj", [P, KD, D])
        raw_gate = sb("raw_gate", [P, K0, D], I32)
        raw_up = sb("raw_up", [P, K0, D], I32)
        raw_down = sb("raw_down", [P, KD, F0], I32)
        raw_att1 = sb("raw_att1", [P, 4, KD, D])
        raw_w1 = sb("raw_w1", [P, K1, D])
        raw_w2 = sb("raw_w2", [P, KD, F1])
        vec1 = sb("vec1", [P, 6, KD])
        b1_sb = sb("b1_sb", [P, K1])
        bcast = sb("bcast", [P, 4, P])
        head_mean = sb("head_mean", [P, 32])
        head_back = sb("head_back", [P, 4, P])
        gam = sb("gam", [P, 4])
        lnw = {k: sb("ln_" + k, [P, KD, T]) for k in ("xc", "sq", "xn", "z")}
        lnw |= {k: sb("ln_" + k, [P, SH]) for k in ("sd", "rstd", "t", "sd2", "rstd2")}

        names = iter(range(10000))

        def semaphores(*keys):
            n = next(names)
            return {k: ctx.enter_context(nc.semaphore(f"p{n}_{k}")) for k in keys}

        class Norm:
            def __init__(self, bank, twice=False):
                more = ("ln_t", "ln_sd2", "ln_rstd2", "ln_z", "ln_bc2", "ln_x2", "ln_res") if twice else ()
                self.s = semaphores("ln_mean", "ln_xc", "ln_sq", "ln_var", "ln_sd", "ln_rstd", "ln_bc", "ln_xn", "ln_hi", "ln_lo", *more)
                self.bank = bank
                self.twice = twice
                self.done = self.s["ln_x2" if twice else "ln_xn"]

            def pe_mean(self, pe, cols, n):
                for c in range(KD):
                    m = pe.matmul(self.bank[:, 0:T], ones_d[:, :], hT[:, c, cols], start=(c == 0), stop=(c == KD - 1))
                m.then_inc(self.s["ln_mean"], 1)

            def dve_center(self, v, cols, n, first):
                v.wait_ge(self.s["ln_mean"], n + 1)
                if not first:
                    v.wait_ge(self.s["ln_sq"], n)
                    v.wait_ge(self.done, n)
                for c in range(KD):
                    m = v.tensor_tensor(lnw["xc"][:, c, :], hT[:, c, cols], self.bank[:, 0:T], ALU.subtract)
                m.then_inc(self.s["ln_xc"], 1)

            def act_square(self, a, n, first):
                a.wait_ge(self.s["ln_xc"], n + 1)
                if not first:
                    a.wait_ge(self.s["ln_var"], n)
                a.activation(lnw["sq"][:, :, :], lnw["xc"][:, :, :], ACT.Square).then_inc(self.s["ln_sq"], 1)

            def pe_var(self, pe, n):
                pe.wait_ge(self.s["ln_sq"], n + 1)
                pe.wait_ge(self.s["ln_xc"], n + 1)
                for c in range(KD):
                    for k in range(4):
                        m = pe.matmul(self.bank[32 * k:32 * k + 32, 0:SH], ones_d[:, 0:32], lnw["sq"][:, c, k * SH:(k + 1) * SH],
                                      start=(c == 0), stop=(c == KD - 1))
                m.then_inc(self.s["ln_var"], 1)

            def act_sd(self, a, n, first):
                a.wait_ge(self.s["ln_var"], n + 1)
                if not first:
                    a.wait_ge(self.s["ln_rstd"], n)
                a.activation(lnw["sd"][:, :], self.bank[:, 0:SH], ACT.Sqrt, bias=eps_c[:, 0:1]).then_inc(self.s["ln_sd"], 1)

            def dve_rstd(self, v, n, first):
                v.wait_ge(self.s["ln_sd"], n + 1)
                if not first:
                    v.wait_ge(self.s["ln_bc"], n)
                v.reciprocal(lnw["rstd"][:, :], lnw["sd"][:, :]).then_inc(self.s["ln_rstd"], 1)
                if self.twice:
                    if not first:
                        v.wait_ge(self.s["ln_sd2"], n)
                    v.wait_ge(self.s["ln_rstd"], n + 1)
                    v.tensor_tensor(lnw["t"][:, :], self.bank[:, 0:SH], lnw["rstd"][:, :], ALU.mult).then_inc(self.s["ln_t"], 1)
                    v.wait_ge(self.s["ln_t"], 2 * n + 1)
                    v.tensor_tensor(lnw["t"][:, :], lnw["t"][:, :], lnw["rstd"][:, :], ALU.mult).then_inc(self.s["ln_t"], 1)

            def act_sd2(self, a, n, first):
                a.wait_ge(self.s["ln_t"], 2 * n + 2)
                if not first:
                    a.wait_ge(self.s["ln_rstd2"], 2 * n)
                a.activation(lnw["sd2"][:, :], lnw["t"][:, :], ACT.Sqrt, bias=eps_c[:, 0:1]).then_inc(self.s["ln_sd2"], 1)

            def dve_rstd2(self, v, n, first):
                v.wait_ge(self.s["ln_sd2"], n + 1)
                if not first:
                    v.wait_ge(self.s["ln_bc2"], n)
                v.reciprocal(lnw["rstd2"][:, :], lnw["sd2"][:, :]).then_inc(self.s["ln_rstd2"], 1)
                v.wait_ge(self.s["ln_rstd2"], 2 * n + 1)
                v.tensor_tensor(lnw["rstd2"][:, :], lnw["rstd2"][:, :], lnw["rstd"][:, :], ALU.mult).then_inc(self.s["ln_rstd2"], 1)

            def pe_bcast(self, pe, n):
                pe.wait_ge(self.s["ln_rstd"], n + 1)
                if self.twice:
                    pe.wait_ge(self.s["ln_t"], 2 * n + 1)
                for k in range(4):
                    m = pe.matmul(self.bank[:, k * SH:(k + 1) * SH], bcast[:, k, :], lnw["rstd"][:, :], start=True, stop=True)
                m.then_inc(self.s["ln_bc"], 1)

            def dve_scale(self, v, n, first):
                if not first and not self.twice:
                    v.wait_ge(self.s["ln_hi"], n)
                    v.wait_ge(self.s["ln_lo"], n)
                if not first and self.twice:
                    v.wait_ge(self.s["ln_res"], n)
                v.wait_ge(self.s["ln_bc"], n + 1)
                dst = lnw["z"] if self.twice else lnw["xn"]
                for c in range(KD):
                    m = v.tensor_tensor(dst[:, c, :], lnw["xc"][:, c, :], self.bank[:, 0:T], ALU.mult)
                m.then_inc(self.s["ln_z" if self.twice else "ln_xn"], 1)

            def pool_residual(self, p, cols, n):
                p.wait_ge(self.s["ln_z"], n + 1)
                p.tensor_tensor(hT[:, :, cols], hT[:, :, cols], lnw["z"][:, :, :], ALU.add).then_inc(self.s["ln_res"], 1)

            def pe_bcast2(self, pe, n):
                pe.wait_ge(self.s["ln_z"], n + 1)
                pe.wait_ge(self.s["ln_rstd2"], 2 * n + 2)
                for k in range(4):
                    m = pe.matmul(self.bank[:, k * SH:(k + 1) * SH], bcast[:, k, :], lnw["rstd2"][:, :], start=True, stop=True)
                m.then_inc(self.s["ln_bc2"], 1)

            def dve_scale2(self, v, n, first):
                v.wait_ge(self.s["ln_bc2"], n + 1)
                if not first:
                    v.wait_ge(self.s["ln_hi"], n)
                    v.wait_ge(self.s["ln_lo"], n)
                for c in range(KD):
                    m = v.tensor_tensor(lnw["xn"][:, c, :], lnw["xc"][:, c, :], self.bank[:, 0:T], ALU.mult)
                m.then_inc(self.s["ln_x2"], 1)
                v.wait_ge(self.s["ln_x2"], n + 1)
                for c in range(KD):
                    m = v.tensor_scalar(lnw["xn"][:, c, :], lnw["xn"][:, c, :], vec1[:, 1, c:c + 1], vec1[:, 2, c:c + 1],
                                        ALU.mult, ALU.add)
                m.then_inc(self.s["ln_xn"], 1)

            def act_hi(self, a, cols, n):
                a.wait_ge(self.s["ln_xn"], n + 1)
                a.activation(xh[:, :, cols], lnw["xn"][:, :, :], ACT.Copy).then_inc(self.s["ln_hi"], 1)

            def pool_lo(self, p, cols, n):
                p.wait_ge(self.s["ln_hi"], n + 1)
                p.tensor_tensor(xl[:, :, cols], lnw["xn"][:, :, :], xh[:, :, cols], ALU.subtract).then_inc(self.s["ln_lo"], 1)

        def attention(layer):
            ph = ExitStack()
            first_layer = layer == 0
            twice = False
            NP = 3 if first_layer else 4
            KR = 64 + NP * DH
            KX = KR + 2 if first_layer else KR
            HP = H // 2
            JJ = HC // 2
            wqkv = [sb(f"wqkv{layer}{i}", [P, KD, 3 * D], F16, ph) for i in range(2)]
            wpro = [sb(f"wpro{layer}{i}", [P, KD, D], F16, ph) for i in range(2)]
            qc = sb(f"qc{layer}", [P, 4, T], scope=ph)
            qkh = sb(f"qkh{layer}", [P, 4, T], F16, ph)
            qkl = sb(f"qkl{layer}", [P, 4, T], F16, ph)
            qs = [[sb(f"qs{layer}{i}{h}", [P, HP, T], F16, ph) for h in range(2)] for i in range(2)]
            ks = [sb(f"ks{layer}{i}", [P, HP, T], F16, ph) for i in range(2)]
            vp = [sb(f"vp{layer}{i}", [SH, 2, 2, KD * JJ, 2, 32], scope=ph) for i in range(2)]
            onesv = sb(f"onesv{layer}", [SH, 2, 32], scope=ph)
            pr = sb(f"pr{layer}", [SH, 2, JJ, T], scope=ph)
            rden = sb(f"rden{layer}", [P, S], scope=ph)
            on = sb(f"on{layer}", [P, KD, T], scope=ph)
            oh = sb(f"oh{layer}", [P, KD, T], F16, ph)
            ol = sb(f"ol{layer}", [P, KD, T], F16, ph)
            if first_layer:
                qsq = sb("qsq", [P, 4, T], scope=ph)
                qsd = sb("qsd", [P, T], scope=ph)
                qrs = sb("qrs", [P, T], scope=ph)
                mx = sb("mx", [SH, 2, 2, H], scope=ph)
                ml = sb("ml", [SH, 2, 2, 2, H], F16, ph)
                mt = sb("mt", [2 * H, 2, S], F16, ph)
                wmean = sb("wmean", [P, KD, 2 * H], scope=ph)
            else:
                bo01 = sb("bo01", [P, KD], scope=ph)
                upd = sb("upd", [P, KD, T], scope=ph)
            bank = [ps(f"at{layer}{i}", [P, 512], scope=ph) for i in range(8)]
            dense, maxb, expb, avb = bank[0:2], bank[2:4], bank[4:6], bank[6:8]
            bounce = nc.dram_tensor(f"bounce{layer}", (2, 2, 4, P, T), F16).ap()
            own = (("qsq", "qvar", "qsd", "qrs", "qbc", "qn", "qa", "mm", "mx", "ml", "mt", "mtc", "mrow") if first_layer
                   else ("cl", "up"))
            s = semaphores("prep", "zero", "wt", "wcp", "init", "qk", "qc", "qhi", "qlo", "bnc", "stk", "v", "vp", "sc", "ex", "av",
                           "rd", "on", "ohi", "olo", "pj", "h", *own)
            ln = Norm(dense[0])
            NS = 2 * H
            seq = lambda i, bb: bass.ds(i * T + bb * S, S)
            cols = lambda i: bass.ds(i * T, T)
            UPS = 2 * 2 * 6
            unit = lambda u: (u // 12, u // 6 % 2, u % 6 // 3, u % 3 * 3, 3 if u % 3 < 2 else 2)

            with nc.allow_non_contiguous_dma(reason="rows of a head"), nc.Block() as block:
                @block.tensor
                def _(pe):
                    last = {}

                    def claim(b, sem, value):
                        if b in last:
                            pe.wait_ge(*last[b])
                        last[b] = (s[sem] if isinstance(sem, str) else sem, value)

                    def qk(a, k):
                        claim((0, 0, 1, 0)[k], "qc", 4 * a + k + 1)
                        b = dense[(0, 0, 1, 0)[k]]
                        n = 0
                        for wi, xi in ((0, xh), (1, xh), (0, xl)):
                            for c in range(KD):
                                m = pe.matmul(b[:, 0:T], wqkv[wi][:, c, k * P:(k + 1) * P], xi[:, c, cols(a)], start=(n == 0), stop=(n == 5))
                                n += 1
                        m.then_inc(s["qk"], 1)

                    def qvar(a):
                        pe.wait_ge(s["qsq"], 4 * a + 4)
                        claim(1, "qsd", a + 1)
                        for k in range(4):
                            m = pe.matmul(dense[1][32 * k:32 * k + 32, 0:T], head_mean[:, :], qsq[:, k, :], start=True, stop=True)
                        m.then_inc(s["qvar"], 1)

                    def qbc(a, k):
                        pe.wait_ge(s["qrs"], a + 1)
                        b = (1, 0, 1, 0)[k]
                        claim(b, "qn", 4 * a + k + 1)
                        pe.matmul(dense[b][:, 0:T], head_back[:, k, :], qrs[:, :], start=True, stop=True).then_inc(s["qbc"], 1)

                    def maxima(b, u, par):
                        bb, qt, hh, p0, n = unit(u)
                        if u == 0:
                            pe.wait_ge(s["stk"], 192 * (b + 1))
                        if not (isinstance(b, int) and b == 0 and u < 2):
                            pe.wait_ge(s["mx"], UPS * b + u - 1)
                        for x in range(n):
                            m = pe.matmul(maxb[u % 2][0:SH, x * S:(x + 1) * S],
                                          qs[par][hh][0:KR, p0 + x, bb * S + qt * SH:bb * S + (qt + 1) * SH],
                                          ks[par][0:KR, p0 + x, bb * S:(bb + 1) * S], start=True, stop=True)
                        m.then_inc(s["mm"], 1)

                    def turn_maxima(b, bb):
                        pe.wait_ge(s["ml"], 4 * b + 2 * bb + 2)
                        claim(1, "mtc", 2 * b + bb + 1)
                        for qt in range(2):
                            m = pe.transpose(dense[1].bitcast(F16)[0:2 * H, qt * SH:(qt + 1) * SH],
                                             ml[:, bb, qt, :, :].rearrange("p a b -> p (a b)"), ident16[0:SH, 0:SH])
                        m.then_inc(s["mt"], 1)

                    def values(b, bb):
                        claim(1 - bb, "vp", 4 * b + 2 * bb + 2)
                        for kt in range(2):
                            n = 0
                            for xi, wi in ((xh, 0), (xh, 1), (xl, 0)):
                                for c in range(KD):
                                    m = pe.matmul(dense[1 - bb][0:SH, kt * D:(kt + 1) * D], xi[:, c, bass.ds(b * T + bb * S + kt * SH, SH)],
                                                  wqkv[wi][:, c, 2 * D:3 * D], start=(n == 0), stop=(n == 5))
                                    n += 1
                        m.then_inc(s["v"], 1)

                    def scores(i, g, par):
                        t, jj = g // 4, g % 4
                        bb, c, hh = t // 4, t // 2 % 2, t % 2
                        if g % H == 0:
                            if first_layer:
                                pe.wait_ge(s["mrow"], 64 * (2 * i + bb + 1))
                            elif g == 0:
                                pe.wait_ge(s["stk"], 256 * (i + 1))
                        if not (isinstance(i, int) and NS * i + g < 2):
                            pe.wait_ge(s["ex" if first_layer else "cl"], NS * i + g - 1)
                        for kt in range(2):
                            m = pe.matmul(expb[g % 2][0:SH, kt * S:(kt + 1) * S],
                                          ks[par][0:KX, c * JJ + jj, bb * S + kt * SH:bb * S + (kt + 1) * SH],
                                          qs[par][hh][0:KX, c * JJ + jj, bb * S:(bb + 1) * S], start=True, stop=True)
                        m.then_inc(s["sc"], 1)

                    def weighted(i, t, q, par):
                        bb, c, hh = t // 4, t // 2 % 2, t % 2
                        kt, sums = q // 2, q % 2
                        if q == 0:
                            pe.wait_ge(s["ex"], NS * i + 4 * t + 4 if first_layer else 8 * i + t + 1)
                            if t % 4 == 0:
                                pe.wait_ge(s["vp"], 4 * i + 2 * bb + 2)
                            if hh == 0 and not (isinstance(i, int) and 4 * i + 2 * bb + c - 1 <= 0):
                                pe.wait_ge(s["on"], 4 * i + 2 * bb + c - 1)
                        for jj in range(JJ):
                            lhs = onesv[:, hh, :] if sums else vp[par][:, bb, kt, c * JJ + jj, hh, :]
                            m = pe.matmul(avb[c][32 * jj:32 * jj + 32, sums * S:(sums + 1) * S], lhs,
                                          pr[:, t % 2, jj, kt * S:(kt + 1) * S], start=(hh == 0 and q == 0), stop=(hh == 1 and kt == 1),
                                          skip_group_check=True)
                        if q == 3:
                            m.then_inc(s["av"], 1)

                    def project(l, k):
                        pe.wait_ge(s["olo"], 4 * l + 4)
                        claim(1 - k, "h" if first_layer else "up", 2 * l + k + 1)
                        n = 0
                        for wi, oi in ((0, oh), (1, oh), (0, ol)):
                            for c in range(KD):
                                m = pe.matmul(dense[1 - k][:, 0:T], wpro[wi][:, c, k * P:(k + 1) * P], oi[:, c, :], start=(n == 0), stop=(n == 5))
                                n += 1
                        m.then_inc(s["pj"], 1)

                    def norm_mean(l):
                        pe.wait_ge(s["h"], 2 * l + 2)
                        claim(0, ln.s["ln_xc"], l + 1)
                        ln.pe_mean(pe, cols(l), l)

                    def norm_var(l):
                        ln.pe_var(pe, l)
                        last[0] = (ln.s["ln_sd"], l + 1)

                    def norm_back(l):
                        claim(0, ln.done, l + 1)
                        ln.pe_bcast(pe, l)

                    def body(i, par, first, has_a, has_b):
                        a, b, l = i + 2, i + 1, i - 1
                        for g in range(NS):
                            scores(i, g, par)
                            t = g // 4
                            if t >= 1:
                                weighted(i, t - 1, g % 4, par)
                            elif not first:
                                weighted(i - 1, 7, g % 4, 1 - par)
                            if has_a and g in (0, 2, 3, 4):
                                qk(a, (0, 2, 3, 4).index(g))
                            if first_layer and g == 1:
                                turn_maxima(i, 1)
                            if has_b and g in (6, 8):
                                values(b, (g - 6) // 2)
                            if first_layer and has_b and 6 <= g < 6 + UPS:
                                maxima(b, g - 6, 1 - par)
                            if not first and g in (10, 11):
                                project(l, g - 10)
                            if first_layer and has_a and g == 13:
                                qvar(a)
                            if not first and g == 14:
                                norm_mean(l)
                            if not first and g == 17:
                                norm_var(l)
                            if first_layer and has_b and g == 19:
                                turn_maxima(b, 0)
                            if not first and g == 20:
                                norm_back(l)
                            if first_layer and has_a and 22 <= g < 26:
                                qbc(a, g - 22)

                    def prologue():
                        if first_layer:
                            pe.wait_ge(s["prep"], 4)
                        else:
                            for w in range(4):
                                for ci in range(KD):
                                    for co in range(KD):
                                        m = pe.transpose(bank[w][:, ci * D + co * P:ci * D + (co + 1) * P],
                                                         raw_att1[:, w, co, ci * P:(ci + 1) * P], ident[:, :])
                                m.then_inc(s["wt"], 1)
                            pe.wait_ge(s["prep"], 4)
                        pe.wait_ge(s["init"], 7)
                        for a in range(2):
                            for k in range(4):
                                qk(a, k)
                            if first_layer:
                                qvar(a)
                                for k in range(4):
                                    qbc(a, k)
                        for bb in range(2):
                            values(0, bb)
                        if first_layer:
                            for u in range(UPS):
                                maxima(0, u, 0)
                            turn_maxima(0, 0)

                    def epilogue():
                        l = NT - 1
                        for q in range(4):
                            weighted(l, 7, q, l % 2)
                        for k in range(KD):
                            project(l, k)
                        norm_mean(l)
                        norm_var(l)
                        norm_back(l)

                    prologue()
                    for i in range(2):
                        body(i, i, i == 0, True, True)
                    steady = ({0: (s["qn"], lambda i: 4 * i + 8), 1: (s["qn"], lambda i: 4 * i + 7)} if first_layer else
                              {0: (ln.done, lambda i: i - 1), 1: (s["up"], lambda i: 2 * i - 3)})
                    with pe.Fori(1, NT // 2 - 1, 1) as half:
                        for u in range(2):
                            i = half * 2
                            last.update({b: (sem, f(i + u)) for b, (sem, f) in steady.items()})
                            body(i + u, u, False, True, True)
                    for i in range(NT - 2, NT):
                        last.update({b: (sem, f(NT - 2)) for b, (sem, f) in steady.items()} if i == NT - 2 else {})
                        body(i, i % 2, False, False, i < NT - 1)
                    epilogue()

                @block.scalar
                def _(act):
                    def copy_qk(a, k):
                        act.wait_ge(s["qk"], 4 * a + k + 1)
                        if not (isinstance(a, int) and a == 0):
                            act.wait_ge(s["qlo"], a)
                        scale = 1 / WS if first_layer else (0.5 * DH ** -0.5 if k < 2 else 1.0)
                        act.activation(qc[:, k, :], dense[(0, 0, 1, 0)[k]][:, 0:T], ACT.Copy, scale=scale).then_inc(s["qc"], 1)

                    def deviation(a):
                        act.wait_ge(s["qvar"], a + 1)
                        if not (isinstance(a, int) and a == 0):
                            act.wait_ge(s["qrs"], a)
                        act.activation(qsd[:, :], dense[1][:, 0:T], ACT.Sqrt, bias=eps_c[:, 0:1]).then_inc(s["qsd"], 1)

                    def high_qk(a):
                        act.wait_ge(s["qa" if first_layer else "qc"], 4 * a + 4)
                        if not (isinstance(a, int) and a == 0):
                            act.wait_ge(s["bnc"], 32 * a)
                        act.activation(qkh[:, :, :], qc[:, :, :], ACT.Copy).then_inc(s["qhi"], 1)

                    def exponentials(i, g):
                        t, jj = g // 4, g % 4
                        if first_layer:
                            act.wait_ge(s["sc"], NS * i + g + 1)
                            if jj == 0 and not (isinstance(i, int) and 8 * i + t - 1 <= 0):
                                act.wait_ge(s["av"], 8 * i + t - 1)
                            act.activation(pr[:, t % 2, jj, :], expb[g % 2][0:SH, 0:T], ACT.Exp, scale=DH ** -0.5).then_inc(s["ex"], 1)
                        elif jj == 3:
                            act.wait_ge(s["cl"], NS * i + g + 1)
                            act.activation(pr[:, t % 2, :, :], pr[:, t % 2, :, :], ACT.Exp).then_inc(s["ex"], 1)

                    def high_out(i, n):
                        act.wait_ge(s["on"], 4 * i + n + 1)
                        if n == 0 and not (isinstance(i, int) and i == 0):
                            act.wait_ge(s["pj"], 2 * i)
                        bb, c = n // 2, n % 2
                        act.activation(oh[:, c, bb * S:(bb + 1) * S], on[:, c, bb * S:(bb + 1) * S], ACT.Copy).then_inc(s["ohi"], 1)

                    def body(i, par, first, has_a, has_b):
                        a, l = i + 2, i - 1
                        for g in range(NS):
                            exponentials(i, g)
                            if has_a and g in (0, 2, 3, 4):
                                copy_qk(a, (0, 2, 3, 4).index(g))
                            if not first and g == 5:
                                high_out(l, 3)
                            if g in (13, 21, 29):
                                high_out(i, (g - 13) // 8)
                            if not first and g == 16:
                                ln.act_square(act, l, isinstance(l, int) and l == 0)
                            if g == 18:
                                if first_layer and has_a:
                                    deviation(a)
                                if not first:
                                    ln.act_sd(act, l, isinstance(l, int) and l == 0)
                            if not first and g == 22:
                                ln.act_hi(act, cols(l), l)
                            if has_a and g == (28 if first_layer else 8):
                                high_qk(a)

                    if first_layer:
                        act.activation(wqkv[0][:, :, 2 * D:], raw_qkv[:, :, 2 * D:], ACT.Copy, scale=WS).then_inc(s["wcp"], 1)
                        act.activation(wpro[0][:, :, :], raw_proj[:, :, :], ACT.Copy, scale=WS).then_inc(s["wcp"], 1)
                        act.wait_ge(s["wt"], 1)
                        act.activation(wqkv[0][:, :, 0:2 * D], raw_qkv[:, :, 0:2 * D], ACT.Copy, scale=WS).then_inc(s["wcp"], 1)
                    else:
                        for w in range(4):
                            act.wait_ge(s["wt"], w + 1)
                            dst = wqkv[0][:, :, w * D:(w + 1) * D] if w < 3 else wpro[0][:, :, :]
                            act.activation(dst, bank[w][:, :].rearrange("p (c n) -> p c n", c=KD), ACT.Copy).then_inc(s["wcp"], 1)
                    for a in range(2):
                        for k in range(4):
                            copy_qk(a, k)
                        if first_layer:
                            deviation(a)
                        high_qk(a)
                    for i in range(2):
                        body(i, i, i == 0, True, True)
                    with act.Fori(1, NT // 2 - 1, 1) as half:
                        for u in range(2):
                            i = half * 2
                            body(i + u, u, False, True, True)
                    for i in range(NT - 2, NT):
                        body(i, i % 2, False, False, i < NT - 1)
                    l = NT - 1
                    high_out(l, 3)
                    ln.act_square(act, l, False)
                    ln.act_sd(act, l, False)
                    ln.act_hi(act, cols(l), l)

                @block.vector
                def _(v):
                    def invert(a):
                        v.wait_ge(s["qsd"], a + 1)
                        if not (isinstance(a, int) and a == 0):
                            v.wait_ge(s["qbc"], 4 * a)
                        v.reciprocal(qrs[:, :], qsd[:, :]).then_inc(s["qrs"], 1)

                    def scale_qk(a, k):
                        v.wait_ge(s["qbc"], 4 * a + k + 1)
                        v.tensor_tensor(qc[:, k, :], qc[:, k, :], dense[(1, 0, 1, 0)[k]][:, 0:T], ALU.mult).then_inc(s["qn"], 1)
                        v.wait_ge(s["qn"], 4 * a + k + 1)
                        j = 0 if k < 2 else 2
                        v.tensor_scalar(qc[:, k, :], qc[:, k, :], gam[:, j:j + 1], gam[:, j + 1:j + 2], ALU.mult, ALU.add).then_inc(s["qa"], 1)

                    def reduce_maxima(b, u):
                        bb, qt, hh, p0, n = unit(u)
                        v.wait_ge(s["mm"], UPS * b + u + 1)
                        v.tensor_reduce(mx[:, bb, qt, 8 * hh + p0:8 * hh + p0 + n],
                                        maxb[u % 2][0:SH, 0:n * S].rearrange("p (h k) -> p h k", h=n), AX.X, ALU.max).then_inc(s["mx"], 1)

                    def split_maxima(b, bb):
                        v.wait_ge(s["mx"], UPS * b + 12 * (bb + 1))
                        if not (isinstance(b, int) and b == 0):
                            v.wait_ge(s["mt"], 2 * b + bb - 1)
                        v.tensor_scalar(ml[:, bb, :, 0, :], mx[:, bb, :, :], -1.0, None, ALU.mult).then_inc(s["ml"], 1)
                        v.wait_ge(s["ml"], 4 * b + 2 * bb + 1)
                        v.scalar_tensor_tensor(out=ml[:, bb, :, 1, :], in0=mx[:, bb, :, :], scalar=-1.0, in1=ml[:, bb, :, 0, :],
                                               op0=ALU.mult, op1=ALU.subtract).then_inc(s["ml"], 1)

                    def copy_maxima(b, bb):
                        v.wait_ge(s["mt"], 2 * b + bb + 1)
                        if not (isinstance(b, int) and b == 0):
                            v.wait_ge(s["mrow"], 64 * (2 * b + bb - 1))
                        v.tensor_copy(mt[:, bb, :], dense[1].bitcast(F16)[0:2 * H, 0:S]).then_inc(s["mtc"], 1)

                    def copy_values(b, bb, par, first2):
                        v.wait_ge(s["v"], 2 * b + bb + 1)
                        if bb == 0 and not first2:
                            v.wait_ge(s["av"], 8 * (b - 1))
                        src = dense[1 - bb][0:SH, :].rearrange("p (t g h d) -> p (t g) h d", t=2, h=2, d=DH)
                        dst = vp[par][:, bb, :, :, :, :].rearrange("p t g h d -> p (t g) h d")
                        for hh in range(2):
                            v.tensor_scalar(dst[:, :, hh, hh * DH:(hh + 1) * DH], src[:, :, hh, :], 1 / WS if first_layer else 1.0, None,
                                            ALU.mult).then_inc(s["vp"], 1)

                    def clip(i, g):
                        t, jj = g // 4, g % 4
                        v.wait_ge(s["sc"], NS * i + g + 1)
                        if jj == 0 and not (isinstance(i, int) and 8 * i + t - 1 <= 0):
                            v.wait_ge(s["av"], 8 * i + t - 1)
                        v.tensor_scalar(pr[:, t % 2, jj, :], expb[g % 2][0:SH, 0:T], -10.0, 10.0, ALU.max, ALU.min).then_inc(s["cl"], 1)

                    def normalise(i, n):
                        bb, c = n // 2, n % 2
                        v.wait_ge(s["av"], 8 * i + 2 * n + 2)
                        v.reciprocal(rden[:, :], avb[c][:, S:2 * S]).then_inc(s["rd"], 1)
                        v.wait_ge(s["rd"], 4 * i + n + 1)
                        if not (isinstance(i, int) and i == 0):
                            v.wait_ge(s["olo"], 4 * i + n - 3)
                        v.tensor_tensor(on[:, c, bb * S:(bb + 1) * S], avb[c][:, 0:S], rden[:, :], ALU.mult).then_inc(s["on"], 1)

                    def update(l, k):
                        v.wait_ge(s["pj"], 2 * l + k + 1)
                        if first_layer:
                            v.scalar_tensor_tensor(out=hT[:, k, cols(l)], in0=dense[1 - k][:, 0:T], scalar=1 / WS, in1=hT[:, k, cols(l)],
                                                   op0=ALU.mult, op1=ALU.add).then_inc(s["h"], 1)
                        else:
                            if not (isinstance(l, int) and l == 0):
                                v.wait_ge(s["h"], 2 * l)
                            v.tensor_scalar(upd[:, k, :], dense[1 - k][:, 0:T], 0.1, bo01[:, k:k + 1], ALU.mult, ALU.add).then_inc(s["up"], 1)
                            v.wait_ge(s["up"], 2 * l + k + 1)
                            v.tensor_tensor(hT[:, k, cols(l)], hT[:, k, cols(l)], upd[:, k, :], ALU.add).then_inc(s["h"], 1)

                    def body(i, par, first, has_a, has_b):
                        a, b, l = i + 2, i + 1, i - 1
                        l0 = isinstance(l, int) and l == 0
                        for g in range(NS):
                            if not first_layer:
                                clip(i, g)
                            if first_layer and g == 2:
                                copy_maxima(i, 1)
                            if not first and g == 4:
                                normalise(l, 3)
                            if has_b and g in (7, 9):
                                copy_values(b, (g - 7) // 2, 1 - par, first)
                            if first_layer and has_b and 7 <= g < 7 + UPS:
                                reduce_maxima(b, g - 7)
                            if not first and g in (11, 12):
                                update(l, g - 11)
                            if g in (12, 20, 28):
                                normalise(i, (g - 12) // 8)
                            if not first and g == 15:
                                ln.dve_center(v, cols(l), l, l0)
                            if g == 19:
                                if first_layer and has_b:
                                    split_maxima(b, 0)
                                if not first:
                                    ln.dve_rstd(v, l, l0)
                                if first_layer and has_a:
                                    invert(a)
                            if first_layer and has_b and g == 20:
                                copy_maxima(b, 0)
                            if not first and g == 21:
                                ln.dve_scale(v, l, l0)
                            if first_layer and has_a and 23 <= g < 27:
                                scale_qk(a, g - 23)
                            if first_layer and has_b and g == 31:
                                split_maxima(b, 1)

                    if first_layer:
                        w3 = raw_qkv[:, :, 0:2 * D].rearrange("p c (h d) -> p c h d", d=DH)
                        for c in range(KD):
                            m = v.tensor_reduce(wmean[:, c, :], w3[:, c], AX.X, ALU.add)
                        m.then_inc(s["init"], 1)
                        v.wait_ge(s["init"], 1)
                        v.tensor_scalar(wmean[:, :, :], wmean[:, :, :], 1 / DH, None, ALU.mult).then_inc(s["init"], 1)
                        v.wait_ge(s["init"], 2)
                        for c in range(KD):
                            m = v.tensor_tensor(w3[:, c], w3[:, c], wmean[:, c, :].unsqueeze(2).to_broadcast([P, 2 * H, DH]), ALU.subtract)
                        m.then_inc(s["wt"], 1)
                        v.wait_ge(s["wcp"], 3)
                        for c in range(KD):
                            for lo, hi, src in ((wqkv[1], wqkv[0], raw_qkv), (wpro[1], wpro[0], raw_proj)):
                                v.scalar_tensor_tensor(out=lo[:, c, :], in0=src[:, c, :], scalar=WS, in1=hi[:, c, :],
                                                       op0=ALU.mult, op1=ALU.subtract).then_inc(s["prep"], 1)
                    else:
                        v.tensor_scalar(bo01[:, :], vec1[:, 0, :], 0.1, None, ALU.mult).then_inc(s["init"], 1)
                        for w in range(4):
                            v.wait_ge(s["wcp"], w + 1)
                            lo = wqkv[1][:, :, w * D:(w + 1) * D] if w < 3 else wpro[1][:, :, :]
                            hi = wqkv[0][:, :, w * D:(w + 1) * D] if w < 3 else wpro[0][:, :, :]
                            v.tensor_tensor(lo, bank[w][:, :].rearrange("p (c n) -> p c n", c=KD), hi, ALU.subtract).then_inc(s["prep"], 1)
                        v.memset(rden[:, 0:1], 1.0).then_inc(s["init"], 1)
                    for par in range(2):
                        v.memset(vp[par][:, :, :, :, :, :], 0.0).then_inc(s["init"], 1)
                        zero = [(qs[par][0], 64), (qs[par][1], 0)]
                        if first_layer:
                            zero += [(qs[par][0], 32), (qs[par][1], 96), (ks[par], 32)]
                            v.memset(ks[par][96:P, :, :], 1.0)
                        for x, r0 in zero:
                            r9 = 64 if r0 == 32 or r0 == 0 else P
                            m = v.memset(x[r0:r9, :, :].bitcast(I32), 0)
                        m.then_inc(s["zero"], 1)
                    v.memset(onesv[:, :, :], 0.0).then_inc(s["init"], 1)
                    v.wait_ge(s["init"], 5)
                    for hh in range(2):
                        v.memset(onesv[:, hh, hh * DH:(hh + 1) * DH], 1.0).then_inc(s["init"], 1)
                    if first_layer:
                        for a in range(2):
                            invert(a)
                            for k in range(4):
                                scale_qk(a, k)
                    for bb in range(2):
                        copy_values(0, bb, 0, True)
                    if first_layer:
                        for u in range(UPS):
                            reduce_maxima(0, u)
                        split_maxima(0, 0)
                        copy_maxima(0, 0)
                        split_maxima(0, 1)
                    for i in range(2):
                        body(i, i, i == 0, True, True)
                    with v.Fori(1, NT // 2 - 1, 1) as half:
                        for u in range(2):
                            i = half * 2
                            body(i + u, u, False, True, True)
                    for i in range(NT - 2, NT):
                        body(i, i % 2, False, False, i < NT - 1)
                    l = NT - 1
                    normalise(l, 3)
                    for k in range(KD):
                        update(l, k)
                    ln.dve_center(v, cols(l), l, False)
                    ln.dve_rstd(v, l, False)
                    ln.dve_scale(v, l, False)

                @block.gpsimd
                def _(p):
                    def squares(a, k):
                        p.wait_ge(s["qc"], 4 * a + k + 1)
                        if not (isinstance(a, int) and a == 0):
                            p.wait_ge(s["qvar"], a)
                        p.tensor_tensor(qsq[:, k, :], qc[:, k, :], qc[:, k, :], ALU.mult).then_inc(s["qsq"], 1)

                    def low_qk(a):
                        p.wait_ge(s["qhi"], a + 1)
                        if not (isinstance(a, int) and a == 0):
                            p.wait_ge(s["bnc"], 32 * a)
                        p.tensor_tensor(qkl[:, :, :], qc[:, :, :], qkh[:, :, :], ALU.subtract).then_inc(s["qlo"], 1)

                    def low_out(i, n):
                        bb, c = n // 2, n % 2
                        p.wait_ge(s["ohi"], 4 * i + n + 1)
                        p.tensor_tensor(ol[:, c, bb * S:(bb + 1) * S], on[:, c, bb * S:(bb + 1) * S], oh[:, c, bb * S:(bb + 1) * S],
                                        ALU.subtract).then_inc(s["olo"], 1)

                    def body(i, first, has_a):
                        a, l = i + 2, i - 1
                        if first_layer and has_a:
                            squares(a, 0)
                        if not first:
                            low_out(l, 3)
                        if first_layer and has_a:
                            for k in range(1, 4):
                                squares(a, k)
                        if not first_layer and has_a:
                            low_qk(a)
                        low_out(i, 0)
                        low_out(i, 1)
                        if not first:
                            ln.pool_lo(p, cols(l), l)
                        if first_layer and has_a:
                            low_qk(a)
                        low_out(i, 2)

                    for a in range(2):
                        if first_layer:
                            for k in range(4):
                                squares(a, k)
                        low_qk(a)
                    for i in range(2):
                        body(i, i == 0, True)
                    with p.Fori(2, NT - 2, 1) as i:
                        body(i, False, True)
                    for i in range(NT - 2, NT):
                        body(i, False, False)
                    low_out(NT - 1, 3)
                    ln.pool_lo(p, cols(NT - 1), NT - 1)

                @block.sync
                def _(sp):
                    nstk = 16 * 2 * 2 * NP
                    values = [sp.alloc_register(f"wait_a{layer}"), sp.alloc_register(f"wait_b{layer}")]

                    def hold(r, x):
                        if isinstance(x, int):
                            return x
                        sp.reg_mov(values[r], x)
                        return values[r]

                    def leave(a, par, first2):
                        split, free = hold(0, a + 1), None if first2 else hold(1, nstk * (a - 1))
                        sp.wait_ge(s["qlo"], split)
                        if not first2:
                            sp.wait_ge(s["stk"], free)
                        for part, src in enumerate((qkh, qkl)):
                            sp.dma_start(bounce[par, part].rearrange("k p t -> p k t"), src[:, :, :]).then_inc(s["bnc"], 16)

                    def stack(b, par, first2):
                        there, free = hold(0, 32 * (b + 1)), None if first2 else hold(1, NS * (b - 1))
                        sp.wait_ge(s["bnc"], there)
                        if not first2:
                            sp.wait_ge(s["sc"], free)
                        for x in range(2):
                            for part in range(NP):
                                low = ((0, 0, 1), (0, 1, 0))[x][part] if NP == 3 else ((0, 1, 0, 1), (0, 0, 1, 1))[x][part]
                                for hh in range(2):
                                    src = bounce[par, low, 2 * x:2 * x + 2].rearrange("c (j h d) t -> h d (c j) t", h=2, d=DH)[hh]
                                    dst = ks[par] if x else qs[par][hh]
                                    r = 64 * hh + DH * part
                                    sp.dma_start(dst[r:r + DH, :, :], src).then_inc(s["stk"], 16)

                    def maxima_rows(b, bb, par):
                        copied = hold(0, 2 * b + bb + 1)
                        sp.wait_ge(s["mtc"], copied)
                        for hh in range(2):
                            for part in range(2):
                                r = KR + part
                                sp.dma_start(qs[par][hh][r:r + 1, :, bb * S:(bb + 1) * S],
                                             mt[H * part + 8 * hh:H * part + 8 * hh + 8, bb, :]).then_inc(s["mrow"], 16)

                    def body(i, par, first, has_a, has_b):
                        a, b = i + 2, i + 1
                        if has_b:
                            stack(b, 1 - par, first)
                        if first_layer:
                            maxima_rows(i, 1, par)
                            if has_b:
                                maxima_rows(b, 0, 1 - par)
                        if has_a:
                            leave(a, par, False)

                    sp.wait_ge(s["zero"], 2)
                    leave(0, 0, True)
                    stack(0, 0, True)
                    leave(1, 1, True)
                    if first_layer:
                        maxima_rows(0, 0, 0)
                    for i in range(2):
                        body(i, i, i == 0, True, True)
                    with sp.Fori(1, NT // 2 - 1, 1) as half:
                        for u in range(2):
                            i = half * 2
                            body(i + u, u, False, True, True)
                    for i in range(NT - 2, NT):
                        body(i, i % 2, False, False, i < NT - 1)
                    sp.wait_ge(s["bnc"], 32 * NT)
            ph.close()

        def feed_forward(layer):
            ph = ExitStack()
            gated = layer == 0
            M = K0 if gated else K1
            UR = 2 if gated else 4
            HR = M // 2
            NW = (3 if gated else 2) * KD * M
            assert M % UR == 0 and M % HR == 0
            Q = 1 / 127.0
            wt = sb(f"wt{layer}", [P, NW, P], F16, ph)
            w16 = sb(f"w16{layer}", [P, NW * P], F16, ph)
            hid = sb(f"hid{layer}", [P, 2, T], scope=ph)
            act_g = sb(f"act_g{layer}", [P, 2, T], scope=ph)
            hh = sb(f"hh{layer}", [P, HR, T], F16, ph)
            hl = sb(f"hl{layer}", [P, HR, T], F16, ph)
            if not gated:
                alpha1 = sb("alpha1", [P, K1], scope=ph)
                alpha2 = sb("alpha2", [P, KD], scope=ph)
                upd = sb("upd4", [P, KD, T], scope=ph)
                hf = sb("hf", [P, KD, T], scope=ph)
                ot = sb("ot", [SH, 4, D], scope=ph)
            bank = [ps(f"ff{layer}{i}", [P, 512], scope=ph) for i in range(8)]
            s = semaphores("cast", "turn", "wt", "alpha", "up", "hid", "hh", "hl", "dn", "h", *(("act",) if gated else ("upd", "tr", "ot", "out")))
            ln = Norm(bank[6], twice=True) if gated else None
            NB = -(-NW // 8)
            cols = lambda i: bass.ds(i * T, T)
            isz = lambda i: isinstance(i, int) and i == 0

            with nc.Block() as block:
                @block.tensor
                def _(pe):
                    def up(i, m):
                        n0 = M * i + m
                        if not (isinstance(i, int) and n0 < UR):
                            pe.wait_ge(s["hid"], n0 - UR + 1)
                        for g in range(2 if gated else 1):
                            n = 0
                            for x in (xh, xl):
                                for c in range(KD):
                                    mm = pe.matmul(bank[(2 if gated else 1) * (m % UR) + g][:, 0:T], wt[:, (g * KD + c) * M + m, :],
                                                   x[:, c, cols(i)], start=(n == 0), stop=(n == 3))
                                    n += 1
                        mm.then_inc(s["up"], 1)

                    def down(i, m):
                        pe.wait_ge(s["hl"], M * i + m + 1)
                        if m == 0 and not isz(i):
                            pe.wait_ge(s["h" if gated else "upd"], 2 * i)
                        for k in range(KD):
                            for n, x in enumerate((hh, hl)):
                                mm = pe.matmul(bank[4 + k][:, 0:T], wt[:, (2 if gated else 1) * KD * M + m * KD + k, :],
                                               x[:, m % HR, :], start=(m == 0 and n == 0), stop=(m == M - 1 and n == 1))
                        mm.then_inc(s["dn"], 1)

                    def finish(l, m, first):
                        if gated:
                            if m == 2:
                                pe.wait_ge(s["h"], 2 * l + 2)
                                if not first:
                                    pe.wait_ge(ln.done, l)
                                ln.pe_mean(pe, cols(l), l)
                            if m == 3:
                                ln.pe_var(pe, l)
                            if m == 4:
                                ln.pe_bcast(pe, l)
                            if m == 5:
                                ln.pe_bcast2(pe, l)
                        elif m == 3:
                            pe.wait_ge(s["h"], 2 * l + 2)
                            if not first:
                                pe.wait_ge(s["ot"], 2 * l)
                            for q in range(4):
                                for k in range(KD):
                                    mm = pe.transpose(bank[6 + q // 2][0:SH, (q % 2) * D + k * P:(q % 2) * D + (k + 1) * P],
                                                      hf[:, k, q * SH:(q + 1) * SH], ident[:, :])
                                if q % 2:
                                    mm.then_inc(s["tr"], 1)

                    def body(i, first):
                        for m in range(M):
                            up(i, m)
                            if m >= 2:
                                down(i, m - 2)
                            elif not first:
                                down(i - 1, M - 2 + m)
                            if not first:
                                finish(i - 1, m, isz(i - 1))

                    for b in range(NB):
                        for n in range(8 * b, min(NW, 8 * b + 8)):
                            w, r = divmod(n, KD * M)
                            if w < (2 if gated else 1):
                                c, m = divmod(r, M)
                                src = w16[:, (w * KD * M + m * KD + c) * P:(w * KD * M + m * KD + c + 1) * P]
                            else:
                                m, c = divmod(r, KD)
                                src = w16[:, (w * KD * M + c * M + m) * P:(w * KD * M + c * M + m + 1) * P]
                            pe.wait_ge(s["cast"], w + 1)
                            mm = pe.transpose(bank[b].bitcast(F16)[:, (n - 8 * b) * P:(n - 8 * b + 1) * P], src, ident16[:, :])
                        mm.then_inc(s["turn"], 1)
                    pe.wait_ge(s["wt"], NB)
                    body(0, True)
                    body(1, False)
                    with pe.Fori(2, NT, 1) as i:
                        body(i, False)
                    for m in range(2):
                        down(NT - 1, M - 2 + m)
                    for m in range(M):
                        finish(NT - 1, m, False)

                @block.scalar
                def _(a):
                    def nonlinear(i, m):
                        n0 = M * i + m
                        a.wait_ge(s["up"], n0 + 1)
                        if gated:
                            if not (isinstance(i, int) and n0 < 2):
                                a.wait_ge(s["hid"], n0 - 1)
                            a.activation(act_g[:, m % 2, :], bank[2 * (m % UR)][:, 0:T], ACT.Silu, scale=Q).then_inc(s["act"], 1)
                        else:
                            if not (isinstance(i, int) and n0 < 2):
                                a.wait_ge(s["hl"], n0 - 1)
                            a.activation(hid[:, m % 2, :], bank[m % UR][:, 0:T], ACT.Gelu, scale=alpha1[:, m:m + 1],
                                         bias=b1_sb[:, m:m + 1]).then_inc(s["hid"], 1)

                    def finish(l, m):
                        if gated:
                            if m == 3:
                                ln.act_square(a, l, isz(l))
                            if m == 4:
                                ln.act_sd(a, l, isz(l))
                                ln.act_sd2(a, l, isz(l))
                            if m == 5:
                                ln.act_hi(a, cols(l), l)
                        elif m in (4, 5):
                            a.wait_ge(s["tr"], 2 * l + m - 3)
                            if m == 4 and not isz(l):
                                a.wait_ge(s["out"], 16 * l)
                            a.activation(ot[:, 2 * (m - 4):2 * (m - 4) + 2, :],
                                         bank[6 + m - 4][0:SH, :].rearrange("p (q d) -> p q d", q=2), ACT.Copy).then_inc(s["ot"], 1)

                    def body(i, first):
                        for m in range(M):
                            nonlinear(i, m)
                            if not first:
                                finish(i - 1, m)

                    n1 = KD * M * P
                    if gated:
                        a.activation(w16[:, 0:n1], raw_gate[:, :, :].rearrange("p c n -> p (c n)"), ACT.Copy).then_inc(s["cast"], 1)
                    else:
                        a.activation(w16[:, 0:n1], raw_w1[:, :, :].rearrange("p c n -> p (c n)"), ACT.Sign).then_inc(s["cast"], 1)
                        a.activation(w16[:, n1:2 * n1], raw_w2[:, :, :].rearrange("p c n -> p (c n)"), ACT.Sign).then_inc(s["cast"], 1)
                        a.wait_ge(s["alpha"], 4)
                    body(0, True)
                    body(1, False)
                    with a.Fori(2, NT, 1) as i:
                        body(i, False)
                    for m in range(M):
                        finish(NT - 1, m)

                @block.vector
                def _(v):
                    def hidden(i, m):
                        n0 = M * i + m
                        if gated:
                            v.wait_ge(s["act"], n0 + 1)
                            if not (isinstance(i, int) and n0 < 2):
                                v.wait_ge(s["hl"], n0 - 1)
                            v.scalar_tensor_tensor(out=hid[:, m % 2, :], in0=bank[2 * (m % UR) + 1][:, 0:T], scalar=Q,
                                                   in1=act_g[:, m % 2, :], op0=ALU.mult, op1=ALU.mult).then_inc(s["hid"], 1)
                        v.wait_ge(s["hid"], n0 + 1)
                        if not (isinstance(i, int) and n0 < HR):
                            v.wait_ge(s["dn"], n0 - HR + 1)
                        v.tensor_copy(hh[:, m % HR, :], hid[:, m % 2, :]).then_inc(s["hh"], 1)

                    def finish(l, m):
                        if m == 1:
                            v.wait_ge(s["dn"], M * l + M)
                            for k in range(KD):
                                if gated:
                                    v.scalar_tensor_tensor(out=hT[:, k, cols(l)], in0=bank[4 + k][:, 0:T], scalar=Q, in1=hT[:, k, cols(l)],
                                                           op0=ALU.mult, op1=ALU.add).then_inc(s["h"], 1)
                                else:
                                    if k == 0 and not isz(l):
                                        v.wait_ge(s["tr"], 2 * l)
                                    v.tensor_scalar(upd[:, k, :], bank[4 + k][:, 0:T], alpha2[:, k:k + 1], vec1[:, 3, k:k + 1],
                                                    ALU.mult, ALU.add).then_inc(s["upd"], 1)
                            if not gated:
                                v.wait_ge(s["upd"], 2 * l + 2)
                                for k in range(KD):
                                    v.tensor_tensor(hf[:, k, :], hT[:, k, cols(l)], upd[:, k, :], ALU.add).then_inc(s["h"], 1)
                        if gated:
                            if m == 2:
                                ln.dve_center(v, cols(l), l, isz(l))
                            if m == 4:
                                ln.dve_rstd(v, l, isz(l))
                                ln.dve_rstd2(v, l, isz(l))
                                ln.dve_scale(v, l, isz(l))
                            if m == 5:
                                ln.dve_scale2(v, l, isz(l))

                    def body(i, first):
                        for m in range(M):
                            hidden(i, m)
                            if not first:
                                finish(i - 1, m)

                    n1 = KD * M * P
                    if gated:
                        v.tensor_copy(w16[:, n1:2 * n1], raw_up[:, :, :].rearrange("p c n -> p (c n)")).then_inc(s["alpha"], 1)
                        v.wait_ge(s["cast"], 1)
                        v.tensor_copy(w16[:, 2 * n1:3 * n1], raw_down[:, :, :].rearrange("p c n -> p (c n)")).then_inc(s["cast"], 2)
                    else:
                        v.tensor_reduce(alpha1[:, :], raw_w1[:, :, :], AX.X, ALU.add, apply_absolute_value=True).then_inc(s["alpha"], 1)
                        v.tensor_reduce(alpha2[:, :], raw_w2[:, :, :], AX.X, ALU.add, apply_absolute_value=True).then_inc(s["alpha"], 1)
                        v.wait_ge(s["alpha"], 2)
                        v.tensor_scalar(alpha1[:, :], alpha1[:, :], 1.0 / D, None, ALU.mult).then_inc(s["alpha"], 1)
                        v.tensor_scalar(alpha2[:, :], alpha2[:, :], 1.0 / F1, None, ALU.mult).then_inc(s["alpha"], 1)
                    for b in range(NB):
                        v.wait_ge(s["turn"], b + 1)
                        n = min(NW, 8 * b + 8) - 8 * b
                        v.tensor_copy(wt[:, 8 * b:8 * b + n, :], bank[b].bitcast(F16)[:, 0:n * P].rearrange("p (n q) -> p n q", q=P)).then_inc(s["wt"], 1)
                    if not gated:
                        v.wait_ge(s["alpha"], 4)
                    body(0, True)
                    body(1, False)
                    with v.Fori(2, NT, 1) as i:
                        body(i, False)
                    for m in range(M):
                        finish(NT - 1, m)

                @block.gpsimd
                def _(p):
                    def low(i, m):
                        n0 = M * i + m
                        p.wait_ge(s["hh"], n0 + 1)
                        p.tensor_tensor(hl[:, m % HR, :], hid[:, m % 2, :], hh[:, m % HR, :], ALU.subtract).then_inc(s["hl"], 1)

                    def finish(l, m):
                        if gated and m == 4:
                            ln.pool_residual(p, cols(l), l)
                        if gated and m == 5:
                            ln.pool_lo(p, cols(l), l)

                    def body(i, first):
                        for m in range(M):
                            low(i, m)
                            if not first:
                                finish(i - 1, m)

                    body(0, True)
                    body(1, False)
                    with p.Fori(2, NT, 1) as i:
                        body(i, False)
                    for m in range(M):
                        finish(NT - 1, m)

                @block.sync
                def _(sp):
                    if not gated:
                        rows = out.rearrange("b s d -> (b s) d")
                        with sp.Fori(0, NT, 1) as i:
                            row, filled = sp.snap(i * T), sp.snap(2 * i + 2)
                            sp.wait_ge(s["ot"], filled)
                            sp.dma_start(rows[bass.ds(row, T), :].rearrange("(q p) d -> p q d", p=SH), ot[:, :, :]).then_inc(s["out"], 16)
                        sp.wait_ge(s["out"], 16 * NT)
            ph.close()

        ph = ctx.enter_context(ExitStack())
        xs = sb("xs", [BH, C, PT, GW, PT], scope=ph)
        xn0 = sb("xn0", [BH, GW, C, PT, PT], scope=ph)
        stats = sb("stats", [BH, GW, C, 6], scope=ph)
        mv = sb("mv", [BH, GW, 2], scope=ph)
        rs0 = sb("rs0", [BH, GW], scope=ph)
        sd0 = sb("sd0", [BH, GW], scope=ph)
        xpT = sb("xpT", [P, KP, GW, BH], scope=ph)
        tk = sb("tk", [P, KD, GW, BH], scope=ph)
        tsq = sb("tsq", [P, KD, NTI // 2], scope=ph)
        tsd = sb("tsd", [P, NTI // 2], scope=ph)
        trs = sb("trs", [P, NTI // 2], scope=ph)
        wm = sb("wm", [P, KP // C, C, D], scope=ph)
        tx = sb("tx", [ST, B, D], scope=ph)
        g1 = sb("g1", [P, KP // C, C], scope=ph)
        be1 = sb("be1", [P, KP // C, C], scope=ph)
        vec0 = sb("vec0", [P, 3, KD], scope=ph)
        pb = [ps(f"pb{i}", [P, 512], scope=ph) for i in range(8)]
        s = semaphores("x_in", "tok_in", "txt_in", "w_in", "bcast", "cst", "stats", "mv", "sd", "rstd", "xn",
                       "tr", "xp", "mlp", "tk", "mean", "txc", "tsq", "var", "tsd", "trs", "tnx", "taff", "h_img", "ttr", "h_txt")
        ln = Norm(pb[7])
        half = NTI // 2
        GPB = 512 // BH
        with nc.allow_non_contiguous_dma(reason="small vectors"), nc.Block() as block:
            @block.sync
            def _(sp):
                for b in range(B):
                    sp.dma_start(xs[b * GH:(b + 1) * GH, :, :, :, :].rearrange("h c p w q -> h c (p w q)"),
                                 x[b].rearrange("c (h p) w -> h c (p w)", p=PT)).then_inc(s["x_in"], 16)
                sp.dma_start(wm[:, :, :, :], tok_w.rearrange("(a p c) n -> p a c n", a=KP // C, c=C)).then_inc(s["tok_in"], 16)
                sp.dma_start(g1[:, :, :], tok_g1.rearrange("(a p c) -> p a c", a=KP // C, c=C)).then_inc(s["tok_in"], 16)
                sp.dma_start(be1[:, :, :], tok_b1.rearrange("(a p c) -> p a c", a=KP // C, c=C)).then_inc(s["tok_in"], 16)
                for i, v in enumerate((tok_bias, tok_g2, tok_b2)):
                    sp.dma_start(vec0[:, i, :], v.rearrange("(c p) -> p c", p=P)).then_inc(s["tok_in"], 16)
                for q in range(4):
                    b0, b9 = q * B // 4, (q + 1) * B // 4
                    sp.dma_start(tx[:, b0:b9, :], txt[b0:b9].rearrange("b t d -> t b d")).then_inc(s["txt_in"], 16)
                sp.dma_start(raw_qkv[:, :, :], w_qkv.rearrange("(c p) n -> p c n", p=P)).then_inc(s["w_in"], 16)
                sp.dma_start(raw_proj[:, :, :], w_proj.rearrange("(c p) n -> p c n", p=P)).then_inc(s["w_in"], 16)
                sp.dma_start(raw_gate[:, :, :], w_gate.rearrange("(c p) n -> p c n", p=P)).then_inc(s["w_in"], 16)
                sp.dma_start(raw_up[:, :, :], w_up.rearrange("(c p) n -> p c n", p=P)).then_inc(s["w_in"], 16)
                sp.dma_start(raw_down[:, :, :], w_down.rearrange("(c p) n -> p c n", p=P)).then_inc(s["w_in"], 16)
                for i, w in enumerate((wq1, wk1, wv1, wo1)):
                    sp.dma_start(raw_att1[:, i, :, :], w.rearrange("(c p) n -> p c n", p=P)).then_inc(s["w_in"], 16)
                sp.dma_start(raw_w1[:, :, :], w1.rearrange("(c p) n -> p c n", p=P)).then_inc(s["w_in"], 16)
                sp.dma_start(raw_w2[:, :, :], w2.rearrange("(c p) n -> p c n", p=P)).then_inc(s["w_in"], 16)
                for i, v in enumerate((bo1, ln_gamma, ln_beta, b2)):
                    sp.dma_start(vec1[:, i, :], v.rearrange("(c p) -> p c", p=P)).then_inc(s["w_in"], 16)
                sp.dma_start(b1_sb[:, :], b1.rearrange("(c p) -> p c", p=P)).then_inc(s["w_in"], 16)
                for i, v in enumerate((q_gamma, q_beta, k_gamma, k_beta)):
                    for h in range(HC):
                        sp.dma_start(gam[h * DH:(h + 1) * DH, i:i + 1], v.rearrange("(p a) -> p a", a=1)).then_inc(s["w_in"], 16)
                sp.wait_ge(s["w_in"], 16 * (16 + 4 * HC))

            @block.gpsimd
            def _(p):
                p.memset(ident[:, :], 0.0).then_inc(s["cst"], 1)
                p.wait_ge(s["cst"], 1)
                p.affine_select(out=ident[:, :], in_=ident[:, :], compare_op=ALU.not_equal, fill=1.0, base=0,
                                pattern=[[-1, P]], channel_multiplier=1).then_inc(s["cst"], 1)
                p.wait_ge(s["cst"], 2)
                p.tensor_copy(ident16[:, :], ident[:, :]).then_inc(s["cst"], 1)
                p.memset(ones_d[:, :], 1.0 / D).then_inc(s["cst"], 1)
                p.memset(eps_c[:, :], EPS).then_inc(s["cst"], 1)
                p.memset(eps_tok[:, :], EPS_TOK).then_inc(s["cst"], 1)
                p.memset(head_back[:, :, :], 1.0).then_inc(s["cst"], 1)
                p.memset(head_mean[:, :], 1.0 / DH).then_inc(s["cst"], 1)
                p.wait_ge(s["cst"], 8)
                for k in range(4):
                    p.affine_select(out=head_back[:, k, :], in_=head_back[:, k, :], compare_op=ALU.is_ge, fill=0.0,
                                    base=32 * DH * k, pattern=[[1, P]], channel_multiplier=-DH).then_inc(s["cst"], 1)
                p.affine_select(out=head_mean[:, :], in_=head_mean[:, :], compare_op=ALU.is_ge, fill=0.0,
                                base=0, pattern=[[-DH, 32]], channel_multiplier=1).then_inc(s["cst"], 1)
                p.wait_ge(s["cst"], 13)
                for k in range(4):
                    p.affine_select(out=head_back[:, k, :], in_=head_back[:, k, :], compare_op=ALU.is_ge, fill=0.0,
                                    base=DH - 1 - 32 * DH * k, pattern=[[-1, P]], channel_multiplier=DH).then_inc(s["cst"], 1)
                p.affine_select(out=head_mean[:, :], in_=head_mean[:, :], compare_op=ALU.is_ge, fill=0.0,
                                base=DH - 1, pattern=[[DH, 32]], channel_multiplier=-1).then_inc(s["cst"], 1)

                def pool_tile(i):
                    ln.pool_lo(p, bass.ds(i * T, T), i)
                with p.Fori(0, NT, 1) as i:
                    pool_tile(i)

            @block.vector
            def _(v):
                v.memset(bcast[:, :, :], 0.0).then_inc(s["bcast"], 1)
                v.wait_ge(s["bcast"], 1)
                for k in range(4):
                    v.memset(bcast[32 * k:32 * k + 32, k, :], 1.0 / 32).then_inc(s["bcast"], 1)
                v.wait_ge(s["x_in"], 16 * B)
                for w in range(GW):
                    for c in range(C):
                        m = v.bn_stats(stats[:, w, c, :], xs[:, c, :, w, :])
                    m.then_inc(s["stats"], 1)
                for w in range(GW):
                    v.wait_ge(s["stats"], w + 1)
                    v.bn_aggr(mv[:, w, :], stats[:, w, :, :]).then_inc(s["mv"], 1)
                v.wait_ge(s["sd"], 1)
                v.reciprocal(rs0[:, :], sd0[:, :]).then_inc(s["rstd"], 1)
                v.wait_ge(s["rstd"], 1)
                for w in range(GW):
                    for c in range(C):
                        m = v.tensor_scalar(xn0[:, w, c, :, :], xs[:, c, :, w, :], mv[:, w, 0:1], rs0[:, w:w + 1],
                                            ALU.subtract, ALU.mult)
                    m.then_inc(s["xn"], 1)
                v.wait_ge(s["tok_in"], 16 * 6)
                for k in range(KP):
                    for g in range(2):
                        v.wait_ge(s["tr"], 2 * k + g + 1)
                        c, a = k % C, k // C
                        v.tensor_scalar(xpT[:, k, g * 3:g * 3 + 3, :], pb[(2 * k + g) % 4][:, 0:3 * BH].rearrange("p (w n) -> p w n", w=3),
                                        g1[:, a, c:c + 1], be1[:, a, c:c + 1], ALU.mult, ALU.add).then_inc(s["xp"], 1)
                for g in range(2):
                    tg = tk[:, :, g * 3:g * 3 + 3, :].rearrange("p c w n -> p c (w n)")
                    for c in range(KD):
                        v.wait_ge(s["mlp"], 2 * g + c + 1)
                        v.tensor_scalar(tg[:, c, :], pb[4 + c][:, 0:half], vec0[:, 0, c:c + 1], None, ALU.add).then_inc(s["tk"], 1)
                    v.wait_ge(s["mean"], g + 1)
                    v.wait_ge(s["tk"], 2 * g + 2)
                    for c in range(KD):
                        m = v.tensor_tensor(tg[:, c, :], tg[:, c, :], pb[6][:, 0:half], ALU.subtract)
                    m.then_inc(s["txc"], 1)
                    v.wait_ge(s["tsd"], g + 1)
                    v.reciprocal(trs[:, :], tsd[:, :]).then_inc(s["trs"], 1)
                    v.wait_ge(s["trs"], g + 1)
                    for c in range(KD):
                        m = v.tensor_tensor(tg[:, c, :], tg[:, c, :], trs[:, :], ALU.mult)
                    m.then_inc(s["tnx"], 1)
                    v.wait_ge(s["tnx"], g + 1)
                    for c in range(KD):
                        for w in range(g * 3, g * 3 + 3):
                            dst = hT[:, c, :].rearrange("p (b s) -> p b s", b=B)[:, :, w:NI:GW]
                            m = v.tensor_scalar(dst, tk[:, c, w, :].rearrange("p (b h) -> p b h", b=B),
                                                vec0[:, 1, c:c + 1], vec0[:, 2, c:c + 1], ALU.mult, ALU.add)
                    m.then_inc(s["h_img"], 1)
                v.wait_ge(s["h_img"], 2)
                v.wait_ge(s["h_txt"], B)

                def tile(i, first):
                    cols = bass.ds(i * T, T)
                    ln.dve_center(v, cols, i, first)
                    ln.dve_rstd(v, i, first)
                    ln.dve_scale(v, i, first)
                tile(0, True)
                with v.Fori(1, NT, 1) as i:
                    tile(i, False)

            @block.scalar
            def _(a):
                a.wait_ge(s["cst"], 6)
                a.wait_ge(s["mv"], GW)
                a.activation(sd0[:, :], mv[:, :, 1], ACT.Sqrt, bias=eps_tok[0:BH, 0:1]).then_inc(s["sd"], 1)
                for b in range(B):
                    a.wait_ge(s["ttr"], b + 1)
                    a.activation(hT[:, :, b * S + NI:(b + 1) * S],
                                 pb[6 + b % 2][:, 0:KD * ST].rearrange("p (c t) -> p c t", c=KD), ACT.Copy).then_inc(s["h_txt"], 1)
                for g in range(2):
                    a.wait_ge(s["txc"], g + 1)
                    if g:
                        a.wait_ge(s["var"], g)
                    a.activation(tsq[:, :, :], tk[:, :, g * 3:g * 3 + 3, :].rearrange("p c w n -> p c (w n)"), ACT.Square).then_inc(s["tsq"], 1)
                    a.wait_ge(s["var"], g + 1)
                    if g:
                        a.wait_ge(s["trs"], g)
                    a.activation(tsd[:, :], pb[6][:, 0:half], ACT.Sqrt, bias=eps_tok[:, 0:1]).then_inc(s["tsd"], 1)

                def tile(i, first):
                    ln.act_square(a, i, first)
                    ln.act_sd(a, i, first)
                    ln.act_hi(a, bass.ds(i * T, T), i)
                tile(0, True)
                with a.Fori(1, NT, 1) as i:
                    tile(i, False)

            @block.tensor
            def _(pe):
                pe.wait_ge(s["cst"], 6)
                for b in range(B):
                    pe.wait_ge(s["txt_in"], 16 * 4)
                    if b >= 2:
                        pe.wait_ge(s["h_txt"], b - 1)
                    for c in range(KD):
                        m = pe.transpose(pb[6 + b % 2][:, c * ST:(c + 1) * ST], tx[:, b, c * P:(c + 1) * P], ident[0:ST, 0:ST])
                    m.then_inc(s["ttr"], 1)
                for k in range(KP):
                    c, a = k % C, k // C
                    for g in range(2):
                        j = 2 * k + g
                        pe.wait_ge(s["xn"], g * 3 + 3)
                        if j >= 4:
                            pe.wait_ge(s["xp"], j - 3)
                        for w in range(3):
                            m = pe.transpose(pb[j % 4][:, w * BH:(w + 1) * BH],
                                             xn0[:, g * 3 + w, c, a * 8:(a + 1) * 8, :].rearrange("n p q -> n (p q)"), ident[0:BH, 0:BH])
                        m.then_inc(s["tr"], 1)
                pe.wait_ge(s["h_txt"], B)
                for g in range(2):
                    pe.wait_ge(s["xp"], 2 * KP)
                    for n in range(KD):
                        if g:
                            pe.wait_ge(s["tk"], 2)
                        for k in range(KP):
                            c, a = k % C, k // C
                            m = pe.matmul(pb[4 + n][:, 0:half], wm[:, a, c, n * P:(n + 1) * P],
                                          xpT[:, k, g * 3:g * 3 + 3, :].rearrange("p w n -> p (w n)"), start=(k == 0), stop=(k == KP - 1))
                        m.then_inc(s["mlp"], 1)
                    pe.wait_ge(s["tk"], 2 * g + 2)
                    if g:
                        pe.wait_ge(s["tsd"], g)
                    for c in range(KD):
                        m = pe.matmul(pb[6][:, 0:half], ones_d[:, :], tk[:, c, g * 3:g * 3 + 3, :].rearrange("p w n -> p (w n)"),
                                      start=(c == 0), stop=(c == KD - 1))
                    m.then_inc(s["mean"], 1)
                    pe.wait_ge(s["tsq"], g + 1)
                    for c in range(KD):
                        m = pe.matmul(pb[6][:, 0:half], ones_d[:, :], tsq[:, c, :], start=(c == 0), stop=(c == KD - 1))
                    m.then_inc(s["var"], 1)
                pe.wait_ge(s["h_img"], 2)
                pe.wait_ge(s["h_txt"], B)

                def tile(i, first):
                    if not first:
                        pe.wait_ge(ln.done, i)
                    ln.pe_mean(pe, bass.ds(i * T, T), i)
                    ln.pe_var(pe, i)
                    if first:
                        pe.wait_ge(s["cst"], 18)
                        pe.wait_ge(s["bcast"], 5)
                    ln.pe_bcast(pe, i)
                tile(0, True)
                with pe.Fori(1, NT, 1) as i:
                    tile(i, False)
        ph.close()
        attention(0)
        feed_forward(0)
        attention(1)
        feed_forward(1)


_INS = ['x', 'txt', 'L0_tok_g1', 'L0_tok_b1', 'L0_tok_W_mlp', 'L0_tok_b_mlp', 'L0_tok_g2', 'L0_tok_b2',
        'L0_attn_w_qkv', 'L0_attn_w_proj', 'L0_attn_q_gamma', 'L0_attn_q_beta', 'L0_attn_k_gamma', 'L0_attn_k_beta',
        'L0_ffn_w_gate', 'L0_ffn_w_up', 'L0_ffn_w_down', 'L1_attn_Wq', 'L1_attn_Wk', 'L1_attn_Wv', 'L1_attn_Wo',
        'L1_attn_bo', 'L1_attn_ln_gamma', 'L1_attn_ln_beta', 'L1_ffn_w1', 'L1_ffn_b1', 'L1_ffn_w2', 'L1_ffn_b2']


def kernel(**inputs):
    import numpy as _np
    import concourse.bacc as _bacc
    from concourse import mybir as _mybir
    from concourse.bass_utils import run_bass_kernel_spmd as _run

    nc = _bacc.Bacc("TRN2", target_bir_lowering=False, num_devices=1)
    arrays, args = {}, []
    for name in _INS:
        a = _np.ascontiguousarray(inputs[name])
        arrays[f"in_{name}"] = a
        args.append(nc.dram_tensor(f"in_{name}", a.shape, _mybir.dt.from_np(a.dtype), kind="ExternalInput").ap())
    shape = (inputs['x'].shape[0], (inputs['x'].shape[2] // 16) * (inputs['x'].shape[3] // 16) + inputs['txt'].shape[1],
             inputs['txt'].shape[2])
    args.append(nc.dram_tensor("out0", shape, _mybir.dt.float32, kind="ExternalOutput").ap())
    fused_block(nc, *args)
    r = _run(nc, [arrays], core_ids=[0])
    return r.results[0]["out0"]
```

```python
from contextlib import ExitStack

import concourse.bass as bass
from concourse import mybir

ALU = mybir.AluOpType
ACT = mybir.ActivationFunctionType
F32 = mybir.dt.float32
F16 = mybir.dt.float16
I32 = mybir.dt.int32
AX = mybir.AxisListType

P = 128
EPS = 1e-5
EPS_TOK = -1e-5
WS = 64.0



def fused_block(nc, x, txt, tok_g1, tok_b1, tok_w, tok_bias, tok_g2, tok_b2, w_qkv, w_proj, q_gamma, q_beta,
                k_gamma, k_beta, w_gate, w_up, w_down, wq1, wk1, wv1, wo1, bo1, ln_gamma, ln_beta,
                w1, b1, w2, b2, out):
    B, C, HI, WI = x.shape
    _, ST, D = txt.shape
    KD = D // P
    PT = 16
    GH, GW = HI // PT, WI // PT
    NI = GH * GW
    S = NI + ST
    N = B * S
    T = 2 * S
    NT = N // T
    SH = S // 2
    DH = q_gamma.shape[0]
    H = D // DH
    HC = P // DH
    PD = PT * PT * C
    KP = PD // P
    NTI = B * NI
    BH = B * GH
    F0 = w_gate.shape[0]
    K0 = F0 // P
    F1 = w1.shape[0]
    K1 = F1 // P
    assert D == 256 and KD == 2 and DH == 16 and SH <= P and T <= 512 and N % T == 0 and NT % 2 == 0

    with ExitStack() as ctx:
        def sb(name, shape, dt=F32, scope=ctx):
            return scope.enter_context(nc.sbuf_tensor(name, shape, dt))

        def ps(name, shape, dt=F32, scope=ctx):
            return scope.enter_context(nc.psum_tensor(name, shape, dt))

        hT = sb("hT", [P, KD, N])
        xh = sb("xh", [P, KD, N], F16)
        xl = sb("xl", [P, KD, N], F16)
        ident = sb("ident", [P, P])
        ident16 = sb("ident16", [P, P], F16)
        ones_d = sb("ones_d", [P, P])
        eps_tok = sb("eps_tok", [P, 1])
        three_halves = sb("three_halves", [P, SH])
        vec1 = sb("vec1", [P, 6, KD])
        b1_sb = sb("b1_sb", [P, K1])
        bcast = sb("bcast", [P, 4, P])
        head_mean = sb("head_mean", [P, 4, 32])
        head_back = sb("head_back", [P, 4, 4, P])
        beta = sb("beta", [P, 2])
        lnw = {k: sb("ln_" + k, [P, KD, T]) for k in ("xc", "sq", "xn", "z")}
        lnw |= {k: sb("ln_" + k, [P, 2 * SH]) for k in ("ve", "rstd", "t")}

        wqkv = [sb(f"wqkv{i}", [P, KD, 3 * D], F16) for i in range(2)]
        wpro = [sb(f"wpro{i}", [P, KD, D], F16) for i in range(2)]
        qs = [[sb(f"qs{i}{h}", [P, H // 2, T], F16) for h in range(2)] for i in range(2)]
        ks = [sb(f"ks{i}", [P, H // 2, T], F16) for i in range(2)]
        vp = [sb(f"vp{i}", [SH, 2, 2, H // 2, 2, 32]) for i in range(2)]
        onesv = sb("onesv", [SH, 2, 32])
        weights0 = ctx.enter_context(ExitStack())
        raw_qkv = sb("raw_qkv", [P, KD, 3 * D], scope=weights0)
        raw_proj = sb("raw_proj", [P, KD, D], scope=weights0)
        names = iter(range(10000))
        live = []

        def semaphores(*keys):
            n = next(names)
            new = {k: nc.alloc_semaphore(name=f"p{n}_{k}") for k in keys}
            live.extend(new.values())
            return new

        def end_phase():
            nc.clear_and_free_semaphores(live)
            live.clear()
            nc.all_engine_barrier()

        ROOT_POOL, ROOT_DVE = 13, 10

        def root_guess(v, x, r, steps, n):
            v.tensor_scalar(r.bitcast(I32), x.bitcast(I32), -0.5, float(0x5F3759DF - 2 ** 22 - 2 ** 30), ALU.mult, ALU.add).then_inc(steps, 1)

        def root_steps(e, fused, x, r, t, steps, n, part=range(3)):
            base = (ROOT_DVE if fused else ROOT_POOL) * n
            for k in part:
                done = base + 1 + (3 if fused else 4) * k
                e.wait_ge(steps, done)
                e.tensor_tensor(t, r, r, ALU.mult).then_inc(steps, 1)
                e.wait_ge(steps, done + 1)
                e.tensor_tensor(t, t, x, ALU.mult).then_inc(steps, 1)
                e.wait_ge(steps, done + 2)
                if fused:
                    e.scalar_tensor_tensor(out=r, in0=t, scalar=1.5, in1=r, op0=ALU.add, op1=ALU.mult).then_inc(steps, 1)
                else:
                    e.tensor_tensor(t, t, three_halves[:, :], ALU.add).then_inc(steps, 1)
                    e.wait_ge(steps, done + 3)
                    e.tensor_tensor(r, r, t, ALU.mult).then_inc(steps, 1)

        class Norm:
            def __init__(self, bank, fused, twice=False, work=None):
                self.fused = fused
                self.NR = ROOT_DVE if fused else ROOT_POOL
                self.w = work or lnw
                more = ("ln_z", "ln_bc2", "ln_x2", "ln_res") if twice else ()
                self.s = semaphores("ln_mean", "ln_xc", "ln_sq", "ln_var", "ln_ve", "ln_root", "ln_bc", "ln_xn", "ln_hi", "ln_lo", *more)
                self.bank = bank
                self.twice = twice
                self.done = self.s["ln_x2" if twice else "ln_xn"]
                self.last_bc = self.s["ln_bc2" if twice else "ln_bc"]

            def pe_mean(self, pe, cols, n):
                for c in range(KD):
                    m = pe.matmul(self.bank[:, 0:T], ones_d[:, :], hT[:, c, cols], start=(c == 0), stop=(c == KD - 1))
                m.then_inc(self.s["ln_mean"], 1)

            def dve_center(self, v, cols, n, first):
                v.wait_ge(self.s["ln_mean"], n + 1)
                if not first:
                    v.wait_ge(self.s["ln_sq"], n)
                    v.wait_ge(self.done, n)
                for c in range(KD):
                    m = v.tensor_tensor(self.w["xc"][:, c, :], hT[:, c, cols], self.bank[:, 0:T], ALU.subtract)
                m.then_inc(self.s["ln_xc"], 1)

            def act_square(self, a, n, first):
                a.wait_ge(self.s["ln_xc"], n + 1)
                if not first:
                    a.wait_ge(self.s["ln_var"], n)
                a.activation(self.w["sq"][:, :, :], self.w["xc"][:, :, :], ACT.Square).then_inc(self.s["ln_sq"], 1)

            def pe_var(self, pe, n):
                pe.wait_ge(self.s["ln_sq"], n + 1)
                pe.wait_ge(self.s["ln_xc"], n + 1)
                for c in range(KD):
                    for k in range(4):
                        m = pe.matmul(self.bank[32 * k:32 * k + 32, 0:SH], ones_d[:, 0:32], self.w["sq"][:, c, k * SH:(k + 1) * SH],
                                      start=(c == 0), stop=(c == KD - 1))
                m.then_inc(self.s["ln_var"], 1)

            def dve_ve(self, v, n, first):
                v.wait_ge(self.s["ln_var"], n + 1)
                if not first:
                    v.wait_ge(self.s["ln_root"], self.NR * n)
                m = v.tensor_scalar(self.w["ve"][:, 0:SH], self.bank[:, 0:SH], -0.5, -0.5 * EPS, ALU.mult, ALU.add)
                if self.twice:
                    m = v.tensor_scalar(self.w["ve"][:, SH:2 * SH], self.bank[:, 0:SH], -0.5 * (1.0 + EPS), -0.5 * EPS * EPS, ALU.mult, ALU.add)
                m.then_inc(self.s["ln_ve"], 1)

            def dve_guess(self, v, n, first):
                w = slice(0, 2 * SH if self.twice else SH)
                v.wait_ge(self.s["ln_ve"], n + 1)
                if not first:
                    v.wait_ge(self.last_bc, n)
                root_guess(v, self.w["ve"][:, w], self.w["rstd"][:, w], self.s["ln_root"], n)

            def steps(self, e, n, part=range(3)):
                w = slice(0, 2 * SH if self.twice else SH)
                root_steps(e, self.fused, self.w["ve"][:, w], self.w["rstd"][:, w], self.w["t"][:, w], self.s["ln_root"], n, part)

            def pe_bcast(self, pe, n):
                pe.wait_ge(self.s["ln_root"], self.NR * n + self.NR)
                for k in range(4):
                    m = pe.matmul(self.bank[:, k * SH:(k + 1) * SH], bcast[:, k, :], self.w["rstd"][:, 0:SH], start=True, stop=True)
                m.then_inc(self.s["ln_bc"], 1)

            def dve_scale(self, v, n, first):
                if not first and not self.twice:
                    v.wait_ge(self.s["ln_hi"], n)
                    v.wait_ge(self.s["ln_lo"], n)
                if not first and self.twice:
                    v.wait_ge(self.s["ln_res"], n)
                v.wait_ge(self.s["ln_bc"], n + 1)
                dst = self.w["z"] if self.twice else self.w["xn"]
                for c in range(KD):
                    m = v.tensor_tensor(dst[:, c, :], self.w["xc"][:, c, :], self.bank[:, 0:T], ALU.mult)
                m.then_inc(self.s["ln_z" if self.twice else "ln_xn"], 1)

            def pool_residual(self, p, cols, n):
                p.wait_ge(self.s["ln_z"], n + 1)
                p.tensor_tensor(hT[:, :, cols], hT[:, :, cols], self.w["z"][:, :, :], ALU.add).then_inc(self.s["ln_res"], 1)

            def pe_bcast2(self, pe, n):
                pe.wait_ge(self.s["ln_z"], n + 1)
                for k in range(4):
                    m = pe.matmul(self.bank[:, k * SH:(k + 1) * SH], bcast[:, k, :], self.w["rstd"][:, SH:2 * SH], start=True, stop=True)
                m.then_inc(self.s["ln_bc2"], 1)

            def dve_scale2(self, v, n, first):
                v.wait_ge(self.s["ln_bc2"], n + 1)
                if not first:
                    v.wait_ge(self.s["ln_hi"], n)
                    v.wait_ge(self.s["ln_lo"], n)
                for c in range(KD):
                    m = v.tensor_tensor(self.w["xn"][:, c, :], self.w["xc"][:, c, :], self.bank[:, 0:T], ALU.mult)
                m.then_inc(self.s["ln_x2"], 1)
                v.wait_ge(self.s["ln_x2"], n + 1)
                for c in range(KD):
                    m = v.tensor_scalar(self.w["xn"][:, c, :], self.w["xn"][:, c, :], vec1[:, 1, c:c + 1], vec1[:, 2, c:c + 1],
                                        ALU.mult, ALU.add)
                m.then_inc(self.s["ln_xn"], 1)

            def act_hi(self, a, cols, n):
                a.wait_ge(self.s["ln_xn"], n + 1)
                a.activation(xh[:, :, cols], self.w["xn"][:, :, :], ACT.Copy).then_inc(self.s["ln_hi"], 1)

            def pool_lo(self, p, cols, n):
                p.wait_ge(self.s["ln_hi"], n + 1)
                p.tensor_tensor(xl[:, :, cols], self.w["xn"][:, :, :], xh[:, :, cols], ALU.subtract).then_inc(self.s["ln_lo"], 1)

        def attention(layer):
            ph = ExitStack()
            first_layer = layer == 0
            twice = False
            NP = 3 if first_layer else 4
            KR = 64 + NP * DH
            KX = KR + 2 if first_layer else KR
            HP = H // 2
            JJ = HC // 2
            PR = 4
            QK = 1
            HIGH = 23 if first_layer else 5
            LAG = 2 if first_layer else 3
            qc = sb(f"qc{layer}", [P, 4, T], scope=ph)
            qkh = sb(f"qkh{layer}", [P, 4, T], F16, ph)
            qkl = sb(f"qkl{layer}", [P, 4, T], F16, ph)
            pr = sb(f"pr{layer}", [SH, PR, JJ, T], scope=ph)
            rden = sb(f"rden{layer}", [P, 2, S], scope=ph)
            on = sb(f"on{layer}", [P, KD, T], scope=ph)
            oh = sb(f"oh{layer}", [P, KD, T], F16, ph)
            ol = sb(f"ol{layer}", [P, KD, T], F16, ph)
            if first_layer:
                qsq = sb("qsq", [P, 4, T], scope=ph)
                qve = sb("qve", [P, SH], scope=ph)
                qnt = sb("qnt", [P, SH], scope=ph)
                qrs = sb("qrs", [P, SH], scope=ph)
                mx = sb("mx", [SH, 2, 2, H], scope=ph)
                ml = sb("ml", [SH, 2, 2, 2, H], F16, ph)
                mt = sb("mt", [2 * H, 2, S], F16, ph)
            else:
                bo01 = sb("bo01", [P, KD], scope=ph)
                upd = sb("upd", [P, KD, T], scope=ph)
            bank = [ps(f"at{layer}{i}", [P, 512], scope=ph) for i in range(8)]
            dense, maxb, expb, avb = bank[0:2], bank[2:4], bank[4:6] if first_layer else bank[2:6], bank[6:8]
            ER = len(expb)
            bounce = nc.dram_tensor(f"bounce{layer}", (2, 2, 4, P, T), F16).ap()
            own = (("qsq", "qvar", "qve", "qroot", "qbc", "qn", "qa", "mm", "mx", "ml", "mt", "mtc", "mrow") if first_layer
                   else ("cl", "up", "att_in", "prep", "zero", "wt", "wcp"))
            s = semaphores("w_in", "qk", "qc", "qhi", "qlo", "qout", "kout", "stk", "v", "vp", "sc", "ex", "av",
                           "rd", "on", "ohi", "olo", "pj", "h", *own)
            ln = Norm(dense[0], False)
            NS = 2 * H
            seq = lambda i, bb: bass.ds(i * T + bb * S, S)
            cols = lambda i: bass.ds(i * T, T)
            UPS = 2 * 2 * 6
            unit = lambda u: (u // 12, u // 6 % 2, u % 6 // 3, u % 3 * 3, 3 if u % 3 < 2 else 2)

            with nc.allow_non_contiguous_dma(reason="rows of a head"), nc.Block() as block:
                @block.tensor
                def _(pe):
                    last = {}

                    def claim(b, sem, value):
                        if b in last:
                            pe.wait_ge(*last[b])
                        last[b] = (s[sem] if isinstance(sem, str) else sem, value)

                    def qk(a, k):
                        claim(k % 2, "qc", 4 * a + k + 1)
                        b = dense[k % 2]
                        n = 0
                        for wi, xi in ((0, xh), (1, xh), (0, xl)):
                            for c in range(KD):
                                m = pe.matmul(b[:, 0:T], wqkv[wi][:, c, k * P:(k + 1) * P], xi[:, c, cols(a)], start=(n == 0), stop=(n == 5))
                                n += 1
                        m.then_inc(s["qk"], 1)

                    def qvar(a):
                        pe.wait_ge(s["qsq"], 4 * a + 4)
                        claim(1, "qve", a + 1)
                        for k in range(4):
                            for j in range(4):
                                m = pe.matmul(dense[1][32 * j:32 * j + 32, 0:SH], head_mean[:, k, :], qsq[:, k, j * SH:(j + 1) * SH],
                                              start=(k == 0), stop=(k == 3))
                        m.then_inc(s["qvar"], 1)

                    def qbc(a, k):
                        pe.wait_ge(s["qroot"], ROOT_POOL * (a + 1))
                        b = (1, 0, 1, 0)[k]
                        claim(b, "qn", 4 * a + k + 1)
                        for j in range(4):
                            m = pe.matmul(dense[b][:, j * SH:(j + 1) * SH], head_back[:, j, k, :], qrs[:, :], start=True, stop=True)
                        m.then_inc(s["qbc"], 1)

                    def maxima(b, u, par):
                        bb, qt, hh, p0, n = unit(u)
                        if u == 0:
                            pe.wait_ge(s["stk"], 192 * (b + 1))
                        if not (isinstance(b, int) and b == 0 and u < 2):
                            pe.wait_ge(s["mx"], UPS * b + u - 1)
                        for x in range(n):
                            m = pe.matmul(maxb[u % 2][0:SH, x * S:(x + 1) * S],
                                          qs[par][hh][0:KR, p0 + x, bb * S + qt * SH:bb * S + (qt + 1) * SH],
                                          ks[par][0:KR, p0 + x, bb * S:(bb + 1) * S], start=True, stop=True)
                        m.then_inc(s["mm"], 1)

                    def turn_maxima(b, bb):
                        pe.wait_ge(s["ml"], 4 * b + 2 * bb + 2)
                        claim(1, "mtc", 2 * b + bb + 1)
                        for qt in range(2):
                            m = pe.transpose(dense[1].bitcast(F16)[0:2 * H, qt * SH:(qt + 1) * SH],
                                             ml[:, bb, qt, :, :].rearrange("p a b -> p (a b)"), ident16[0:SH, 0:SH])
                        m.then_inc(s["mt"], 1)

                    def values(b, bb, kt):
                        if kt == 0:
                            claim(1 - bb, "vp", 4 * b + 2 * bb + 2)
                        n = 0
                        for xi, wi in ((xh, 0), (xh, 1), (xl, 0)):
                            for c in range(KD):
                                m = pe.matmul(dense[1 - bb][0:SH, kt * D:(kt + 1) * D], xi[:, c, bass.ds(b * T + bb * S + kt * SH, SH)],
                                              wqkv[wi][:, c, 2 * D:3 * D], start=(n == 0), stop=(n == 5))
                                n += 1
                        if kt:
                            m.then_inc(s["v"], 1)

                    def scores(i, g, par):
                        t, jj = g // 4, g % 4
                        bb, c, hh = t // 4, t // 2 % 2, t % 2
                        if g % H == 0:
                            if first_layer:
                                pe.wait_ge(s["mrow"], 64 * (2 * i + bb + 1))
                            elif g == 0:
                                pe.wait_ge(s["stk"], 256 * (i + 1))
                        if not (isinstance(i, int) and NS * i + g < ER):
                            pe.wait_ge(s["ex" if first_layer else "cl"], NS * i + g - ER + 1)
                        for kt in range(2):
                            m = pe.matmul(expb[g % ER][0:SH, kt * S:(kt + 1) * S],
                                          ks[par][0:KX, c * JJ + jj, bb * S + kt * SH:bb * S + (kt + 1) * SH],
                                          qs[par][hh][0:KX, c * JJ + jj, bb * S:(bb + 1) * S], start=True, stop=True)
                        m.then_inc(s["sc"], 1)

                    def weighted(i, t, q, par):
                        bb, c, hh = t // 4, t // 2 % 2, t % 2
                        kt, sums = q // 2, q % 2
                        if q == 0:
                            pe.wait_ge(s["ex"], NS * i + 4 * t + 4 if first_layer else 8 * i + t + 1)
                            if t % 4 == 0:
                                pe.wait_ge(s["vp"], 4 * i + 2 * bb + 2)
                            if hh == 0 and not (isinstance(i, int) and 4 * i + 2 * bb + c - 1 <= 0):
                                pe.wait_ge(s["on"], 4 * i + 2 * bb + c - 1)
                        for jj in range(JJ):
                            lhs = onesv[:, hh, :] if sums else vp[par][:, bb, kt, c * JJ + jj, hh, :]
                            m = pe.matmul(avb[c][32 * jj:32 * jj + 32, sums * S:(sums + 1) * S], lhs,
                                          pr[:, t % PR, jj, kt * S:(kt + 1) * S], start=(hh == 0 and q == 0), stop=(hh == 1 and kt == 1),
                                          skip_group_check=True)
                        if q == 3:
                            m.then_inc(s["av"], 1)

                    def project(l, k):
                        pe.wait_ge(s["olo"], 4 * l + 4)
                        claim(1 - k, "h" if first_layer else "up", 2 * l + k + 1)
                        n = 0
                        for wi, oi in ((0, oh), (1, oh), (0, ol)):
                            for c in range(KD):
                                m = pe.matmul(dense[1 - k][:, 0:T], wpro[wi][:, c, k * P:(k + 1) * P], oi[:, c, :], start=(n == 0), stop=(n == 5))
                                n += 1
                        m.then_inc(s["pj"], 1)

                    def norm_mean(l):
                        pe.wait_ge(s["h"], 2 * l + 2)
                        claim(0, ln.s["ln_xc"], l + 1)
                        ln.pe_mean(pe, cols(l), l)

                    def norm_var(l):
                        ln.pe_var(pe, l)
                        last[0] = (ln.s["ln_ve"], l + 1)

                    def norm_back(l):
                        claim(0, ln.done, l + 1)
                        ln.pe_bcast(pe, l)

                    def body(i, par, first, has_a, has_b):
                        a, b, l = i + 2, i + 1, i - 1
                        for g in range(NS):
                            scores(i, g, par)
                            t, q = divmod(g - 4 - LAG, 4)
                            if t >= 0:
                                weighted(i, t, q, par)
                            elif not first:
                                weighted(i - 1, 8 + t, q, 1 - par)
                            if first_layer and first and g < 6:
                                for u in range(2):
                                    maxima(i, UPS // 2 + 2 * g + u, par)
                            if first_layer and g == 6:
                                turn_maxima(i, 1)
                            if has_a and g == QK:
                                for k in range(4):
                                    qk(a, k)
                            if has_b and 7 <= g < 11:
                                values(b, (g - 7) // 2, (g - 7) % 2)
                            if first_layer and has_b and 8 <= g < 8 + UPS:
                                maxima(b, g - 8, 1 - par)
                            if not first and g in (12, 13):
                                project(l, g - 12)
                            if first_layer and has_a and g == 11:
                                qvar(a)
                            if not first and g == 16:
                                norm_mean(l)
                            if not first and g == 19:
                                norm_var(l)
                            if first_layer and has_b and g == 21:
                                turn_maxima(b, 0)
                            if first_layer and has_a and 22 <= g < 26:
                                qbc(a, g - 22)
                            if not first and g == 26:
                                norm_back(l)

                    def prologue():
                        if not first_layer:
                            pe.wait_ge(s["att_in"], 64)
                            for w in range(4):
                                for ci in range(KD):
                                    for co in range(KD):
                                        m = pe.transpose(bank[w][:, ci * D + co * P:ci * D + (co + 1) * P],
                                                         raw_att1[:, w, co, ci * P:(ci + 1) * P], ident[:, :])
                                m.then_inc(s["wt"], 1)
                            pe.wait_ge(s["prep"], 4)
                        for a in range(2):
                            for k in range(4):
                                qk(a, k)
                            if first_layer:
                                qvar(a)
                                for k in range(4):
                                    qbc(a, k)
                        for bb in range(2):
                            for kt in range(2):
                                values(0, bb, kt)
                        if first_layer:
                            for u in range(UPS // 2):
                                maxima(0, u, 0)
                            turn_maxima(0, 0)

                    def epilogue():
                        l = NT - 1
                        for g in range(NS, NS + 4 + LAG):
                            t, q = divmod(g - 4 - LAG, 4)
                            weighted(l, t, q, l % 2)
                        for k in range(KD):
                            project(l, k)
                        norm_mean(l)
                        norm_var(l)
                        norm_back(l)

                    prologue()
                    for i in range(2):
                        body(i, i, i == 0, True, True)
                    steady = ({0: (ln.done, lambda i: i - 1), 1: (s["qn"], lambda i: 4 * i + 7)} if first_layer else
                              {0: (ln.done, lambda i: i - 1), 1: (s["up"], lambda i: 2 * i - 3)})
                    with pe.Fori(1, NT // 2 - 1, 1) as half:
                        for u in range(2):
                            i = half * 2
                            last.update({b: (sem, f(i + u)) for b, (sem, f) in steady.items()})
                            body(i + u, u, False, True, True)
                    for i in range(NT - 2, NT):
                        last.update({b: (sem, f(NT - 2)) for b, (sem, f) in steady.items()} if i == NT - 2 else {})
                        body(i, i % 2, False, False, i < NT - 1)
                    epilogue()

                @block.scalar
                def _(act):
                    def copy_qk(a, k):
                        act.wait_ge(s["qk"], 4 * a + k + 1)
                        if not (isinstance(a, int) and a == 0):
                            act.wait_ge(s["qlo"], 4 * a + k - 3)
                        scale = 1 / WS if first_layer else (0.5 * DH ** -0.5 if k < 2 else 1.0)
                        act.activation(qc[:, k, :], dense[k % 2][:, 0:T], ACT.Copy, scale=scale).then_inc(s["qc"], 1)

                    def high_qk(a, k):
                        if first_layer:
                            act.wait_ge(s["qn"], 4 * a + k + 1)
                            act.activation(qc[:, k, :], qc[:, k, :], ACT.Identity, bias=beta[:, k // 2:k // 2 + 1]).then_inc(s["qa"], 1)
                        act.wait_ge(s["qa" if first_layer else "qc"], 4 * a + k + 1)
                        if not (isinstance(a, int) and a == 0):
                            act.wait_ge(s[("qout", "kout")[k // 2]], 32 * a)
                        act.activation(qkh[:, k, :], qc[:, k, :], ACT.Copy).then_inc(s["qhi"], 1)

                    def exponentials(i, g):
                        t, jj = g // 4, g % 4
                        if first_layer:
                            act.wait_ge(s["sc"], NS * i + g + 1)
                            if jj == 0 and not (isinstance(i, int) and 8 * i + t - PR + 1 <= 0):
                                act.wait_ge(s["av"], 8 * i + t - PR + 1)
                            act.activation(pr[:, t % PR, jj, :], expb[g % ER][0:SH, 0:T], ACT.Exp, scale=DH ** -0.5).then_inc(s["ex"], 1)
                        elif jj == 3:
                            act.wait_ge(s["cl"], NS * i + g + 1)
                            act.activation(pr[:, t % PR, :, :], pr[:, t % PR, :, :], ACT.Exp).then_inc(s["ex"], 1)

                    def copy_values(b, bb, par, first2):
                        act.wait_ge(s["v"], 2 * b + bb + 1)
                        if bb == 0 and not first2:
                            act.wait_ge(s["av"], 8 * (b - 1))
                        src = dense[1 - bb][0:SH, :].rearrange("p (t g h d) -> p (t g) h d", t=2, h=2, d=DH)
                        dst = vp[par][:, bb, :, :, :, :].rearrange("p t g h d -> p (t g) h d")
                        for hh in range(2):
                            act.activation(dst[:, :, hh, hh * DH:(hh + 1) * DH], src[:, :, hh, :], ACT.Copy,
                                           scale=1 / WS if first_layer else 1.0).then_inc(s["vp"], 1)

                    def high_out(i, n):
                        act.wait_ge(s["on"], 4 * i + n + 1)
                        if n == 0 and not (isinstance(i, int) and i == 0):
                            act.wait_ge(s["pj"], 2 * i)
                        bb, c = n // 2, n % 2
                        act.activation(oh[:, c, bb * S:(bb + 1) * S], on[:, c, bb * S:(bb + 1) * S], ACT.Copy).then_inc(s["ohi"], 1)

                    def body(i, par, first, has_a, has_b):
                        a, b, l = i + 2, i + 1, i - 1
                        for g in range(NS):
                            exponentials(i, g)
                            if has_a and g == QK:
                                for k in range(4):
                                    copy_qk(a, k)
                            if not first and g == 5 + LAG:
                                high_out(l, 3)
                            if has_b and g in (9, 11):
                                copy_values(b, (g - 9) // 2, 1 - par, first)
                            if g in (15, 23, 31):
                                high_out(i, (g - 15) // 8)
                            if not first and g == 18:
                                ln.act_square(act, l, isinstance(l, int) and l == 0)
                            if not first and g == 28:
                                ln.act_hi(act, cols(l), l)
                            if has_a and g - HIGH in range(4):
                                high_qk(a, g - HIGH)

                    if not first_layer:
                        for w in range(4):
                            act.wait_ge(s["wt"], w + 1)
                            dst = wqkv[0][:, :, w * D:(w + 1) * D] if w < 3 else wpro[0][:, :, :]
                            act.activation(dst, bank[w][:, :].rearrange("p (c n) -> p c n", c=KD), ACT.Copy).then_inc(s["wcp"], 1)
                    for a in range(2):
                        for k in range(4):
                            copy_qk(a, k)
                        for k in range(4):
                            high_qk(a, k)
                    for bb in range(2):
                        copy_values(0, bb, 0, True)
                    for i in range(2):
                        body(i, i, i == 0, True, True)
                    with act.Fori(1, NT // 2 - 1, 1) as half:
                        for u in range(2):
                            i = half * 2
                            body(i + u, u, False, True, True)
                    for i in range(NT - 2, NT):
                        body(i, i % 2, False, False, i < NT - 1)
                    l = NT - 1
                    high_out(l, 3)
                    ln.act_square(act, l, False)
                    ln.act_hi(act, cols(l), l)

                @block.vector
                def _(v):
                    def q_variance(a):
                        v.wait_ge(s["qvar"], a + 1)
                        if not (isinstance(a, int) and a == 0):
                            v.wait_ge(s["qroot"], ROOT_POOL * a)
                        v.tensor_scalar(qve[:, :], dense[1][:, 0:SH], -0.5, -0.5 * EPS, ALU.mult, ALU.add).then_inc(s["qve"], 1)
                        v.wait_ge(s["qve"], a + 1)
                        if not (isinstance(a, int) and a == 0):
                            v.wait_ge(s["qbc"], 4 * a)
                        root_guess(v, qve[:, :], qrs[:, :], s["qroot"], a)

                    def scale_qk(a, k):
                        v.wait_ge(s["qbc"], 4 * a + k + 1)
                        v.tensor_tensor(qc[:, k, :], qc[:, k, :], dense[(1, 0, 1, 0)[k]][:, 0:T], ALU.mult).then_inc(s["qn"], 1)

                    def reduce_maxima(b, u):
                        bb, qt, hh, p0, n = unit(u)
                        v.wait_ge(s["mm"], UPS * b + u + 1)
                        v.tensor_reduce(mx[:, bb, qt, 8 * hh + p0:8 * hh + p0 + n],
                                        maxb[u % 2][0:SH, 0:n * S].rearrange("p (h k) -> p h k", h=n), AX.X, ALU.max).then_inc(s["mx"], 1)

                    def split_maxima(b, bb):
                        v.wait_ge(s["mx"], UPS * b + 12 * (bb + 1))
                        if not (isinstance(b, int) and b == 0):
                            v.wait_ge(s["mt"], 2 * b + bb - 1)
                        v.tensor_scalar(ml[:, bb, :, 0, :], mx[:, bb, :, :], -1.0, None, ALU.mult).then_inc(s["ml"], 1)
                        v.wait_ge(s["ml"], 4 * b + 2 * bb + 1)
                        v.scalar_tensor_tensor(out=ml[:, bb, :, 1, :], in0=mx[:, bb, :, :], scalar=-1.0, in1=ml[:, bb, :, 0, :],
                                               op0=ALU.mult, op1=ALU.subtract).then_inc(s["ml"], 1)

                    def copy_maxima(b, bb):
                        v.wait_ge(s["mt"], 2 * b + bb + 1)
                        if not (isinstance(b, int) and b == 0):
                            v.wait_ge(s["mrow"], 64 * (2 * b + bb - 1))
                        v.tensor_copy(mt[:, bb, :], dense[1].bitcast(F16)[0:2 * H, 0:S]).then_inc(s["mtc"], 1)

                    def clip(i, g):
                        t, jj = g // 4, g % 4
                        v.wait_ge(s["sc"], NS * i + g + 1)
                        if jj == 0 and not (isinstance(i, int) and 8 * i + t - PR + 1 <= 0):
                            v.wait_ge(s["av"], 8 * i + t - PR + 1)
                        v.tensor_scalar(pr[:, t % PR, jj, :], expb[g % ER][0:SH, 0:T], -10.0, 10.0, ALU.max, ALU.min).then_inc(s["cl"], 1)

                    def normalise(i, n):
                        bb, c = n // 2, n % 2
                        v.wait_ge(s["av"], 8 * i + 2 * n + 2)
                        v.reciprocal(rden[:, c, :], avb[c][:, S:2 * S]).then_inc(s["rd"], 1)
                        v.wait_ge(s["rd"], 4 * i + n + 1)
                        if not (isinstance(i, int) and i == 0):
                            v.wait_ge(s["olo"], 4 * i + n - 3)
                        v.tensor_tensor(on[:, c, bb * S:(bb + 1) * S], avb[c][:, 0:S], rden[:, c, :], ALU.mult).then_inc(s["on"], 1)

                    def update(l, k):
                        v.wait_ge(s["pj"], 2 * l + k + 1)
                        if first_layer:
                            v.scalar_tensor_tensor(out=hT[:, k, cols(l)], in0=dense[1 - k][:, 0:T], scalar=1 / WS, in1=hT[:, k, cols(l)],
                                                   op0=ALU.mult, op1=ALU.add).then_inc(s["h"], 1)
                        else:
                            if not (isinstance(l, int) and l == 0):
                                v.wait_ge(s["h"], 2 * l)
                            v.tensor_scalar(upd[:, k, :], dense[1 - k][:, 0:T], 0.1, bo01[:, k:k + 1], ALU.mult, ALU.add).then_inc(s["up"], 1)
                            v.wait_ge(s["up"], 2 * l + k + 1)
                            v.tensor_tensor(hT[:, k, cols(l)], hT[:, k, cols(l)], upd[:, k, :], ALU.add).then_inc(s["h"], 1)

                    def body(i, par, first, has_a, has_b):
                        a, b, l = i + 2, i + 1, i - 1
                        l0 = isinstance(l, int) and l == 0
                        for g in range(NS):
                            if not first_layer:
                                clip(i, g)
                            if first_layer and has_b and 8 <= g < 8 + UPS:
                                reduce_maxima(b, g - 8)
                            if first_layer and first and g < 6:
                                for u in range(2):
                                    reduce_maxima(i, UPS // 2 + 2 * g + u)
                                if g == 5:
                                    split_maxima(i, 1)
                            if first_layer and g == 6:
                                copy_maxima(i, 1)
                            if not first and g == 4 + LAG:
                                normalise(l, 3)
                            if not first and g in (13, 14):
                                update(l, g - 13)
                            if g in (12 + LAG, 20 + LAG, 28 + LAG):
                                normalise(i, (g - 12 - LAG) // 8)
                            if first_layer and has_b and g == 19:
                                split_maxima(b, 0)
                            if not first and g == 17:
                                ln.dve_center(v, cols(l), l, l0)
                            if not first and g == 20:
                                ln.dve_ve(v, l, l0)
                                ln.dve_guess(v, l, l0)
                            if first_layer and has_a and g == 12:
                                q_variance(a)
                            if first_layer and has_b and g == 21:
                                copy_maxima(b, 0)
                            if not first and g == 27:
                                ln.dve_scale(v, l, l0)
                            if first_layer and has_a and 22 <= g < 26:
                                scale_qk(a, g - 22)
                            if first_layer and has_b and g == 31:
                                split_maxima(b, 1)

                    if not first_layer:
                        for par in range(2):
                            v.memset(qs[par][0][96:P, :, :].bitcast(I32), 0).then_inc(s["zero"], 1)
                        v.tensor_scalar(bo01[:, :], vec1[:, 0, :], 0.1, None, ALU.mult)
                        for w in range(4):
                            v.wait_ge(s["wcp"], w + 1)
                            lo = wqkv[1][:, :, w * D:(w + 1) * D] if w < 3 else wpro[1][:, :, :]
                            hi = wqkv[0][:, :, w * D:(w + 1) * D] if w < 3 else wpro[0][:, :, :]
                            v.tensor_tensor(lo, bank[w][:, :].rearrange("p (c n) -> p c n", c=KD), hi, ALU.subtract).then_inc(s["prep"], 1)
                    if first_layer:
                        for a in range(2):
                            q_variance(a)
                            for k in range(4):
                                scale_qk(a, k)
                    if first_layer:
                        for u in range(UPS // 2):
                            reduce_maxima(0, u)
                        split_maxima(0, 0)
                        copy_maxima(0, 0)
                    for i in range(2):
                        body(i, i, i == 0, True, True)
                    with v.Fori(1, NT // 2 - 1, 1) as half:
                        for u in range(2):
                            i = half * 2
                            body(i + u, u, False, True, True)
                    for i in range(NT - 2, NT):
                        body(i, i % 2, False, False, i < NT - 1)
                    l = NT - 1
                    normalise(l, 3)
                    for k in range(KD):
                        update(l, k)
                    ln.dve_center(v, cols(l), l, False)
                    ln.dve_ve(v, l, False)
                    ln.dve_guess(v, l, False)
                    ln.dve_scale(v, l, False)

                @block.gpsimd
                def _(p):
                    def squares(a, k):
                        p.wait_ge(s["qc"], 4 * a + k + 1)
                        if not (isinstance(a, int) and a == 0):
                            p.wait_ge(s["qvar"], a)
                        p.tensor_tensor(qsq[:, k, :], qc[:, k, :], qc[:, k, :], ALU.mult).then_inc(s["qsq"], 1)

                    def low_qk(a):
                        for k in range(4):
                            p.wait_ge(s["qhi"], 4 * a + k + 1)
                            if not (isinstance(a, int) and a == 0):
                                p.wait_ge(s[("qout", "kout")[k // 2]], 32 * a)
                            p.tensor_tensor(qkl[:, k, :], qc[:, k, :], qkh[:, k, :], ALU.subtract).then_inc(s["qlo"], 1)

                    def low_out(i, n):
                        bb, c = n // 2, n % 2
                        p.wait_ge(s["ohi"], 4 * i + n + 1)
                        p.tensor_tensor(ol[:, c, bb * S:(bb + 1) * S], on[:, c, bb * S:(bb + 1) * S], oh[:, c, bb * S:(bb + 1) * S],
                                        ALU.subtract).then_inc(s["olo"], 1)

                    def q_root(a):
                        root_steps(p, False, qve[:, :], qrs[:, :], qnt[:, :], s["qroot"], a)

                    def body(i, first, has_a):
                        a, l = i + 2, i - 1
                        if first_layer and has_a:
                            for k in range(4):
                                squares(a, k)
                        if not first_layer and has_a:
                            low_qk(a)
                        if not first:
                            low_out(l, 3)
                        if first_layer and has_a:
                            q_root(a)
                        low_out(i, 0)
                        if not first:
                            ln.steps(p, l)
                        low_out(i, 1)
                        if first_layer and has_a:
                            low_qk(a)
                        if not first:
                            ln.pool_lo(p, cols(l), l)
                        low_out(i, 2)

                    for a in range(2):
                        if first_layer:
                            for k in range(4):
                                squares(a, k)
                            q_root(a)
                        low_qk(a)
                    for i in range(2):
                        body(i, i == 0, True)
                    with p.Fori(2, NT - 2, 1) as i:
                        body(i, False, True)
                    for i in range(NT - 2, NT):
                        body(i, False, False)
                    low_out(NT - 1, 3)
                    ln.steps(p, NT - 1)
                    ln.pool_lo(p, cols(NT - 1), NT - 1)

                @block.sync
                def _(sp):
                    nstk = 16 * 2 * 2 * NP
                    values = [sp.alloc_register(f"wait_a{layer}"), sp.alloc_register(f"wait_b{layer}")]

                    def hold(r, x):
                        if isinstance(x, int):
                            return x
                        sp.reg_mov(values[r], x)
                        return values[r]

                    def leave(a, par, first2):
                        for x in range(2):
                            split, free = hold(0, 4 * a + 2 * x + 2), None if first2 else hold(1, nstk * (a - 1))
                            sp.wait_ge(s["qlo"], split)
                            if not first2:
                                sp.wait_ge(s["stk"], free)
                            for part, src in enumerate((qkh, qkl)):
                                sp.dma_start(bounce[par, part, 2 * x:2 * x + 2].rearrange("k p t -> p k t"),
                                             src[:, 2 * x:2 * x + 2, :]).then_inc(s[("qout", "kout")[x]], 16)

                    def stack(b, par, first2):
                        for x in range(2):
                            there, free = hold(0, 32 * (b + 1)), None if first2 else hold(1, NS * (b - 1))
                            sp.wait_ge(s[("qout", "kout")[x]], there)
                            if not first2:
                                sp.wait_ge(s["sc"], free)
                            for part in range(NP):
                                low = ((0, 1, 0, 1), (0, 0, 1, 1))[x][part]
                                for hh in range(2):
                                    src = bounce[par, low, 2 * x:2 * x + 2].rearrange("c (j h d) t -> h d (c j) t", h=2, d=DH)[hh]
                                    dst = ks[par] if x else qs[par][hh]
                                    r = 64 * hh + DH * part
                                    sp.dma_start(dst[r:r + DH, :, :], src).then_inc(s["stk"], 16)

                    def maxima_rows(b, bb, par):
                        copied = hold(0, 2 * b + bb + 1)
                        sp.wait_ge(s["mtc"], copied)
                        for hh in range(2):
                            for part in range(2):
                                r = KR + part
                                sp.dma_start(qs[par][hh][r:r + 1, :, bb * S:(bb + 1) * S],
                                             mt[H * part + 8 * hh:H * part + 8 * hh + 8, bb, :]).then_inc(s["mrow"], 16)

                    def body(i, par, first, has_a, has_b):
                        a, b = i + 2, i + 1
                        if has_b:
                            stack(b, 1 - par, first)
                        if first_layer:
                            maxima_rows(i, 1, par)
                            if has_b:
                                maxima_rows(b, 0, 1 - par)
                        if has_a:
                            leave(a, par, False)

                    if first_layer:
                        for raw, w in ((raw_gate, w_gate), (raw_up, w_up), (raw_down, w_down)):
                            sp.dma_start(raw[:, :, :], w.rearrange("(c p) n -> p c n", p=P)).then_inc(s["w_in"], 16)
                    else:
                        for i, w in enumerate((wq1, wk1, wv1, wo1)):
                            sp.dma_start(raw_att1[:, i, :, :], w.rearrange("(c p) n -> p c n", p=P)).then_inc(s["att_in"], 16)
                        sp.dma_start(raw_w1[:, :, :], w1.rearrange("(c p) n -> p c n", p=P)).then_inc(s["w_in"], 16)
                        sp.dma_start(raw_w2[:, :, :], w2.rearrange("(c p) n -> p c n", p=P)).then_inc(s["w_in"], 16)
                        sp.wait_ge(s["zero"], 2)
                    leave(0, 0, True)
                    stack(0, 0, True)
                    leave(1, 1, True)
                    if first_layer:
                        maxima_rows(0, 0, 0)
                    for i in range(2):
                        body(i, i, i == 0, True, True)
                    with sp.Fori(1, NT // 2 - 1, 1) as half:
                        for u in range(2):
                            i = half * 2
                            body(i + u, u, False, True, True)
                    for i in range(NT - 2, NT):
                        body(i, i % 2, False, False, i < NT - 1)
                    sp.wait_ge(s["qout"], 32 * NT)
                    sp.wait_ge(s["kout"], 32 * NT)
                    sp.wait_ge(s["w_in"], 48 if first_layer else 32)
            ph.close()

        def feed_forward(layer):
            ph = ExitStack()
            gated = layer == 0
            M = K0 if gated else K1
            UR = 2 if gated else 4
            HR = M // 2
            NW = (3 if gated else 2) * KD * M
            assert M % UR == 0 and M % HR == 0
            Q = 1 / 127.0
            wt = sb(f"wt{layer}", [P, NW, P], F16, ph)
            w16 = sb(f"w16{layer}", [P, NW * P], F16, ph)
            hid = sb(f"hid{layer}", [P, 2, T], scope=ph)
            act_g = sb(f"act_g{layer}", [P, 2, T], scope=ph)
            hh = sb(f"hh{layer}", [P, HR, T], F16, ph)
            hl = sb(f"hl{layer}", [P, HR, T], F16, ph)
            if not gated:
                alpha1 = sb("alpha1", [P, K1], scope=ph)
                alpha2 = sb("alpha2", [P, KD], scope=ph)
                upd = sb("upd4", [P, KD, T], scope=ph)
                hf = sb("hf", [P, KD, T], scope=ph)
                ot = sb("ot", [SH, 4, D], scope=ph)
            bank = [ps(f"ff{layer}{i}", [P, 512], scope=ph) for i in range(8)]
            s = semaphores("cast", "turn", "wt", "alpha", "up", "hid", "hh", "hl", "dn", "h", *(("act",) if gated else ("upd", "tr", "ot", "out")))
            ln = Norm(bank[6], True, twice=True) if gated else None
            NB = -(-NW // 8)
            cols = lambda i: bass.ds(i * T, T)
            isz = lambda i: isinstance(i, int) and i == 0

            with nc.Block() as block:
                @block.tensor
                def _(pe):
                    def up(i, m):
                        n0 = M * i + m
                        if not (isinstance(i, int) and n0 < UR):
                            pe.wait_ge(s["hid"], n0 - UR + 1)
                        for g in range(2 if gated else 1):
                            n = 0
                            for x in (xh, xl):
                                for c in range(KD):
                                    mm = pe.matmul(bank[(2 if gated else 1) * (m % UR) + g][:, 0:T], wt[:, (g * KD + c) * M + m, :],
                                                   x[:, c, cols(i)], start=(n == 0), stop=(n == 3))
                                    n += 1
                        mm.then_inc(s["up"], 1)

                    def down(i, m):
                        pe.wait_ge(s["hl"], M * i + m + 1)
                        if m == 0 and not isz(i):
                            pe.wait_ge(s["h" if gated else "upd"], 2 * i)
                        for k in range(KD):
                            for n, x in enumerate((hh, hl)):
                                mm = pe.matmul(bank[4 + k][:, 0:T], wt[:, (2 if gated else 1) * KD * M + m * KD + k, :],
                                               x[:, m % HR, :], start=(m == 0 and n == 0), stop=(m == M - 1 and n == 1))
                        mm.then_inc(s["dn"], 1)

                    def finish(l, m, first):
                        if gated:
                            if m == 2:
                                pe.wait_ge(s["h"], 2 * l + 2)
                                if not first:
                                    pe.wait_ge(ln.done, l)
                                ln.pe_mean(pe, cols(l), l)
                            if m == 3:
                                ln.pe_var(pe, l)
                            if m == 5:
                                ln.pe_bcast(pe, l)
                            if m == M:
                                ln.pe_bcast2(pe, l)
                        elif m == 3:
                            pe.wait_ge(s["h"], 2 * l + 2)
                            if not first:
                                pe.wait_ge(s["ot"], 2 * l)
                            for q in range(4):
                                for k in range(KD):
                                    mm = pe.transpose(bank[6 + q // 2][0:SH, (q % 2) * D + k * P:(q % 2) * D + (k + 1) * P],
                                                      hf[:, k, q * SH:(q + 1) * SH], ident[:, :])
                                if q % 2:
                                    mm.then_inc(s["tr"], 1)

                    def body(i, first, late=True):
                        for m in range(M):
                            up(i, m)
                            if m >= 2:
                                down(i, m - 2)
                            elif not first:
                                down(i - 1, M - 2 + m)
                            if late and m < 2:
                                finish(i - 2, M + m, isz(i - 2))
                            if not first:
                                finish(i - 1, m, isz(i - 1))

                    for b in range(NB):
                        for n in range(8 * b, min(NW, 8 * b + 8)):
                            w, r = divmod(n, KD * M)
                            if w < (2 if gated else 1):
                                c, m = divmod(r, M)
                                src = w16[:, (w * KD * M + m * KD + c) * P:(w * KD * M + m * KD + c + 1) * P]
                            else:
                                m, c = divmod(r, KD)
                                src = w16[:, (w * KD * M + c * M + m) * P:(w * KD * M + c * M + m + 1) * P]
                            pe.wait_ge(s["cast"], w + 1)
                            mm = pe.transpose(bank[b].bitcast(F16)[:, (n - 8 * b) * P:(n - 8 * b + 1) * P], src, ident16[:, :])
                        mm.then_inc(s["turn"], 1)
                    pe.wait_ge(s["wt"], NB)
                    body(0, True, False)
                    body(1, False, False)
                    body(2, False)
                    with pe.Fori(3, NT, 1) as i:
                        body(i, False)
                    for m in range(2):
                        down(NT - 1, M - 2 + m)
                    for m in range(2):
                        finish(NT - 2, M + m, False)
                    for m in range(M + 2):
                        finish(NT - 1, m, False)

                @block.scalar
                def _(a):
                    def nonlinear(i, m):
                        n0 = M * i + m
                        a.wait_ge(s["up"], n0 + 1)
                        if gated:
                            if not (isinstance(i, int) and n0 < 2):
                                a.wait_ge(s["hid"], n0 - 1)
                            a.activation(act_g[:, m % 2, :], bank[2 * (m % UR)][:, 0:T], ACT.Silu, scale=Q).then_inc(s["act"], 1)
                        else:
                            if not (isinstance(i, int) and n0 < 2):
                                a.wait_ge(s["hl"], n0 - 1)
                            a.activation(hid[:, m % 2, :], bank[m % UR][:, 0:T], ACT.Gelu, scale=alpha1[:, m:m + 1],
                                         bias=b1_sb[:, m:m + 1]).then_inc(s["hid"], 1)

                    def finish(l, m):
                        if gated:
                            if m == 3:
                                ln.act_square(a, l, isz(l))
                            if m == M + 1:
                                ln.act_hi(a, cols(l), l)
                        elif m in (4, 5):
                            a.wait_ge(s["tr"], 2 * l + m - 3)
                            if m == 4 and not isz(l):
                                a.wait_ge(s["out"], 16 * l)
                            a.activation(ot[:, 2 * (m - 4):2 * (m - 4) + 2, :],
                                         bank[6 + m - 4][0:SH, :].rearrange("p (q d) -> p q d", q=2), ACT.Copy).then_inc(s["ot"], 1)

                    def body(i, first, late=True):
                        for m in range(M):
                            nonlinear(i, m)
                            if late and m < 2:
                                finish(i - 2, M + m)
                            if not first:
                                finish(i - 1, m)

                    n1 = KD * M * P
                    if gated:
                        a.activation(w16[:, 0:n1], raw_gate[:, :, :].rearrange("p c n -> p (c n)"), ACT.Copy).then_inc(s["cast"], 1)
                    else:
                        a.activation(w16[:, 0:n1], raw_w1[:, :, :].rearrange("p c n -> p (c n)"), ACT.Sign).then_inc(s["cast"], 1)
                        a.activation(w16[:, n1:2 * n1], raw_w2[:, :, :].rearrange("p c n -> p (c n)"), ACT.Sign).then_inc(s["cast"], 1)
                        a.wait_ge(s["alpha"], 4)
                    body(0, True, False)
                    body(1, False, False)
                    body(2, False)
                    with a.Fori(3, NT, 1) as i:
                        body(i, False)
                    for m in range(2):
                        finish(NT - 2, M + m)
                    for m in range(M + 2):
                        finish(NT - 1, m)

                @block.vector
                def _(v):
                    def hidden(i, m):
                        n0 = M * i + m
                        if gated:
                            v.wait_ge(s["act"], n0 + 1)
                            if not (isinstance(i, int) and n0 < 2):
                                v.wait_ge(s["hl"], n0 - 1)
                            v.scalar_tensor_tensor(out=hid[:, m % 2, :], in0=bank[2 * (m % UR) + 1][:, 0:T], scalar=Q,
                                                   in1=act_g[:, m % 2, :], op0=ALU.mult, op1=ALU.mult).then_inc(s["hid"], 1)
                        v.wait_ge(s["hid"], n0 + 1)
                        if not (isinstance(i, int) and n0 < HR):
                            v.wait_ge(s["dn"], n0 - HR + 1)
                        v.tensor_copy(hh[:, m % HR, :], hid[:, m % 2, :]).then_inc(s["hh"], 1)

                    def finish(l, m):
                        if m == 1:
                            v.wait_ge(s["dn"], M * l + M)
                            for k in range(KD):
                                if gated:
                                    v.scalar_tensor_tensor(out=hT[:, k, cols(l)], in0=bank[4 + k][:, 0:T], scalar=Q, in1=hT[:, k, cols(l)],
                                                           op0=ALU.mult, op1=ALU.add).then_inc(s["h"], 1)
                                else:
                                    if k == 0 and not isz(l):
                                        v.wait_ge(s["tr"], 2 * l)
                                    v.tensor_scalar(upd[:, k, :], bank[4 + k][:, 0:T], alpha2[:, k:k + 1], vec1[:, 3, k:k + 1],
                                                    ALU.mult, ALU.add).then_inc(s["upd"], 1)
                            if not gated:
                                v.wait_ge(s["upd"], 2 * l + 2)
                                for k in range(KD):
                                    v.tensor_tensor(hf[:, k, :], hT[:, k, cols(l)], upd[:, k, :], ALU.add).then_inc(s["h"], 1)
                        if gated:
                            if m == 2:
                                ln.dve_center(v, cols(l), l, isz(l))
                            if m == 3:
                                ln.dve_ve(v, l, isz(l))
                                ln.dve_guess(v, l, isz(l))
                                ln.steps(v, l, range(0, 1))
                            if m == 4:
                                ln.steps(v, l, range(1, 3))
                            if m == 5:
                                ln.dve_scale(v, l, isz(l))
                            if m == M:
                                ln.dve_scale2(v, l, isz(l))

                    def body(i, first, late=True):
                        for m in range(M):
                            hidden(i, m)
                            if late and m < 2:
                                finish(i - 2, M + m)
                            if not first:
                                finish(i - 1, m)

                    n1 = KD * M * P
                    if gated:
                        v.tensor_copy(w16[:, n1:2 * n1], raw_up[:, :, :].rearrange("p c n -> p (c n)")).then_inc(s["alpha"], 1)
                        v.wait_ge(s["cast"], 1)
                        v.tensor_copy(w16[:, 2 * n1:3 * n1], raw_down[:, :, :].rearrange("p c n -> p (c n)")).then_inc(s["cast"], 2)
                    else:
                        v.tensor_reduce(alpha1[:, :], raw_w1[:, :, :], AX.X, ALU.add, apply_absolute_value=True).then_inc(s["alpha"], 1)
                        v.tensor_reduce(alpha2[:, :], raw_w2[:, :, :], AX.X, ALU.add, apply_absolute_value=True).then_inc(s["alpha"], 1)
                        v.wait_ge(s["alpha"], 2)
                        v.tensor_scalar(alpha1[:, :], alpha1[:, :], 1.0 / D, None, ALU.mult).then_inc(s["alpha"], 1)
                        v.tensor_scalar(alpha2[:, :], alpha2[:, :], 1.0 / F1, None, ALU.mult).then_inc(s["alpha"], 1)
                    for b in range(NB):
                        v.wait_ge(s["turn"], b + 1)
                        n = min(NW, 8 * b + 8) - 8 * b
                        v.tensor_copy(wt[:, 8 * b:8 * b + n, :], bank[b].bitcast(F16)[:, 0:n * P].rearrange("p (n q) -> p n q", q=P)).then_inc(s["wt"], 1)
                    if not gated:
                        v.wait_ge(s["alpha"], 4)
                    body(0, True, False)
                    body(1, False, False)
                    body(2, False)
                    with v.Fori(3, NT, 1) as i:
                        body(i, False)
                    for m in range(2):
                        finish(NT - 2, M + m)
                    for m in range(M + 2):
                        finish(NT - 1, m)

                @block.gpsimd
                def _(p):
                    def low(i, m):
                        n0 = M * i + m
                        p.wait_ge(s["hh"], n0 + 1)
                        p.tensor_tensor(hl[:, m % HR, :], hid[:, m % 2, :], hh[:, m % HR, :], ALU.subtract).then_inc(s["hl"], 1)

                    def finish(l, m):
                        if gated and m == 5:
                            ln.pool_residual(p, cols(l), l)
                        if gated and m == M + 1:
                            ln.pool_lo(p, cols(l), l)

                    def body(i, first, late=True):
                        for m in range(M):
                            low(i, m)
                            if late and m < 2:
                                finish(i - 2, M + m)
                            if not first:
                                finish(i - 1, m)

                    body(0, True, False)
                    body(1, False, False)
                    body(2, False)
                    with p.Fori(3, NT, 1) as i:
                        body(i, False)
                    for m in range(2):
                        finish(NT - 2, M + m)
                    for m in range(M + 2):
                        finish(NT - 1, m)

                @block.sync
                def _(sp):
                    if not gated:
                        rows = out.rearrange("b s d -> (b s) d")
                        with sp.Fori(0, NT, 1) as i:
                            row, filled = sp.snap(i * T), sp.snap(2 * i + 2)
                            sp.wait_ge(s["ot"], filled)
                            sp.dma_start(rows[bass.ds(row, T), :].rearrange("(q p) d -> p q d", p=SH), ot[:, :, :]).then_inc(s["out"], 16)
                        sp.wait_ge(s["out"], 16 * NT)
            ph.close()

        ph = ctx.enter_context(ExitStack())
        xs = sb("xs", [BH, C, PT, GW, PT], scope=ph)
        xn0 = sb("xn0", [BH, GW, C, PT, PT], scope=ph)
        stats = sb("stats", [BH, GW, C, 6], scope=ph)
        mv = sb("mv", [BH, GW, 2], scope=ph)
        rs0 = sb("rs0", [BH, GW], scope=ph)
        sd0 = sb("sd0", [BH, GW], scope=ph)
        xpT = sb("xpT", [P, KP, GW, BH], scope=ph)
        in_xh = xh[:, :, :].rearrange("p c n -> p (c n)").bitcast(F32)
        in_xl = xl[:, :, :].rearrange("p c n -> p (c n)").bitcast(F32)
        wm = in_xh[:, 0:KP * D].rearrange("p (a c n) -> p a c n", a=KP // C, c=C)
        trs = in_xh[:, KP * D:KP * D + NTI].rearrange("p (g n) -> p g n", g=2)
        tsd = [in_xh[:, KP * D + NTI:KP * D + NTI + NTI // 2], in_xl[:, 2 * KD * NTI:2 * KD * NTI + NTI // 2]]
        tk = in_xl[:, 0:KD * NTI].rearrange("p (c w n) -> p c w n", c=KD, w=GW)
        tsq = in_xl[:, KD * NTI:2 * KD * NTI].rearrange("p (g c n) -> p g c n", g=2, c=KD)
        gain = sb("gain", [P, 2, DH], scope=ph)
        wmean = sb("wmean", [P, KD, 2 * H], scope=ph)
        tx = sb("tx", [ST, B, D], scope=ph)
        g1 = sb("g1", [P, KP // C, C], scope=ph)
        be1 = sb("be1", [P, KP // C, C], scope=ph)
        vec0 = sb("vec0", [P, 3, KD], scope=ph)
        pb = [ps(f"pb{i}", [P, 512], scope=ph) for i in range(8)]
        s = semaphores("roots", "x0", "x1", "x2", "gain", "wq_in", "wm", "wc", "wcp", "wlo", "zero_q", "zero", "tok_in", "txt_in", "w_in", "bcast", "cst", "stats", "mv", "sd", "rstd", "xn",
                       "tr", "xp", "mlp", "tk", "mean", "txc", "tsq", "var", "tsd", "trs", "tnx", "taff", "h_img", "ttr", "h_txt")
        half = NTI // 2
        big = KD * T
        work = [lnw]
        for q in range(1, 4):
            flat = sb(f"ln_more{q}", [P, 3 * big], scope=ph)[:, :] if q == 3 else tx[:, :, :].rearrange("p b d -> p (b d)")[:, 3 * big * (q - 1):3 * big * q]
            work.append({k: flat[:, n * big:(n + 1) * big].rearrange("p (c t) -> p c t", c=KD) for n, k in enumerate(("xc", "sq", "xn"))}
)
        spread4 = [sb(f"ln4_{k}", [P, 4, SH], scope=ph) for k in ("ve", "rstd", "t")]
        work = [w | {k: x[:, q, :] for k, x in zip(("ve", "rstd", "t"), spread4)} for q, w in enumerate(work)]
        lns = [Norm(pb[4 + q], True, work=work[q]) for q in range(4)]
        for n4 in lns:
            n4.s["ln_root"] = s["roots"]
        tile_cols = lambda g, q: bass.ds((4 * g + q) * T, T)
        assert NT % 4 == 0 and ST == P
        with nc.allow_non_contiguous_dma(reason="small vectors"), nc.Block() as block:
            @block.sync
            def _(sp):
                for c in range(C):
                    sp.dma_start(xs[:, c, :, :, :].rearrange("n p w q -> n (p w q)"),
                                 x[:, c].rearrange("b (h p) w -> b h (p w)", p=PT)).then_inc(s[f"x{c}"], 16)
                for i, v in enumerate((q_gamma, k_gamma)):
                    sp.dma_start(gain[:, i, :], v.rearrange("(a d) -> a d", a=1).to_broadcast([P, DH])).then_inc(s["gain"], 16)
                sp.dma_start(raw_qkv[:, :, :], w_qkv.rearrange("(c p) n -> p c n", p=P)).then_inc(s["wq_in"], 16)
                sp.dma_start(raw_proj[:, :, :], w_proj.rearrange("(c p) n -> p c n", p=P)).then_inc(s["wq_in"], 16)
                sp.dma_start(wm[:, :, :, :], tok_w.rearrange("(a p c) n -> p a c n", a=KP // C, c=C)).then_inc(s["tok_in"], 16)
                sp.dma_start(g1[:, :, :], tok_g1.rearrange("(a p c) -> p a c", a=KP // C, c=C)).then_inc(s["tok_in"], 16)
                sp.dma_start(be1[:, :, :], tok_b1.rearrange("(a p c) -> p a c", a=KP // C, c=C)).then_inc(s["tok_in"], 16)
                for i, v in enumerate((tok_bias, tok_g2, tok_b2)):
                    sp.dma_start(vec0[:, i, :], v.rearrange("(c p) -> p c", p=P)).then_inc(s["tok_in"], 16)
                for q in range(4):
                    b0, b9 = q * B // 4, (q + 1) * B // 4
                    sp.dma_start(tx[:, b0:b9, :], txt[b0:b9].rearrange("b t d -> t b d")).then_inc(s["txt_in"], 16)
                for i, v in enumerate((bo1, ln_gamma, ln_beta, b2)):
                    sp.dma_start(vec1[:, i, :], v.rearrange("(c p) -> p c", p=P)).then_inc(s["w_in"], 16)
                sp.dma_start(b1_sb[:, :], b1.rearrange("(c p) -> p c", p=P)).then_inc(s["w_in"], 16)
                for i, v in enumerate((q_beta, k_beta)):
                    for h in range(HC):
                        sp.dma_start(beta[h * DH:(h + 1) * DH, i:i + 1], v.rearrange("(p a) -> p a", a=1)).then_inc(s["w_in"], 16)
                sp.wait_ge(s["w_in"], 16 * (5 + 2 * HC))

            @block.gpsimd
            def _(p):
                p.memset(ident[:, :], 0.0).then_inc(s["cst"], 1)
                p.wait_ge(s["cst"], 1)
                p.affine_select(out=ident[:, :], in_=ident[:, :], compare_op=ALU.not_equal, fill=1.0, base=0,
                                pattern=[[-1, P]], channel_multiplier=1).then_inc(s["cst"], 1)
                p.wait_ge(s["cst"], 2)
                p.tensor_copy(ident16[:, :], ident[:, :]).then_inc(s["cst"], 1)
                p.memset(ones_d[:, :], 1.0 / D).then_inc(s["cst"], 1)
                p.memset(three_halves[:, :], 1.5).then_inc(s["cst"], 1)
                p.memset(eps_tok[:, :], EPS_TOK).then_inc(s["cst"], 1)
                p.memset(head_back[:, :, :, :], 1.0).then_inc(s["cst"], 1)
                p.memset(head_mean[:, :, :], 1.0 / DH).then_inc(s["cst"], 1)
                p.wait_ge(s["cst"], 8)
                p.affine_select(out=head_back[:, :, :, :], in_=head_back[:, :, :, :], compare_op=ALU.is_ge, fill=0.0,
                                base=0, pattern=[[32 * DH, 4], [HC * DH, 4], [1, P]], channel_multiplier=-DH).then_inc(s["cst"], 1)
                p.affine_select(out=head_mean[:, :, :], in_=head_mean[:, :, :], compare_op=ALU.is_ge, fill=0.0,
                                base=0, pattern=[[HC * DH, 4], [-DH, 32]], channel_multiplier=1).then_inc(s["cst"], 1)
                p.wait_ge(s["cst"], 10)
                p.affine_select(out=head_back[:, :, :, :], in_=head_back[:, :, :, :], compare_op=ALU.is_ge, fill=0.0,
                                base=DH - 1, pattern=[[-32 * DH, 4], [-HC * DH, 4], [-1, P]], channel_multiplier=DH).then_inc(s["cst"], 1)
                p.affine_select(out=head_mean[:, :, :], in_=head_mean[:, :, :], compare_op=ALU.is_ge, fill=0.0,
                                base=DH - 1, pattern=[[-HC * DH, 4], [DH, 32]], channel_multiplier=-1).then_inc(s["cst"], 1)

                p.wait_ge(s["cst"], 12)
                p.wait_ge(s["gain"], 32)
                for k in range(4):
                    hb = head_back[:, :, k, :].rearrange("p j (h d) -> p j h d", d=DH)
                    p.tensor_tensor(hb, hb, gain[:, k // 2, :].unsqueeze(1).unsqueeze(1).to_broadcast([P, 4, HC, DH]), ALU.mult).then_inc(s["cst"], 1)
                n = 0
                for par in range(2):
                    for hh, r0, r9 in ((0, 32, 64), (0, 64, P), (1, 0, 64), (1, 96, P)):
                        p.wait_ge(*((s["zero_q"], n) if n else (s["cst"], 16)))
                        p.memset(qs[par][hh][r0:r9, :, :].bitcast(I32), 0).then_inc(s["zero_q"], 1)
                        n += 1

                p.wait_ge(s["zero_q"], 8)

                def group(g):
                    for q in range(4):
                        lns[q].pool_lo(p, tile_cols(g, q), g)
                group(0)
                with p.Fori(1, NT // 4, 1) as g:
                    group(g)

            @block.vector
            def _(v):
                v.memset(bcast[:, :, :], 0.0).then_inc(s["bcast"], 1)
                v.wait_ge(s["bcast"], 1)
                for k in range(4):
                    v.memset(bcast[32 * k:32 * k + 32, k, :], 1.0 / 32).then_inc(s["bcast"], 1)
                v.memset(vp[0][:, :, :, :, :, :], 0.0).then_inc(s["zero"], 1)
                v.memset(onesv[:, :, :], 0.0).then_inc(s["bcast"], 1)
                v.wait_ge(s["bcast"], 6)
                for hh in range(2):
                    v.memset(onesv[:, hh, hh * DH:(hh + 1) * DH], 1.0).then_inc(s["bcast"], 1)
                for c in range(C):
                    v.wait_ge(s[f"x{c}"], 16)
                    for w in range(GW):
                        m = v.bn_stats(stats[:, w, c, :], xs[:, c, :, w, :])
                        if c == C - 1:
                            m.then_inc(s["stats"], 1)
                for w in range(GW):
                    v.wait_ge(s["stats"], w + 1)
                    v.bn_aggr(mv[:, w, :], stats[:, w, :, :]).then_inc(s["mv"], 1)
                v.wait_ge(s["sd"], 1)
                v.reciprocal(rs0[:, :], sd0[:, :]).then_inc(s["rstd"], 1)
                v.wait_ge(s["rstd"], 1)
                for w in range(GW):
                    for c in range(C):
                        m = v.tensor_scalar(xn0[:, w, c, :, :], xs[:, c, :, w, :], mv[:, w, 0:1], rs0[:, w:w + 1],
                                            ALU.subtract, ALU.mult)
                    m.then_inc(s["xn"], 1)
                v.wait_ge(s["tok_in"], 16 * 6)
                for k in range(KP):
                    for g in range(2):
                        v.wait_ge(s["tr"], 2 * k + g + 1)
                        c, a = k % C, k // C
                        v.tensor_scalar(xpT[:, k, g * 3:g * 3 + 3, :], pb[(2 * k + g) % 4][:, 0:3 * BH].rearrange("p (w n) -> p w n", w=3),
                                        g1[:, a, c:c + 1], be1[:, a, c:c + 1], ALU.mult, ALU.add).then_inc(s["xp"], 1)
                v.wait_ge(s["wq_in"], 32)
                w3 = raw_qkv[:, :, 0:2 * D].rearrange("p c (h d) -> p c h d", d=DH)
                for c in range(KD):
                    m = v.tensor_reduce(wmean[:, c, :], w3[:, c], AX.X, ALU.add)
                m.then_inc(s["wm"], 1)
                v.wait_ge(s["wm"], 1)
                v.tensor_scalar(wmean[:, :, :], wmean[:, :, :], 1 / DH, None, ALU.mult).then_inc(s["wm"], 1)
                v.wait_ge(s["wm"], 2)
                for c in range(KD):
                    m = v.tensor_tensor(w3[:, c], w3[:, c], wmean[:, c, :].unsqueeze(2).to_broadcast([P, 2 * H, DH]), ALU.subtract)
                m.then_inc(s["wc"], 1)
                tg = [tk[:, :, g * 3:g * 3 + 3, :].rearrange("p c w n -> p c (w n)") for g in range(2)]
                for g in range(2):
                    for c in range(KD):
                        v.wait_ge(s["mlp"], 2 * g + c + 1)
                        v.tensor_scalar(tg[g][:, c, :], pb[4 * g + c][:, 0:half], vec0[:, 0, c:c + 1], None, ALU.add).then_inc(s["tk"], 1)
                for g in range(2):
                    v.wait_ge(s["mean"], g + 1)
                    v.wait_ge(s["tk"], 2 * g + 2)
                    for c in range(KD):
                        m = v.tensor_tensor(tg[g][:, c, :], tg[g][:, c, :], pb[4 * g + 2][:, 0:half], ALU.subtract)
                    m.then_inc(s["txc"], 1)
                v.wait_ge(s["wcp"], 3)
                for c in range(KD):
                    for lo, hi, src in ((wqkv[1], wqkv[0], raw_qkv), (wpro[1], wpro[0], raw_proj)):
                        v.scalar_tensor_tensor(out=lo[:, c, :], in0=src[:, c, :], scalar=WS, in1=hi[:, c, :],
                                               op0=ALU.mult, op1=ALU.subtract).then_inc(s["wlo"], 1)
                for g in range(2):
                    v.wait_ge(s["tsd"], g + 1)
                    v.reciprocal(trs[:, g, :], tsd[g]).then_inc(s["trs"], 1)
                for g in range(2):
                    v.wait_ge(s["trs"], g + 1)
                    for c in range(KD):
                        m = v.tensor_tensor(tg[g][:, c, :], tg[g][:, c, :], trs[:, g, :], ALU.mult)
                    m.then_inc(s["tnx"], 1)
                for g in range(2):
                    v.wait_ge(s["tnx"], g + 1)
                    for c in range(KD):
                        for w in range(g * 3, g * 3 + 3):
                            dst = hT[:, c, :].rearrange("p (b s) -> p b s", b=B)[:, :, w:NI:GW]
                            m = v.tensor_scalar(dst, tk[:, c, w, :].rearrange("p (b h) -> p b h", b=B),
                                                vec0[:, 1, c:c + 1], vec0[:, 2, c:c + 1], ALU.mult, ALU.add)
                    m.then_inc(s["h_img"], 1)
                v.wait_ge(s["h_img"], 2)
                v.wait_ge(s["h_txt"], B)

                def group(g, first):
                    for q in range(4):
                        lns[q].dve_center(v, tile_cols(g, q), g, first)
                    for q in range(4):
                        lns[q].dve_ve(v, g, first)
                    for q in range(4):
                        v.wait_ge(lns[q].s["ln_ve"], g + 1)
                        if not first:
                            v.wait_ge(lns[q].s["ln_bc"], g)
                    ve, rstd, tmp = (x[:, :, :] for x in spread4)
                    root_guess(v, ve, rstd, s["roots"], g)
                    root_steps(v, True, ve, rstd, tmp, s["roots"], g)
                    for q in range(4):
                        lns[q].dve_scale(v, g, first)
                group(0, True)
                with v.Fori(1, NT // 4, 1) as g:
                    group(g, False)
                v.memset(vp[1][:, :, :, :, :, :], 0.0).then_inc(s["zero"], 1)
                for par in range(2):
                    v.memset(ks[par][96:P, :, :], 1.0).then_inc(s["zero"], 1)
                    v.memset(ks[par][32:64, :, :].bitcast(I32), 0).then_inc(s["zero"], 1)

            @block.scalar
            def _(a):
                a.wait_ge(s["cst"], 6)
                a.wait_ge(s["mv"], GW)
                a.activation(sd0[:, :], mv[:, :, 1], ACT.Sqrt, bias=eps_tok[0:BH, 0:1]).then_inc(s["sd"], 1)
                a.wait_ge(s["wq_in"], 32)
                a.activation(wqkv[0][:, :, 2 * D:], raw_qkv[:, :, 2 * D:], ACT.Copy, scale=WS).then_inc(s["wcp"], 1)
                a.activation(wpro[0][:, :, :], raw_proj[:, :, :], ACT.Copy, scale=WS).then_inc(s["wcp"], 1)
                for b in range(B):
                    a.wait_ge(s["ttr"], b + 1)
                    a.activation(hT[:, :, b * S + NI:(b + 1) * S],
                                 pb[6 + b % 2][:, 0:KD * ST].rearrange("p (c t) -> p c t", c=KD), ACT.Copy).then_inc(s["h_txt"], 1)
                a.wait_ge(s["wc"], 1)
                a.activation(wqkv[0][:, :, 0:2 * D], raw_qkv[:, :, 0:2 * D], ACT.Copy, scale=WS).then_inc(s["wcp"], 1)
                for g in range(2):
                    a.wait_ge(s["txc"], g + 1)
                    a.activation(tsq[:, g, :, :], tk[:, :, g * 3:g * 3 + 3, :].rearrange("p c w n -> p c (w n)"), ACT.Square).then_inc(s["tsq"], 1)
                for g in range(2):
                    a.wait_ge(s["var"], g + 1)
                    a.activation(tsd[g], pb[4 * g + 2][:, 0:half], ACT.Sqrt, bias=eps_tok[:, 0:1]).then_inc(s["tsd"], 1)

                def group(g, first):
                    for q in range(4):
                        lns[q].act_square(a, g, first)
                    for q in range(4):
                        lns[q].act_hi(a, tile_cols(g, q), g)
                group(0, True)
                with a.Fori(1, NT // 4, 1) as g:
                    group(g, False)

            @block.tensor
            def _(pe):
                pe.wait_ge(s["cst"], 6)
                def text(b):
                    if b >= 2:
                        pe.wait_ge(s["h_txt"], b - 1)
                    for c in range(KD):
                        m = pe.transpose(pb[6 + b % 2][:, c * ST:(c + 1) * ST], tx[:, b, c * P:(c + 1) * P], ident[0:ST, 0:ST])
                    m.then_inc(s["ttr"], 1)
                pe.wait_ge(s["txt_in"], 16 * 4)
                for b in range(B // 2):
                    text(b)
                for k in range(KP):
                    c, a = k % C, k // C
                    for g in range(2):
                        j = 2 * k + g
                        pe.wait_ge(s["xn"], g * 3 + 3)
                        if j >= 4:
                            pe.wait_ge(s["xp"], j - 3)
                        for w in range(3):
                            m = pe.transpose(pb[j % 4][:, w * BH:(w + 1) * BH],
                                             xn0[:, g * 3 + w, c, a * 8:(a + 1) * 8, :].rearrange("n p q -> n (p q)"), ident[0:BH, 0:BH])
                        m.then_inc(s["tr"], 1)
                for b in range(B // 2, B):
                    text(b)
                pe.wait_ge(s["xp"], 2 * KP)
                for g in range(2):
                    for n in range(KD):
                        for k in range(KP):
                            c, a = k % C, k // C
                            m = pe.matmul(pb[4 * g + n][:, 0:half], wm[:, a, c, n * P:(n + 1) * P],
                                          xpT[:, k, g * 3:g * 3 + 3, :].rearrange("p w n -> p (w n)"), start=(k == 0), stop=(k == KP - 1))
                        m.then_inc(s["mlp"], 1)
                pe.wait_ge(s["h_txt"], B)
                for g in range(2):
                    pe.wait_ge(s["tk"], 2 * g + 2)
                    for c in range(KD):
                        m = pe.matmul(pb[4 * g + 2][:, 0:half], ones_d[:, :], tk[:, c, g * 3:g * 3 + 3, :].rearrange("p w n -> p (w n)"),
                                      start=(c == 0), stop=(c == KD - 1))
                    m.then_inc(s["mean"], 1)
                for g in range(2):
                    pe.wait_ge(s["tsq"], g + 1)
                    for c in range(KD):
                        m = pe.matmul(pb[4 * g + 2][:, 0:half], ones_d[:, :], tsq[:, g, c, :], start=(c == 0), stop=(c == KD - 1))
                    m.then_inc(s["var"], 1)
                pe.wait_ge(s["h_img"], 2)

                def group(g, first):
                    for q in range(4):
                        if not first:
                            pe.wait_ge(lns[q].done, g)
                        lns[q].pe_mean(pe, tile_cols(g, q), g)
                    for q in range(4):
                        lns[q].pe_var(pe, g)
                    if first:
                        pe.wait_ge(s["bcast"], 5)
                    for q in range(4):
                        lns[q].pe_bcast(pe, g)
                group(0, True)
                with pe.Fori(1, NT // 4, 1) as g:
                    group(g, False)
        ph.close()
        end_phase()
        raw_gate = sb("raw_gate", [P, K0, D], I32, scope=weights0)
        raw_up = sb("raw_up", [P, K0, D], I32, scope=weights0)
        raw_down = sb("raw_down", [P, KD, F0], I32, scope=weights0)
        attention(0)
        end_phase()
        feed_forward(0)
        end_phase()
        weights0.close()
        raw_att1 = sb("raw_att1", [P, 4, KD, D])
        raw_w1 = sb("raw_w1", [P, K1, D])
        raw_w2 = sb("raw_w2", [P, KD, F1])
        attention(1)
        end_phase()
        feed_forward(1)


_INS = ['x', 'txt', 'L0_tok_g1', 'L0_tok_b1', 'L0_tok_W_mlp', 'L0_tok_b_mlp', 'L0_tok_g2', 'L0_tok_b2',
        'L0_attn_w_qkv', 'L0_attn_w_proj', 'L0_attn_q_gamma', 'L0_attn_q_beta', 'L0_attn_k_gamma', 'L0_attn_k_beta',
        'L0_ffn_w_gate', 'L0_ffn_w_up', 'L0_ffn_w_down', 'L1_attn_Wq', 'L1_attn_Wk', 'L1_attn_Wv', 'L1_attn_Wo',
        'L1_attn_bo', 'L1_attn_ln_gamma', 'L1_attn_ln_beta', 'L1_ffn_w1', 'L1_ffn_b1', 'L1_ffn_w2', 'L1_ffn_b2']


def kernel(**inputs):
    import numpy as _np
    import concourse.bacc as _bacc
    from concourse import mybir as _mybir
    from concourse.bass_utils import run_bass_kernel_spmd as _run

    nc = _bacc.Bacc("TRN2", target_bir_lowering=False, num_devices=1)
    arrays, args = {}, []
    for name in _INS:
        a = _np.ascontiguousarray(inputs[name])
        arrays[f"in_{name}"] = a
        args.append(nc.dram_tensor(f"in_{name}", a.shape, _mybir.dt.from_np(a.dtype), kind="ExternalInput").ap())
    shape = (inputs['x'].shape[0], (inputs['x'].shape[2] // 16) * (inputs['x'].shape[3] // 16) + inputs['txt'].shape[1],
             inputs['txt'].shape[2])
    args.append(nc.dram_tensor("out0", shape, _mybir.dt.float32, kind="ExternalOutput").ap())
    fused_block(nc, *args)
    r = _run(nc, [arrays], core_ids=[0])
    return r.results[0]["out0"]
```

```python
from contextlib import ExitStack

import concourse.bass as bass
from concourse import mybir

ALU = mybir.AluOpType
ACT = mybir.ActivationFunctionType
F32 = mybir.dt.float32
F16 = mybir.dt.float16
I32 = mybir.dt.int32
AX = mybir.AxisListType

P = 128
EPS = 1e-5
EPS_TOK = -1e-5
WS = 64.0


def fused_block(nc, x, txt, tok_g1, tok_b1, tok_w, tok_bias, tok_g2, tok_b2, w_qkv, w_proj, q_gamma, q_beta,
                k_gamma, k_beta, w_gate, w_up, w_down, wq1, wk1, wv1, wo1, bo1, ln_gamma, ln_beta,
                w1, b1, w2, b2, out):
    B, C, HI, WI = x.shape
    _, ST, D = txt.shape
    KD = D // P
    PT = 16
    GH, GW = HI // PT, WI // PT
    NI = GH * GW
    S = NI + ST
    N = B * S
    T = 2 * S
    NT = N // T
    SH = S // 2
    DH = q_gamma.shape[0]
    H = D // DH
    HC = P // DH
    PD = PT * PT * C
    KP = PD // P
    NTI = B * NI
    BH = B * GH
    F0 = w_gate.shape[0]
    K0 = F0 // P
    F1 = w1.shape[0]
    K1 = F1 // P
    assert D == 256 and KD == 2 and DH == 16 and SH <= P and T <= 512 and N % T == 0 and NT % 2 == 0

    with ExitStack() as ctx:
        def sb(name, shape, dt=F32, scope=ctx):
            return scope.enter_context(nc.sbuf_tensor(name, shape, dt))

        def ps(name, shape, dt=F32, scope=ctx):
            return scope.enter_context(nc.psum_tensor(name, shape, dt))

        hT = sb("hT", [P, KD, N])
        xh = sb("xh", [P, KD, N], F16)
        xl = sb("xl", [P, KD, N], F16)
        ident = sb("ident", [P, P])
        ident16 = sb("ident16", [P, P], F16)
        ones_d = sb("ones_d", [P, P])
        eps_tok = sb("eps_tok", [P, 1])
        three_halves = sb("three_halves", [P, SH])
        vec1 = sb("vec1", [P, 4, KD])
        b1_sb = sb("b1_sb", [P, K1])
        spread_in = sb("spread_in", [P, 4, SH])
        bcast = sb("bcast", [P, P])
        head_mean = sb("head_mean", [P, 4, 32])
        head_back = sb("head_back", [P, 4, P])
        beta = sb("beta", [P, 2])
        lnw = {k: sb("ln_" + k, [P, KD, T]) for k in ("xc", "sq", "xn", "z")}
        lnw |= {k: sb("ln_" + k, [P, 2 * SH]) for k in ("ve", "rstd", "t")}
        lnw["wide"] = sb("ln_wide", [P, 2, 4, SH])

        wqkv = [sb(f"wqkv{i}", [P, KD, 3 * D], F16) for i in range(2)]
        wpro = [sb(f"wpro{i}", [P, KD, D], F16) for i in range(2)]
        qs = [[sb(f"qs{i}{h}", [P, H // 2, T], F16) for h in range(2)] for i in range(2)]
        ks = [sb(f"ks{i}", [P, H // 2, T], F16) for i in range(2)]
        vp = [sb(f"vp{i}", [SH, 2, 2, H // 2, 2, 32]) for i in range(2)]
        onesv = sb("onesv", [SH, 2, 32])
        raw_att1 = sb("raw_att", [P, 4, KD, D])
        raw_att0 = raw_att1[:, :, :, :].rearrange("p w c n -> p (w c n)")
        raw_qkv = raw_att0[:, 0:KD * 3 * D].rearrange("p (c n) -> p c n", c=KD)
        raw_proj = raw_att0[:, KD * 3 * D:].rearrange("p (c n) -> p c n", c=KD)
        names = iter(range(10000))
        live = []

        def semaphores(*keys):
            n = next(names)
            new = {k: nc.alloc_semaphore(name=f"p{n}_{k}") for k in keys}
            live.extend(new.values())
            return new

        def end_phase():
            nc.clear_and_free_semaphores(live)
            live.clear()
            nc.all_engine_barrier()

        ROOT_POOL, ROOT_DVE = 14, 11

        def root_guess(v, x, r, steps, n):
            v.tensor_scalar(r.bitcast(I32), x.bitcast(I32), -0.5, float(0x5F3759DF - 2 ** 22 - 2 ** 30), ALU.mult, ALU.add).then_inc(steps, 1)

        def root_steps(e, fused, x, r, t, steps, base, part=range(3)):
            for k in part:
                done = base + 1 + (3 if fused else 4) * k
                e.wait_ge(steps, done)
                e.tensor_tensor(t, r, r, ALU.mult).then_inc(steps, 1)
                e.wait_ge(steps, done + 1)
                e.tensor_tensor(t, t, x, ALU.mult).then_inc(steps, 1)
                e.wait_ge(steps, done + 2)
                if fused:
                    e.scalar_tensor_tensor(out=r, in0=t, scalar=1.5, in1=r, op0=ALU.add, op1=ALU.mult).then_inc(steps, 1)
                else:
                    e.tensor_tensor(t, t, three_halves[:, :], ALU.add).then_inc(steps, 1)
                    e.wait_ge(steps, done + 3)
                    e.tensor_tensor(r, r, t, ALU.mult).then_inc(steps, 1)

        def widen(e, wide, r):
            return e.tensor_tensor(wide, spread_in[:, :, :], r.unsqueeze(1).to_broadcast([P, 4, SH]), ALU.mult)

        class Norm:
            def __init__(self, bank, fused, twice=False, work=None, late=False, s=None):
                self.late = late
                self.fused = fused
                self.NR = (ROOT_DVE if fused else ROOT_POOL) + (1 if twice else 0)
                self.w = work or lnw
                more = ("ln_z", "ln_bc2", "ln_x2", "ln_res") if twice else ()
                self.s = s or semaphores("ln_mean", "ln_xc", "ln_sq", "ln_var", "ln_ve", "ln_root", "ln_bc", "ln_xn", "ln_hi", "ln_lo", *more)
                self.bank = bank
                self.twice = twice
                self.done = self.s["ln_x2" if twice else "ln_xn"]
                self.last_bc = self.s["ln_bc2" if twice else "ln_bc"]

            def pe_mean(self, pe, cols, n):
                for c in range(KD):
                    m = pe.matmul(self.bank[:, 0:T], ones_d[:, :], hT[:, c, cols], start=(c == 0), stop=(c == KD - 1))
                m.then_inc(self.s["ln_mean"], 1)

            def dve_center(self, v, cols, n, first):
                v.wait_ge(self.s["ln_mean"], n + 1)
                if not first:
                    v.wait_ge(self.s["ln_sq"], n)
                    v.wait_ge(self.done, n)
                if not first and self.late:
                    v.wait_ge(self.s["ln_hi"], n)
                    v.wait_ge(self.s["ln_lo"], n)
                for c in range(KD):
                    m = v.tensor_tensor(self.w["xc"][:, c, :], hT[:, c, cols], self.bank[:, 0:T], ALU.subtract)
                m.then_inc(self.s["ln_xc"], 1)

            def act_square(self, a, n, first):
                a.wait_ge(self.s["ln_xc"], n + 1)
                if not first:
                    a.wait_ge(self.s["ln_var"], n)
                a.activation(self.w["sq"][:, :, :], self.w["xc"][:, :, :], ACT.Square).then_inc(self.s["ln_sq"], 1)

            def pe_var(self, pe, n):
                pe.wait_ge(self.s["ln_sq"], n + 1)
                pe.wait_ge(self.s["ln_xc"], n + 1)
                for c in range(KD):
                    for k in range(4):
                        m = pe.matmul(self.bank[32 * k:32 * k + 32, 0:SH], ones_d[:, 0:32], self.w["sq"][:, c, k * SH:(k + 1) * SH],
                                      start=(c == 0), stop=(c == KD - 1))
                m.then_inc(self.s["ln_var"], 1)

            def dve_ve(self, v, n, first):
                v.wait_ge(self.s["ln_var"], n + 1)
                if not first:
                    v.wait_ge(self.s["ln_root"], self.NR * n)
                m = v.tensor_scalar(self.w["ve"][:, 0:SH], self.bank[:, 0:SH], -0.5, -0.5 * EPS, ALU.mult, ALU.add)
                if self.twice:
                    m = v.tensor_scalar(self.w["ve"][:, SH:2 * SH], self.bank[:, 0:SH], -0.5 * (1.0 + EPS), -0.5 * EPS * EPS, ALU.mult, ALU.add)
                m.then_inc(self.s["ln_ve"], 1)

            def dve_guess(self, v, n, first):
                w = slice(0, 2 * SH if self.twice else SH)
                v.wait_ge(self.s["ln_ve"], n + 1)
                if not first:
                    v.wait_ge(self.last_bc, n)
                root_guess(v, self.w["ve"][:, w], self.w["rstd"][:, w], self.s["ln_root"], n)

            def steps(self, e, n, part=range(3)):
                w = slice(0, 2 * SH if self.twice else SH)
                root_steps(e, self.fused, self.w["ve"][:, w], self.w["rstd"][:, w], self.w["t"][:, w], self.s["ln_root"], self.NR * n, part)
                if 2 in part:
                    self.wide(e, n, 0)

            def wide(self, e, n, f):
                e.wait_ge(self.s["ln_root"], self.NR * n + self.NR - (2 if self.twice else 1))
                widen(e, self.w["wide"][:, f, :, :], self.w["rstd"][:, f * SH:(f + 1) * SH]).then_inc(self.s["ln_root"], 1)

            def pe_bcast(self, pe, n, roots=None):
                pe.wait_ge(self.s["ln_root"], roots or self.NR * n + self.NR - (1 if self.twice else 0))
                pe.matmul(self.bank[:, 0:T], bcast[:, :], self.w["wide"][:, 0, :, :].rearrange("p k j -> p (k j)"),
                          start=True, stop=True).then_inc(self.s["ln_bc"], 1)

            def dve_scale(self, v, n, first):
                if not first and not self.twice and not self.late:
                    v.wait_ge(self.s["ln_hi"], n)
                    v.wait_ge(self.s["ln_lo"], n)
                if not first and self.twice:
                    v.wait_ge(self.s["ln_res"], n)
                v.wait_ge(self.s["ln_bc"], n + 1)
                dst = self.w["z"] if self.twice else self.w["xn"]
                for c in range(KD):
                    m = v.tensor_tensor(dst[:, c, :], self.w["xc"][:, c, :], self.bank[:, 0:T], ALU.mult)
                m.then_inc(self.s["ln_z" if self.twice else "ln_xn"], 1)

            def pool_residual(self, p, cols, n):
                p.wait_ge(self.s["ln_z"], n + 1)
                p.tensor_tensor(hT[:, :, cols], hT[:, :, cols], self.w["z"][:, :, :], ALU.add).then_inc(self.s["ln_res"], 1)

            def pe_bcast2(self, pe, n):
                pe.wait_ge(self.s["ln_root"], self.NR * n + self.NR)
                pe.wait_ge(self.s["ln_z"], n + 1)
                pe.matmul(self.bank[:, 0:T], bcast[:, :], self.w["wide"][:, 1, :, :].rearrange("p k j -> p (k j)"),
                          start=True, stop=True).then_inc(self.s["ln_bc2"], 1)

            def dve_scale2(self, v, n, first):
                v.wait_ge(self.s["ln_bc2"], n + 1)
                if not first:
                    v.wait_ge(self.s["ln_hi"], n)
                    v.wait_ge(self.s["ln_lo"], n)
                for c in range(KD):
                    m = v.tensor_tensor(self.w["xn"][:, c, :], self.w["xc"][:, c, :], self.bank[:, 0:T], ALU.mult)
                m.then_inc(self.s["ln_x2"], 1)
                v.wait_ge(self.s["ln_x2"], n + 1)
                for c in range(KD):
                    m = v.tensor_scalar(self.w["xn"][:, c, :], self.w["xn"][:, c, :], vec1[:, 1, c:c + 1], vec1[:, 2, c:c + 1],
                                        ALU.mult, ALU.add)
                m.then_inc(self.s["ln_xn"], 1)

            def act_hi(self, a, cols, n):
                a.wait_ge(self.s["ln_xn"], n + 1)
                a.activation(xh[:, :, cols], self.w["xn"][:, :, :], ACT.Copy).then_inc(self.s["ln_hi"], 1)

            def pool_lo(self, p, cols, n):
                p.wait_ge(self.s["ln_hi"], n + 1)
                p.tensor_tensor(xl[:, :, cols], self.w["xn"][:, :, :], xh[:, :, cols], ALU.subtract).then_inc(self.s["ln_lo"], 1)

        def attention(layer):
            ph = ExitStack()
            first_layer = layer == 0
            NP = 3 if first_layer else 4
            KR = 64 + NP * DH
            KX = KR + 2 if first_layer else KR
            JJ = HC // 2
            PR = 4
            QK = 0 if first_layer else 1
            HIGH = 23 if first_layer else 5
            MEAN = 16 if first_layer else 15
            SPREAD = 26 if first_layer else 27
            VAL = 7 if first_layer else 6
            BACK = 11
            later = lambda i: not isinstance(i, int) or i >= 2
            LAG = 2 if first_layer else 3
            qc = sb(f"qc{layer}", [P, 4, T], scope=ph)
            qkh = sb(f"qkh{layer}", [P, 4, T], F16, ph)
            qkl = sb(f"qkl{layer}", [P, 4, T], F16, ph)
            pr = sb(f"pr{layer}", [SH, PR, JJ, T], scope=ph)
            rden = sb(f"rden{layer}", [P, 2, S], scope=ph)
            on = sb(f"on{layer}", [P, KD, T], scope=ph)
            oh = sb(f"oh{layer}", [P, KD, T], F16, ph)
            ol = sb(f"ol{layer}", [P, KD, T], F16, ph)
            if first_layer:
                qsq = sb("qsq", [P, 4, T], scope=ph)
                qve = sb("qve", [P, SH], scope=ph)
                qnt = sb("qnt", [P, SH], scope=ph)
                qrs = sb("qrs", [P, SH], scope=ph)
                qwide = sb("qwide", [P, 4, SH], scope=ph)
                mx = sb("mx", [SH, 2, 2, H], scope=ph)
                ml = sb("ml", [SH, 2, 2, 2, H], F16, ph)
                mt = sb("mt", [2 * H, 2, S], F16, ph)
            else:
                bo01 = sb("bo01", [P, KD], scope=ph)
                upd = sb("upd", [P, KD, T], scope=ph)
            bank = [ps(f"at{layer}{i}", [P, 512], scope=ph) for i in range(8)]
            dense, maxb, expb, avb = bank[0:2], bank[2:4], bank[4:6] if first_layer else bank[2:6], bank[6:8]
            ER = len(expb)
            bounce = nc.dram_tensor(f"bounce{layer}", (2, 2, 4, P, T), F16).ap()
            own = (("qsq", "qvar", "qve", "qroot", "qbc", "qn", "qa", "mm", "mx", "ml", "mt", "mtc", "mrow") if first_layer
                   else ("cl", "up", "bo", "prep", "zero", "wt", "wcp"))
            s = semaphores("w_in", "qk", "qc", "qhi", "qlo", "qout", "kout", "stk", "v", "vp", "sc", "ex", "av",
                           "rd", "on", "ohi", "olo", "pj", "h", *own)
            ln = Norm(dense[0], False, late=True)
            NS = 2 * H
            cols = lambda i: bass.ds(i * T, T)
            UPS = 2 * 2 * 6
            unit = lambda u: (u // 12, u // 6 % 2, u % 6 // 3, u % 3 * 3, 3 if u % 3 < 2 else 2)

            with nc.allow_non_contiguous_dma(reason="rows of a head"), nc.Block() as block:
                def low_qk(e, a):
                    for k in range(4):
                        e.wait_ge(s["qhi"], 4 * a + k + 1)
                        if not (isinstance(a, int) and a == 0):
                            e.wait_ge(s[("qout", "kout")[k // 2]], 32 * a)
                        e.tensor_tensor(qkl[:, k, :], qc[:, k, :], qkh[:, k, :], ALU.subtract).then_inc(s["qlo"], 1)

                @block.tensor
                def _(pe):
                    last = {}

                    def claim(b, sem, value):
                        if b in last:
                            pe.wait_ge(*last[b])
                        last[b] = (s[sem] if isinstance(sem, str) else sem, value)

                    def qk(a, k):
                        claim(k % 2, "qc", 4 * a + k + 1)
                        b = dense[k % 2]
                        n = 0
                        for wi, xi in ((0, xh), (1, xh), (0, xl)):
                            for c in range(KD):
                                m = pe.matmul(b[:, 0:T], wqkv[wi][:, c, k * P:(k + 1) * P], xi[:, c, cols(a)], start=(n == 0), stop=(n == 5))
                                n += 1
                        m.then_inc(s["qk"], 1)

                    def qvar(a):
                        pe.wait_ge(s["qsq"], 4 * a + 4)
                        claim(1, "qve", a + 1)
                        for k in range(4):
                            for j in range(4):
                                m = pe.matmul(dense[1][32 * j:32 * j + 32, 0:SH], head_mean[:, k, :], qsq[:, k, j * SH:(j + 1) * SH],
                                              start=(k == 0), stop=(k == 3))
                        m.then_inc(s["qvar"], 1)

                    def qbc(a, k):
                        pe.wait_ge(s["qroot"], ROOT_POOL * (a + 1))
                        b = (1, 0, 1, 0)[k]
                        claim(b, "qn", 4 * a + k + 1)
                        pe.matmul(dense[b][:, 0:T], head_back[:, k, :], qwide[:, :, :].rearrange("p j n -> p (j n)"),
                                  start=True, stop=True).then_inc(s["qbc"], 1)

                    def maxima(b, u, par):
                        bb, qt, hh, p0, n = unit(u)
                        if u == 0:
                            pe.wait_ge(s["stk"], 192 * (b + 1))
                        if not (isinstance(b, int) and b == 0 and u < 2):
                            pe.wait_ge(s["mx"], UPS * b + u - 1)
                        for x in range(n):
                            m = pe.matmul(maxb[u % 2][0:SH, x * S:(x + 1) * S],
                                          qs[par][hh][0:KR, p0 + x, bb * S + qt * SH:bb * S + (qt + 1) * SH],
                                          ks[par][0:KR, p0 + x, bb * S:(bb + 1) * S], start=True, stop=True)
                        m.then_inc(s["mm"], 1)

                    def turn_maxima(b, bb):
                        pe.wait_ge(s["ml"], 4 * b + 2 * bb + 2)
                        claim(1, "mtc", 2 * b + bb + 1)
                        for qt in range(2):
                            m = pe.transpose(dense[1].bitcast(F16)[0:2 * H, qt * SH:(qt + 1) * SH],
                                             ml[:, bb, qt, :, :].rearrange("p a b -> p (a b)"), ident16[0:SH, 0:SH])
                        m.then_inc(s["mt"], 1)

                    def values(b, bb, kt):
                        if kt == 0:
                            claim(1 - bb, "vp", 4 * b + 2 * bb + 2)
                        n = 0
                        for xi, wi in ((xh, 0), (xh, 1), (xl, 0)):
                            for c in range(KD):
                                m = pe.matmul(dense[1 - bb][0:SH, kt * D:(kt + 1) * D], xi[:, c, bass.ds(b * T + bb * S + kt * SH, SH)],
                                              wqkv[wi][:, c, 2 * D:3 * D], start=(n == 0), stop=(n == 5))
                                n += 1
                        if kt:
                            m.then_inc(s["v"], 1)

                    def scores(i, g, par):
                        t, jj = g // 4, g % 4
                        bb, c, hh = t // 4, t // 2 % 2, t % 2
                        if g % H == 0:
                            if first_layer:
                                pe.wait_ge(s["mrow"], 64 * (2 * i + bb + 1))
                            elif g == 0:
                                pe.wait_ge(s["stk"], 256 * (i + 1))
                        if not (isinstance(i, int) and NS * i + g < ER):
                            pe.wait_ge(s["ex" if first_layer else "cl"], NS * i + g - ER + 1)
                        for kt in range(2):
                            m = pe.matmul(expb[g % ER][0:SH, kt * S:(kt + 1) * S],
                                          ks[par][0:KX, c * JJ + jj, bb * S + kt * SH:bb * S + (kt + 1) * SH],
                                          qs[par][hh][0:KX, c * JJ + jj, bb * S:(bb + 1) * S], start=True, stop=True)
                        m.then_inc(s["sc"], 1)

                    def weighted(i, t, q, par):
                        bb, c, hh = t // 4, t // 2 % 2, t % 2
                        kt, sums = q // 2, q % 2
                        if q == 0:
                            pe.wait_ge(s["ex"], NS * i + 4 * t + 4 if first_layer else 8 * i + t + 1)
                            if t % 4 == 0:
                                pe.wait_ge(s["vp"], 4 * i + 2 * bb + 2)
                            if hh == 0 and not (isinstance(i, int) and 4 * i + 2 * bb + c - 1 <= 0):
                                pe.wait_ge(s["on"], 4 * i + 2 * bb + c - 1)
                        for jj in range(JJ):
                            lhs = onesv[:, hh, :] if sums else vp[par][:, bb, kt, c * JJ + jj, hh, :]
                            m = pe.matmul(avb[c][32 * jj:32 * jj + 32, sums * S:(sums + 1) * S], lhs,
                                          pr[:, t % PR, jj, kt * S:(kt + 1) * S], start=(hh == 0 and q == 0), stop=(hh == 1 and kt == 1),
                                          skip_group_check=True)
                        if q == 3:
                            m.then_inc(s["av"], 1)

                    def project(l, k):
                        pe.wait_ge(s["olo"], 4 * l + 4)
                        claim(1 - k, "h" if first_layer else "up", 2 * l + k + 1)
                        n = 0
                        for wi, oi in ((0, oh), (1, oh), (0, ol)):
                            for c in range(KD):
                                m = pe.matmul(dense[1 - k][:, 0:T], wpro[wi][:, c, k * P:(k + 1) * P], oi[:, c, :], start=(n == 0), stop=(n == 5))
                                n += 1
                        m.then_inc(s["pj"], 1)

                    def norm_mean(l):
                        pe.wait_ge(s["h"], 2 * l + 2)
                        claim(0, ln.s["ln_xc"], l + 1)
                        ln.pe_mean(pe, cols(l), l)

                    def norm_var(l):
                        claim(0, ln.s["ln_ve"], l + 1)
                        ln.pe_var(pe, l)

                    def norm_back(l):
                        claim(0, ln.done, l + 1)
                        ln.pe_bcast(pe, l)

                    def body(i, par, first, has_a, has_b):
                        a, b, l = i + 2, i + 1, i - 1
                        for g in range(NS):
                            scores(i, g, par)
                            t, q = divmod(g - 4 - LAG, 4)
                            if t >= 0:
                                weighted(i, t, q, par)
                            elif not first:
                                weighted(i - 1, 8 + t, q, 1 - par)
                            if first_layer and first and g < 6:
                                maxima(i, 3 * UPS // 4 + g, par)
                            if first_layer and g == 6:
                                turn_maxima(i, 1)
                            if has_a and g == QK:
                                for k in range(4):
                                    qk(a, k)
                            if has_b and VAL <= g < VAL + 4:
                                values(b, (g - VAL) // 2, (g - VAL) % 2)
                            if first_layer and has_b and 8 <= g < 8 + UPS:
                                maxima(b, g - 8, 1 - par)
                            if later(i) and g == BACK:
                                norm_back(i - 2)
                            if not first and g in (12, 13):
                                project(l, g - 12)
                            if first_layer and has_a and g == 11:
                                qvar(a)
                            if not first and g == MEAN:
                                norm_mean(l)
                            if not first and g == SPREAD:
                                norm_var(l)
                            if first_layer and has_b and g == 21:
                                turn_maxima(b, 0)
                            if first_layer and has_a and 22 <= g < 26:
                                qbc(a, g - 22)

                    def prologue():
                        if not first_layer:
                            for w in range(4):
                                for ci in range(KD):
                                    for co in range(KD):
                                        m = pe.transpose(bank[w][:, ci * D + co * P:ci * D + (co + 1) * P],
                                                         raw_att1[:, w, co, ci * P:(ci + 1) * P], ident[:, :])
                                m.then_inc(s["wt"], 1)
                            pe.wait_ge(s["prep"], 2)
                        for a in range(2):
                            for k in range(4):
                                qk(a, k)
                            if first_layer:
                                qvar(a)
                            if a == 0:
                                if not first_layer:
                                    pe.wait_ge(s["prep"], 4)
                                for bb in range(2):
                                    for kt in range(2):
                                        values(0, bb, kt)
                            if first_layer:
                                for k in range(4):
                                    qbc(a, k)
                        if first_layer:
                            for u in range(UPS // 2):
                                maxima(0, u, 0)
                            turn_maxima(0, 0)
                            for u in range(UPS // 2, 3 * UPS // 4):
                                maxima(0, u, 0)

                    def epilogue():
                        l = NT - 1
                        norm_back(l - 1)
                        for g in range(NS, NS + 4 + LAG):
                            t, q = divmod(g - 4 - LAG, 4)
                            weighted(l, t, q, l % 2)
                        for k in range(KD):
                            project(l, k)
                        norm_mean(l)
                        norm_var(l)
                        norm_back(l)

                    prologue()
                    for i in range(2):
                        body(i, i, i == 0, True, True)
                    steady = {0: (ln.s["ln_ve"], lambda i: i - 1),
                              1: (s["qn"], lambda i: 4 * i + 7) if first_layer else (s["up"], lambda i: 2 * i - 3)}
                    with pe.Fori(1, NT // 2 - 1, 1) as half:
                        for u in range(2):
                            i = half * 2
                            last.update({b: (sem, f(i + u)) for b, (sem, f) in steady.items()})
                            body(i + u, u, False, True, True)
                    for i in range(NT - 2, NT):
                        last.update({b: (sem, f(NT - 2)) for b, (sem, f) in steady.items()} if i == NT - 2 else {})
                        body(i, i % 2, False, False, i < NT - 1)
                    epilogue()

                @block.scalar
                def _(act):
                    def copy_qk(a, k):
                        act.wait_ge(s["qk"], 4 * a + k + 1)
                        if not (isinstance(a, int) and a == 0):
                            act.wait_ge(s["qlo"], 4 * a + k - 3)
                        scale = 1 / WS if first_layer else (0.5 * DH ** -0.5 if k < 2 else 1.0)
                        act.activation(qc[:, k, :], dense[k % 2][:, 0:T], ACT.Copy, scale=scale).then_inc(s["qc"], 1)

                    def high_qk(a, k):
                        if first_layer:
                            act.wait_ge(s["qn"], 4 * a + k + 1)
                            act.activation(qc[:, k, :], qc[:, k, :], ACT.Identity, bias=beta[:, k // 2:k // 2 + 1]).then_inc(s["qa"], 1)
                        act.wait_ge(s["qa" if first_layer else "qc"], 4 * a + k + 1)
                        if not (isinstance(a, int) and a == 0):
                            act.wait_ge(s[("qout", "kout")[k // 2]], 32 * a)
                        act.activation(qkh[:, k, :], qc[:, k, :], ACT.Copy).then_inc(s["qhi"], 1)

                    def exponentials(i, g):
                        t, jj = g // 4, g % 4
                        if first_layer:
                            act.wait_ge(s["sc"], NS * i + g + 1)
                            if jj == 0 and not (isinstance(i, int) and 8 * i + t - PR + 1 <= 0):
                                act.wait_ge(s["av"], 8 * i + t - PR + 1)
                            act.activation(pr[:, t % PR, jj, :], expb[g % ER][0:SH, 0:T], ACT.Exp, scale=DH ** -0.5).then_inc(s["ex"], 1)
                        elif jj == 3:
                            act.wait_ge(s["cl"], NS * i + g + 1)
                            act.activation(pr[:, t % PR, :, :], pr[:, t % PR, :, :], ACT.Exp).then_inc(s["ex"], 1)

                    def copy_values(b, bb, par, first2):
                        act.wait_ge(s["v"], 2 * b + bb + 1)
                        if bb == 0 and not first2:
                            act.wait_ge(s["av"], 8 * (b - 1))
                        src = dense[1 - bb][0:SH, :].rearrange("p (t g h d) -> p (t g) h d", t=2, h=2, d=DH)
                        dst = vp[par][:, bb, :, :, :, :].rearrange("p t g h d -> p (t g) h d")
                        for hh in range(2):
                            act.activation(dst[:, :, hh, hh * DH:(hh + 1) * DH], src[:, :, hh, :], ACT.Copy,
                                           scale=1 / WS if first_layer else 1.0).then_inc(s["vp"], 1)

                    def update1(l, k):
                        act.wait_ge(s["pj"], 2 * l + k + 1)
                        if not (isinstance(l, int) and l == 0):
                            act.wait_ge(s["h"], 2 * l)
                        act.activation(upd[:, k, :], dense[1 - k][:, 0:T], ACT.Identity, scale=0.1, bias=bo01[:, k:k + 1]).then_inc(s["up"], 1)

                    def high_out(i, n):
                        act.wait_ge(s["on"], 4 * i + n + 1)
                        if n == 0 and not (isinstance(i, int) and i == 0):
                            act.wait_ge(s["pj"], 2 * i)
                        bb, c = n // 2, n % 2
                        act.activation(oh[:, c, bb * S:(bb + 1) * S], on[:, c, bb * S:(bb + 1) * S], ACT.Copy).then_inc(s["ohi"], 1)

                    def body(i, par, first, has_a, has_b):
                        a, b, l = i + 2, i + 1, i - 1
                        for g in range(NS):
                            exponentials(i, g)
                            if has_a and g == QK:
                                for k in range(4):
                                    copy_qk(a, k)
                            if not first and g == 5 + LAG:
                                high_out(l, 3)
                            if has_b and g in (VAL + 1, VAL + 3):
                                copy_values(b, (g - VAL - 1) // 2, 1 - par, first)
                            if g in (15, 23, 31):
                                high_out(i, (g - 15) // 8)
                            if not first and g == MEAN + 2:
                                ln.act_square(act, l, isinstance(l, int) and l == 0)
                            if later(i) and g == BACK + 2:
                                ln.act_hi(act, cols(i - 2), i - 2)
                            if not first_layer and not first and g in (12, 13):
                                update1(l, g - 12)
                            if has_a and g - HIGH in range(4):
                                high_qk(a, g - HIGH)

                    if not first_layer:
                        act.wait_ge(s["bo"], 1)
                        for w in range(4):
                            act.wait_ge(s["wt"], w + 1)
                            dst = wqkv[0][:, :, w * D:(w + 1) * D] if w < 3 else wpro[0][:, :, :]
                            act.activation(dst, bank[w][:, :].rearrange("p (c n) -> p c n", c=KD), ACT.Copy).then_inc(s["wcp"], 1)
                    for a in range(2):
                        for k in range(4):
                            copy_qk(a, k)
                        if first_layer and a == 0:
                            for bb in range(2):
                                copy_values(0, bb, 0, True)
                        for k in range(4):
                            high_qk(a, k)
                        if not first_layer and a == 0:
                            for bb in range(2):
                                copy_values(0, bb, 0, True)
                    for i in range(2):
                        body(i, i, i == 0, True, True)
                    with act.Fori(1, NT // 2 - 1, 1) as half:
                        for u in range(2):
                            i = half * 2
                            body(i + u, u, False, True, True)
                    for i in range(NT - 2, NT):
                        body(i, i % 2, False, False, i < NT - 1)
                    l = NT - 1
                    ln.act_hi(act, cols(l - 1), l - 1)
                    high_out(l, 3)
                    if not first_layer:
                        for k in range(KD):
                            update1(l, k)
                    ln.act_square(act, l, False)
                    ln.act_hi(act, cols(l), l)

                @block.vector
                def _(v):
                    def q_variance(a):
                        v.wait_ge(s["qvar"], a + 1)
                        if not (isinstance(a, int) and a == 0):
                            v.wait_ge(s["qroot"], ROOT_POOL * a)
                        v.tensor_scalar(qve[:, :], dense[1][:, 0:SH], -0.5, -0.5 * EPS, ALU.mult, ALU.add).then_inc(s["qve"], 1)
                        v.wait_ge(s["qve"], a + 1)
                        if not (isinstance(a, int) and a == 0):
                            v.wait_ge(s["qbc"], 4 * a)
                        root_guess(v, qve[:, :], qrs[:, :], s["qroot"], a)

                    def scale_qk(a, k):
                        v.wait_ge(s["qbc"], 4 * a + k + 1)
                        v.tensor_tensor(qc[:, k, :], qc[:, k, :], dense[(1, 0, 1, 0)[k]][:, 0:T], ALU.mult).then_inc(s["qn"], 1)

                    def reduce_maxima(b, u):
                        bb, qt, hh, p0, n = unit(u)
                        v.wait_ge(s["mm"], UPS * b + u + 1)
                        v.tensor_reduce(mx[:, bb, qt, 8 * hh + p0:8 * hh + p0 + n],
                                        maxb[u % 2][0:SH, 0:n * S].rearrange("p (h k) -> p h k", h=n), AX.X, ALU.max).then_inc(s["mx"], 1)

                    def split_maxima(b, bb):
                        v.wait_ge(s["mx"], UPS * b + 12 * (bb + 1))
                        if not (isinstance(b, int) and b == 0):
                            v.wait_ge(s["mt"], 2 * b + bb - 1)
                        v.tensor_scalar(ml[:, bb, :, 0, :], mx[:, bb, :, :], -1.0, None, ALU.mult).then_inc(s["ml"], 1)
                        v.wait_ge(s["ml"], 4 * b + 2 * bb + 1)
                        v.scalar_tensor_tensor(out=ml[:, bb, :, 1, :], in0=mx[:, bb, :, :], scalar=-1.0, in1=ml[:, bb, :, 0, :],
                                               op0=ALU.mult, op1=ALU.subtract).then_inc(s["ml"], 1)

                    def copy_maxima(b, bb):
                        v.wait_ge(s["mt"], 2 * b + bb + 1)
                        if not (isinstance(b, int) and b == 0):
                            v.wait_ge(s["mrow"], 64 * (2 * b + bb - 1))
                        v.tensor_copy(mt[:, bb, :], dense[1].bitcast(F16)[0:2 * H, 0:S]).then_inc(s["mtc"], 1)

                    def clip(i, g):
                        t, jj = g // 4, g % 4
                        v.wait_ge(s["sc"], NS * i + g + 1)
                        if jj == 0 and not (isinstance(i, int) and 8 * i + t - PR + 1 <= 0):
                            v.wait_ge(s["av"], 8 * i + t - PR + 1)
                        v.tensor_scalar(pr[:, t % PR, jj, :], expb[g % ER][0:SH, 0:T], -10.0, 10.0, ALU.max, ALU.min).then_inc(s["cl"], 1)

                    def normalise(i, n):
                        bb, c = n // 2, n % 2
                        v.wait_ge(s["av"], 8 * i + 2 * n + 2)
                        v.reciprocal(rden[:, c, :], avb[c][:, S:2 * S]).then_inc(s["rd"], 1)
                        v.wait_ge(s["rd"], 4 * i + n + 1)
                        if not (isinstance(i, int) and i == 0):
                            v.wait_ge(s["olo"], 4 * i + n - 3)
                        v.tensor_tensor(on[:, c, bb * S:(bb + 1) * S], avb[c][:, 0:S], rden[:, c, :], ALU.mult).then_inc(s["on"], 1)

                    def update(l, k):
                        if first_layer:
                            v.wait_ge(s["pj"], 2 * l + k + 1)
                            v.scalar_tensor_tensor(out=hT[:, k, cols(l)], in0=dense[1 - k][:, 0:T], scalar=1 / WS, in1=hT[:, k, cols(l)],
                                                   op0=ALU.mult, op1=ALU.add).then_inc(s["h"], 1)
                        else:
                            v.wait_ge(s["up"], 2 * l + k + 1)
                            v.tensor_tensor(hT[:, k, cols(l)], hT[:, k, cols(l)], upd[:, k, :], ALU.add).then_inc(s["h"], 1)

                    def body(i, par, first, has_a, has_b):
                        a, b, l = i + 2, i + 1, i - 1
                        l0 = isinstance(l, int) and l == 0
                        for g in range(NS):
                            if not first_layer:
                                clip(i, g)
                            if first_layer and has_b and 8 <= g < 8 + UPS:
                                reduce_maxima(b, g - 8)
                            if first_layer and first and g < 6:
                                reduce_maxima(i, 3 * UPS // 4 + g)
                                if g == 5:
                                    split_maxima(i, 1)
                            if first_layer and g == 6:
                                copy_maxima(i, 1)
                            if not first and g == 4 + LAG:
                                normalise(l, 3)
                            if not first and g in (13, 14):
                                update(l, g - 13)
                            if g in (12 + LAG, 20 + LAG, 28 + LAG):
                                normalise(i, (g - 12 - LAG) // 8)
                            if first_layer and has_b and g == 19:
                                split_maxima(b, 0)
                            if not first and g == MEAN + 1:
                                ln.dve_center(v, cols(l), l, l0)
                            if not first and g == SPREAD:
                                ln.dve_ve(v, l, l0)
                                ln.dve_guess(v, l, l0)
                            if first_layer and has_a and g == 11:
                                q_variance(a)
                            if first_layer and has_b and g == 21:
                                copy_maxima(b, 0)
                            if later(i) and g == BACK + 1:
                                ln.dve_scale(v, i - 2, False)
                            if first_layer and has_a and 22 <= g < 26:
                                scale_qk(a, g - 22)
                            if first_layer and has_b and g == 31:
                                split_maxima(b, 1)

                    def widen_root(a):
                        v.wait_ge(s["qroot"], ROOT_POOL * (a + 1) - 1)
                        widen(v, qwide[:, :, :], qrs[:, :]).then_inc(s["qroot"], 1)

                    if not first_layer:
                        v.tensor_scalar(bo01[:, :], vec1[:, 0, :], 0.1, None, ALU.mult).then_inc(s["bo"], 1)
                        for w in range(4):
                            v.wait_ge(s["wcp"], w + 1)
                            lo = wqkv[1][:, :, w * D:(w + 1) * D] if w < 3 else wpro[1][:, :, :]
                            hi = wqkv[0][:, :, w * D:(w + 1) * D] if w < 3 else wpro[0][:, :, :]
                            v.tensor_tensor(lo, bank[w][:, :].rearrange("p (c n) -> p c n", c=KD), hi, ALU.subtract).then_inc(s["prep"], 1)
                    if first_layer:
                        for a in range(2):
                            q_variance(a)
                            root_steps(v, False, qve[:, :], qrs[:, :], qnt[:, :], s["qroot"], ROOT_POOL * a)
                            widen_root(a)
                            for k in range(4):
                                scale_qk(a, k)
                    else:
                        for a in range(2):
                            low_qk(v, a)
                    if first_layer:
                        for u in range(UPS // 2):
                            reduce_maxima(0, u)
                        split_maxima(0, 0)
                        copy_maxima(0, 0)
                        for u in range(UPS // 2, 3 * UPS // 4):
                            reduce_maxima(0, u)
                    for i in range(2):
                        body(i, i, i == 0, True, True)
                    with v.Fori(1, NT // 2 - 1, 1) as half:
                        for u in range(2):
                            i = half * 2
                            body(i + u, u, False, True, True)
                    for i in range(NT - 2, NT):
                        body(i, i % 2, False, False, i < NT - 1)
                    l = NT - 1
                    ln.dve_scale(v, l - 1, False)
                    normalise(l, 3)
                    for k in range(KD):
                        update(l, k)
                    ln.dve_center(v, cols(l), l, False)
                    ln.dve_ve(v, l, False)
                    ln.dve_guess(v, l, False)
                    ln.steps(v, l)
                    ln.dve_scale(v, l, False)

                @block.gpsimd
                def _(p):
                    def squares(a, k):
                        p.wait_ge(s["qc"], 4 * a + k + 1)
                        if not (isinstance(a, int) and a == 0):
                            p.wait_ge(s["qvar"], a)
                        p.tensor_tensor(qsq[:, k, :], qc[:, k, :], qc[:, k, :], ALU.mult).then_inc(s["qsq"], 1)

                    def low_out(i, n):
                        bb, c = n // 2, n % 2
                        p.wait_ge(s["ohi"], 4 * i + n + 1)
                        p.tensor_tensor(ol[:, c, bb * S:(bb + 1) * S], on[:, c, bb * S:(bb + 1) * S], oh[:, c, bb * S:(bb + 1) * S],
                                        ALU.subtract).then_inc(s["olo"], 1)

                    def q_root(a):
                        root_steps(p, False, qve[:, :], qrs[:, :], qnt[:, :], s["qroot"], ROOT_POOL * a)
                        p.wait_ge(s["qroot"], ROOT_POOL * (a + 1) - 1)
                        widen(p, qwide[:, :, :], qrs[:, :]).then_inc(s["qroot"], 1)

                    def body(i, first, has_a):
                        a, l = i + 2, i - 1
                        if first_layer and has_a:
                            for k in range(4):
                                squares(a, k)
                        if not first_layer and has_a:
                            low_qk(p, a)
                        if not first:
                            low_out(l, 3)
                        if first_layer and has_a:
                            q_root(a)
                        if later(i):
                            ln.pool_lo(p, cols(i - 2), i - 2)
                        low_out(i, 0)
                        low_out(i, 1)
                        if first_layer and has_a:
                            low_qk(p, a)
                        if not first:
                            ln.steps(p, l)
                        low_out(i, 2)

                    if not first_layer:
                        for par in range(2):
                            p.memset(qs[par][0][96:P, :, :].bitcast(I32), 0).then_inc(s["zero"], 1)
                    for a in range(2):
                        if first_layer:
                            for k in range(4):
                                squares(a, k)
                            low_qk(p, a)
                    for i in range(2):
                        body(i, i == 0, True)
                    with p.Fori(2, NT - 2, 1) as i:
                        body(i, False, True)
                    for i in range(NT - 2, NT):
                        body(i, False, False)
                    ln.pool_lo(p, cols(NT - 2), NT - 2)
                    low_out(NT - 1, 3)
                    ln.pool_lo(p, cols(NT - 1), NT - 1)

                @block.sync
                def _(sp):
                    nstk = 16 * 2 * 2 * NP
                    values = [sp.alloc_register(f"wait_a{layer}"), sp.alloc_register(f"wait_b{layer}")]

                    def hold(r, x):
                        if isinstance(x, int):
                            return x
                        sp.reg_mov(values[r], x)
                        return values[r]

                    def leave(a, par, first2):
                        for x in range(2):
                            split, free = hold(0, 4 * a + 2 * x + 2), None if first2 else hold(1, nstk * (a - 1))
                            sp.wait_ge(s["qlo"], split)
                            if not first2:
                                sp.wait_ge(s["stk"], free)
                            for part, src in enumerate((qkh, qkl)):
                                sp.dma_start(bounce[par, part, 2 * x:2 * x + 2].rearrange("k p t -> p k t"),
                                             src[:, 2 * x:2 * x + 2, :]).then_inc(s[("qout", "kout")[x]], 16)

                    def stack(b, par, first2):
                        for x in range(2):
                            there, free = hold(0, 32 * (b + 1)), None if first2 else hold(1, NS * (b - 1))
                            sp.wait_ge(s[("qout", "kout")[x]], there)
                            if not first2:
                                sp.wait_ge(s["sc"], free)
                            for part in range(NP):
                                low = ((0, 1, 0, 1), (0, 0, 1, 1))[x][part]
                                for hh in range(2):
                                    src = bounce[par, low, 2 * x:2 * x + 2].rearrange("c (j h d) t -> h d (c j) t", h=2, d=DH)[hh]
                                    dst = ks[par] if x else qs[par][hh]
                                    r = 64 * hh + DH * part
                                    sp.dma_start(dst[r:r + DH, :, :], src).then_inc(s["stk"], 16)

                    def maxima_rows(b, bb, par):
                        copied = hold(0, 2 * b + bb + 1)
                        sp.wait_ge(s["mtc"], copied)
                        for hh in range(2):
                            for part in range(2):
                                r = KR + part
                                sp.dma_start(qs[par][hh][r:r + 1, :, bb * S:(bb + 1) * S],
                                             mt[H * part + 8 * hh:H * part + 8 * hh + 8, bb, :]).then_inc(s["mrow"], 16)

                    def body(i, par, first, has_a, has_b):
                        a, b = i + 2, i + 1
                        if has_b:
                            stack(b, 1 - par, first)
                        if first_layer:
                            maxima_rows(i, 1, par)
                            if has_b:
                                maxima_rows(b, 0, 1 - par)
                        if has_a:
                            leave(a, par, False)

                    if first_layer:
                        for raw, w in ((raw_gate, w_gate), (raw_up, w_up), (raw_down, w_down)):
                            sp.dma_start(raw[:, :, :], w.rearrange("(c p) n -> p c n", p=P)).then_inc(s["w_in"], 16)
                    else:
                        sp.dma_start(raw_w1[:, :, :], w1.rearrange("(c p) n -> p c n", p=P)).then_inc(s["w_in"], 16)
                        sp.dma_start(raw_w2[:, :, :], w2.rearrange("(c p) n -> p c n", p=P)).then_inc(s["w_in"], 16)
                        sp.wait_ge(s["zero"], 2)
                    leave(0, 0, True)
                    stack(0, 0, True)
                    leave(1, 1, True)
                    if first_layer:
                        maxima_rows(0, 0, 0)
                    for i in range(2):
                        body(i, i, i == 0, True, True)
                    with sp.Fori(1, NT // 2 - 1, 1) as half:
                        for u in range(2):
                            i = half * 2
                            body(i + u, u, False, True, True)
                    for i in range(NT - 2, NT):
                        body(i, i % 2, False, False, i < NT - 1)
                    sp.wait_ge(s["qout"], 32 * NT)
                    sp.wait_ge(s["kout"], 32 * NT)
                    sp.wait_ge(s["w_in"], 48 if first_layer else 32)
            ph.close()

        def feed_forward(layer):
            ph = ExitStack()
            gated = layer == 0
            WIDE2 = 6
            M = K0 if gated else K1
            UR = 2 if gated else 4
            HR = M // 2
            NW = (3 if gated else 2) * KD * M
            assert M % UR == 0 and M % HR == 0
            Q = 1 / 127.0
            wt = sb(f"wt{layer}", [P, NW, P], F16, ph)
            w16 = sb(f"w16{layer}", [P, NW * P], F16, ph)
            hid = sb(f"hid{layer}", [P, 2, T], scope=ph)
            act_g = sb(f"act_g{layer}", [P, 2, T], scope=ph)
            hh = sb(f"hh{layer}", [P, HR, T], F16, ph)
            hl = sb(f"hl{layer}", [P, HR, T], F16, ph)
            if not gated:
                alpha1 = sb("alpha1", [P, K1], scope=ph)
                alpha2 = sb("alpha2", [P, KD], scope=ph)
                upd = sb("upd4", [P, KD, T], scope=ph)
                hf = sb("hf", [P, KD, T], scope=ph)
                ot = sb("ot", [SH, 4, D], scope=ph)
            bank = [ps(f"ff{layer}{i}", [P, 512], scope=ph) for i in range(8)]
            s = semaphores("cast", "turn", "wt", "alpha", "up", "hid", "hh", "hl", "dn", "h", *(("act", "att_in") if gated else ("upd", "tr", "ot", "out")))
            ln = Norm(bank[6], True, twice=True) if gated else None
            NB = -(-NW // 8)
            cols = lambda i: bass.ds(i * T, T)
            isz = lambda i: isinstance(i, int) and i == 0

            with nc.Block() as block:
                @block.tensor
                def _(pe):
                    def up(i, m):
                        n0 = M * i + m
                        if not (isinstance(i, int) and n0 < UR):
                            pe.wait_ge(s["hid"], n0 - UR + 1)
                        for g in range(2 if gated else 1):
                            n = 0
                            for x in (xh, xl):
                                for c in range(KD):
                                    mm = pe.matmul(bank[(2 if gated else 1) * (m % UR) + g][:, 0:T], wt[:, (g * KD + c) * M + m, :],
                                                   x[:, c, cols(i)], start=(n == 0), stop=(n == 3))
                                    n += 1
                        mm.then_inc(s["up"], 1)

                    def down(i, m):
                        pe.wait_ge(s["hl"], M * i + m + 1)
                        for k in range(KD):
                            if m == 0 and not isz(i):
                                pe.wait_ge(s["h" if gated else "upd"], 2 * i + k - 1)
                            for n, x in enumerate((hh, hl)):
                                mm = pe.matmul(bank[4 + k][:, 0:T], wt[:, (2 if gated else 1) * KD * M + m * KD + k, :],
                                               x[:, m % HR, :], start=(m == 0 and n == 0), stop=(m == M - 1 and n == 1))
                        mm.then_inc(s["dn"], 1)

                    def finish(l, m, first):
                        if gated:
                            if m == 2:
                                pe.wait_ge(s["h"], 2 * l + 2)
                                if not first:
                                    pe.wait_ge(ln.done, l)
                                ln.pe_mean(pe, cols(l), l)
                            if m == 3:
                                ln.pe_var(pe, l)
                            if m == M:
                                ln.pe_bcast(pe, l)
                            if m == M + 1:
                                ln.pe_bcast2(pe, l)
                        elif m == 3:
                            pe.wait_ge(s["h"], 2 * l + 2)
                            if not first:
                                pe.wait_ge(s["ot"], 2 * l)
                            for q in range(4):
                                for k in range(KD):
                                    mm = pe.transpose(bank[6 + q // 2][0:SH, (q % 2) * D + k * P:(q % 2) * D + (k + 1) * P],
                                                      hf[:, k, q * SH:(q + 1) * SH], ident[:, :])
                                if q % 2:
                                    mm.then_inc(s["tr"], 1)

                    def body(i, first, late=True):
                        for m in range(M):
                            up(i, m)
                            if m >= 2:
                                down(i, m - 2)
                            elif not first:
                                down(i - 1, M - 2 + m)
                            if late and m < 3:
                                finish(i - 2, M + m, isz(i - 2))
                            if not first:
                                finish(i - 1, m, isz(i - 1))

                    for b in range(NB):
                        for n in range(8 * b, min(NW, 8 * b + 8)):
                            w, r = divmod(n, KD * M)
                            if w < (2 if gated else 1):
                                c, m = divmod(r, M)
                                src = w16[:, (w * KD * M + m * KD + c) * P:(w * KD * M + m * KD + c + 1) * P]
                            else:
                                m, c = divmod(r, KD)
                                src = w16[:, (w * KD * M + c * M + m) * P:(w * KD * M + c * M + m + 1) * P]
                            pe.wait_ge(s["cast"], w + 1)
                            mm = pe.transpose(bank[b].bitcast(F16)[:, (n - 8 * b) * P:(n - 8 * b + 1) * P], src, ident16[:, :])
                        mm.then_inc(s["turn"], 1)
                    pe.wait_ge(s["wt"], NB)
                    body(0, True, False)
                    body(1, False, False)
                    body(2, False)
                    with pe.Fori(3, NT, 1) as i:
                        body(i, False)
                    for m in range(2):
                        down(NT - 1, M - 2 + m)
                    for m in range(3):
                        finish(NT - 2, M + m, False)
                    for m in range(M + 3):
                        finish(NT - 1, m, False)

                @block.scalar
                def _(a):
                    def nonlinear(i, m):
                        n0 = M * i + m
                        a.wait_ge(s["up"], n0 + 1)
                        if gated:
                            if not (isinstance(i, int) and n0 < 2):
                                a.wait_ge(s["hid"], n0 - 1)
                            a.activation(act_g[:, m % 2, :], bank[2 * (m % UR)][:, 0:T], ACT.Silu, scale=Q).then_inc(s["act"], 1)
                        else:
                            if not (isinstance(i, int) and n0 < 2):
                                a.wait_ge(s["hl"], n0 - 1)
                            a.activation(hid[:, m % 2, :], bank[m % UR][:, 0:T], ACT.Gelu, scale=alpha1[:, m:m + 1],
                                         bias=b1_sb[:, m:m + 1]).then_inc(s["hid"], 1)

                    def finish(l, m):
                        if gated:
                            if m == 3:
                                ln.act_square(a, l, isz(l))
                            if m == M + 2:
                                ln.act_hi(a, cols(l), l)
                        elif m in (4, 5):
                            a.wait_ge(s["tr"], 2 * l + m - 3)
                            if m == 4 and not isz(l):
                                a.wait_ge(s["out"], 16 * l)
                            a.activation(ot[:, 2 * (m - 4):2 * (m - 4) + 2, :],
                                         bank[6 + m - 4][0:SH, :].rearrange("p (q d) -> p q d", q=2), ACT.Copy).then_inc(s["ot"], 1)

                    def body(i, first, late=True):
                        for m in range(M):
                            nonlinear(i, m)
                            if late and m < 3:
                                finish(i - 2, M + m)
                            if not first:
                                finish(i - 1, m)

                    n1 = KD * M * P
                    if gated:
                        a.activation(w16[:, 0:n1], raw_gate[:, :, :].rearrange("p c n -> p (c n)"), ACT.Copy).then_inc(s["cast"], 1)
                    else:
                        a.activation(w16[:, 0:n1], raw_w1[:, :, :].rearrange("p c n -> p (c n)"), ACT.Sign).then_inc(s["cast"], 1)
                        a.activation(w16[:, n1:2 * n1], raw_w2[:, :, :].rearrange("p c n -> p (c n)"), ACT.Sign).then_inc(s["cast"], 1)
                        a.wait_ge(s["alpha"], 4)
                    body(0, True, False)
                    body(1, False, False)
                    body(2, False)
                    with a.Fori(3, NT, 1) as i:
                        body(i, False)
                    for m in range(3):
                        finish(NT - 2, M + m)
                    for m in range(M + 3):
                        finish(NT - 1, m)

                @block.vector
                def _(v):
                    def hidden(i, m):
                        n0 = M * i + m
                        if gated:
                            v.wait_ge(s["act"], n0 + 1)
                            if not (isinstance(i, int) and n0 < 2):
                                v.wait_ge(s["hl"], n0 - 1)
                            v.scalar_tensor_tensor(out=hid[:, m % 2, :], in0=bank[2 * (m % UR) + 1][:, 0:T], scalar=Q,
                                                   in1=act_g[:, m % 2, :], op0=ALU.mult, op1=ALU.mult).then_inc(s["hid"], 1)
                        v.wait_ge(s["hid"], n0 + 1)
                        if not (isinstance(i, int) and n0 < HR):
                            v.wait_ge(s["dn"], n0 - HR + 1)
                        v.tensor_copy(hh[:, m % HR, :], hid[:, m % 2, :]).then_inc(s["hh"], 1)

                    def finish(l, m):
                        if m == 1:
                            v.wait_ge(s["dn"], M * l + M)
                            for k in range(KD):
                                if gated:
                                    v.scalar_tensor_tensor(out=hT[:, k, cols(l)], in0=bank[4 + k][:, 0:T], scalar=Q, in1=hT[:, k, cols(l)],
                                                           op0=ALU.mult, op1=ALU.add).then_inc(s["h"], 1)
                                else:
                                    if k == 0 and not isz(l):
                                        v.wait_ge(s["tr"], 2 * l)
                                    v.tensor_scalar(upd[:, k, :], bank[4 + k][:, 0:T], alpha2[:, k:k + 1], vec1[:, 3, k:k + 1],
                                                    ALU.mult, ALU.add).then_inc(s["upd"], 1)
                            if not gated:
                                v.wait_ge(s["upd"], 2 * l + 2)
                                for k in range(KD):
                                    v.tensor_tensor(hf[:, k, :], hT[:, k, cols(l)], upd[:, k, :], ALU.add).then_inc(s["h"], 1)
                        if gated:
                            if m == 2:
                                ln.dve_center(v, cols(l), l, isz(l))
                            if m == 3:
                                ln.dve_ve(v, l, isz(l))
                                ln.dve_guess(v, l, isz(l))
                                ln.steps(v, l, range(0, 1))
                            if m in (4, 5):
                                ln.steps(v, l, range(m - 3, m - 2))
                            if m == WIDE2:
                                ln.wide(v, l, 1)
                            if m == M:
                                ln.dve_scale(v, l, isz(l))
                            if m == M + 1:
                                ln.dve_scale2(v, l, isz(l))

                    def body(i, first, late=True):
                        for m in range(M):
                            if gated and not first and m == 1:
                                finish(i - 1, m)
                            hidden(i, m)
                            if late and m < 3:
                                finish(i - 2, M + m)
                            if not first and not (gated and m == 1):
                                finish(i - 1, m)

                    n1 = KD * M * P
                    if gated:
                        v.tensor_copy(w16[:, n1:2 * n1], raw_up[:, :, :].rearrange("p c n -> p (c n)")).then_inc(s["alpha"], 1)
                        v.wait_ge(s["cast"], 1)
                        v.tensor_copy(w16[:, 2 * n1:3 * n1], raw_down[:, :, :].rearrange("p c n -> p (c n)")).then_inc(s["cast"], 2)
                    else:
                        v.tensor_reduce(alpha1[:, :], raw_w1[:, :, :], AX.X, ALU.add, apply_absolute_value=True).then_inc(s["alpha"], 1)
                        v.tensor_reduce(alpha2[:, :], raw_w2[:, :, :], AX.X, ALU.add, apply_absolute_value=True).then_inc(s["alpha"], 1)
                        v.wait_ge(s["alpha"], 2)
                        v.tensor_scalar(alpha1[:, :], alpha1[:, :], 1.0 / D, None, ALU.mult).then_inc(s["alpha"], 1)
                        v.tensor_scalar(alpha2[:, :], alpha2[:, :], 1.0 / F1, None, ALU.mult).then_inc(s["alpha"], 1)
                    for b in range(NB):
                        v.wait_ge(s["turn"], b + 1)
                        n = min(NW, 8 * b + 8) - 8 * b
                        v.tensor_copy(wt[:, 8 * b:8 * b + n, :], bank[b].bitcast(F16)[:, 0:n * P].rearrange("p (n q) -> p n q", q=P)).then_inc(s["wt"], 1)
                    if not gated:
                        v.wait_ge(s["alpha"], 4)
                    body(0, True, False)
                    body(1, False, False)
                    body(2, False)
                    with v.Fori(3, NT, 1) as i:
                        body(i, False)
                    for m in range(3):
                        finish(NT - 2, M + m)
                    for m in range(M + 3):
                        finish(NT - 1, m)

                @block.gpsimd
                def _(p):
                    def low(i, m):
                        n0 = M * i + m
                        p.wait_ge(s["hh"], n0 + 1)
                        p.tensor_tensor(hl[:, m % HR, :], hid[:, m % 2, :], hh[:, m % HR, :], ALU.subtract).then_inc(s["hl"], 1)

                    def finish(l, m):
                        if gated and m == M:
                            ln.pool_residual(p, cols(l), l)
                        if gated and m == M + 2:
                            ln.pool_lo(p, cols(l), l)

                    def body(i, first, late=True):
                        for m in range(M):
                            low(i, m)
                            if late and m < 3:
                                finish(i - 2, M + m)
                            if not first:
                                finish(i - 1, m)

                    body(0, True, False)
                    body(1, False, False)
                    body(2, False)
                    with p.Fori(3, NT, 1) as i:
                        body(i, False)
                    for m in range(3):
                        finish(NT - 2, M + m)
                    for m in range(M + 3):
                        finish(NT - 1, m)

                @block.sync
                def _(sp):
                    if gated:
                        for i, w in enumerate((wq1, wk1, wv1, wo1)):
                            sp.dma_start(raw_att1[:, i, :, :], w.rearrange("(c p) n -> p c n", p=P)).then_inc(s["att_in"], 16)
                        sp.wait_ge(s["att_in"], 64)
                    else:
                        rows = out.rearrange("b s d -> (b s) d")
                        with sp.Fori(0, NT, 1) as i:
                            row, filled = sp.snap(i * T), sp.snap(2 * i + 2)
                            sp.wait_ge(s["ot"], filled)
                            sp.dma_start(rows[bass.ds(row, T), :].rearrange("(q p) d -> p q d", p=SH), ot[:, :, :]).then_inc(s["out"], 16)
                        sp.wait_ge(s["out"], 16 * NT)
            ph.close()

        ph = ctx.enter_context(ExitStack())
        xs = sb("xs", [BH, C, PT, GW, PT], scope=ph)
        xn0 = sb("xn0", [BH, GW, C, PT, PT], scope=ph)
        stats = sb("stats", [BH, GW, C, 6], scope=ph)
        mv = sb("mv", [BH, GW, 2], scope=ph)
        rs0 = sb("rs0", [BH, GW], scope=ph)
        sd0 = sb("sd0", [BH, GW], scope=ph)
        xpT = sb("xpT", [P, KP, GW, BH], scope=ph)
        in_xh = xh[:, :, :].rearrange("p c n -> p (c n)").bitcast(F32)
        in_xl = xl[:, :, :].rearrange("p c n -> p (c n)").bitcast(F32)
        wm = in_xh[:, 0:KP * D].rearrange("p (a c n) -> p a c n", a=KP // C, c=C)
        trs = in_xh[:, KP * D:KP * D + NTI].rearrange("p (g n) -> p g n", g=2)
        tsd = [in_xh[:, KP * D + NTI:KP * D + NTI + NTI // 2], in_xl[:, 2 * KD * NTI:2 * KD * NTI + NTI // 2]]
        tk = in_xl[:, 0:KD * NTI].rearrange("p (c w n) -> p c w n", c=KD, w=GW)
        tsq = in_xl[:, KD * NTI:2 * KD * NTI].rearrange("p (g c n) -> p g c n", g=2, c=KD)
        gain = sb("gain", [P, 2, DH], scope=ph)
        heads = [lnw[k][:, :, :].rearrange("p c t -> p (c t)")[:, 0:4 * P].rearrange("p (k f) -> p k f", k=4) for k in ("xc", "sq", "xn", "z")]
        wmean = sb("wmean", [P, KD, 2 * H], scope=ph)
        tx = sb("tx", [ST, B, D], scope=ph)
        g1 = sb("g1", [P, KP // C, C], scope=ph)
        be1 = sb("be1", [P, KP // C, C], scope=ph)
        vec0 = sb("vec0", [P, 3, KD], scope=ph)
        pb = [ps(f"pb{i}", [P, 512], scope=ph) for i in range(8)]
        s = semaphores("x0", "x1", "x2", "gain", "wq_in", "wm", "wc", "wcp", "wlo", "zero_q", "zero",
                       "tok_in", "txt_in", "w_in", "bcast", "cst", "stats", "mv", "sd", "rstd", "xn",
                       "tr", "xp", "mlp", "tk", "mean", "txc", "tsq", "var", "tsd", "trs", "tnx", "h_img", "ttr", "h_txt")
        half = NTI // 2
        big = KD * T
        flat = tx[:, :, :].rearrange("p b d -> p (b d)")
        more = [sb(f"ln_more{q}", [P, KD, T], scope=ph)[:, :, :] for q in range(2)]
        places = [lnw[k][:, :, :] for k in ("xc", "sq", "xn", "z")] + more
        places += [flat[:, q * big:(q + 1) * big].rearrange("p (c t) -> p c t", c=KD) for q in range(NT + 4 - len(places))]
        spread = [sb(f"lns_{k}", [P, NT, SH], scope=ph) for k in ("ve", "rstd")]
        wide = [places[NT + q // 2].rearrange("p c t -> p (c t)")[:, q % 2 * T:(q % 2 + 1) * T].rearrange("p (f k j) -> p f k j", f=1, k=4)
                for q in range(NT)]
        lns = []
        for q in range(NT):
            lns.append(Norm(pb[q], True, work={"xc": places[q], "xn": places[q], "sq": places[NT + q % 4],
                                               "ve": spread[0][:, q, :], "rstd": spread[1][:, q, :], "wide": wide[q]}, s=lns[0].s if q else None))
        tile_cols = lambda q: bass.ds(q * T, T)
        assert NT == len(pb) and ST == P
        with nc.allow_non_contiguous_dma(reason="small vectors"), nc.Block() as block:
            @block.sync
            def _(sp):
                for c in range(C):
                    sp.dma_start(xs[:, c, :, :, :].rearrange("n p w q -> n (p w q)"),
                                 x[:, c].rearrange("b (h p) w -> b h (p w)", p=PT)).then_inc(s[f"x{c}"], 16)
                for i, v in enumerate((q_gamma, k_gamma)):
                    sp.dma_start(gain[:, i, :], v.rearrange("(a d) -> a d", a=1).to_broadcast([P, DH])).then_inc(s["gain"], 16)
                sp.dma_start(raw_qkv[:, :, :], w_qkv.rearrange("(c p) n -> p c n", p=P)).then_inc(s["wq_in"], 16)
                sp.dma_start(raw_proj[:, :, :], w_proj.rearrange("(c p) n -> p c n", p=P)).then_inc(s["wq_in"], 16)
                sp.dma_start(wm[:, :, :, :], tok_w.rearrange("(a p c) n -> p a c n", a=KP // C, c=C)).then_inc(s["tok_in"], 16)
                sp.dma_start(g1[:, :, :], tok_g1.rearrange("(a p c) -> p a c", a=KP // C, c=C)).then_inc(s["tok_in"], 16)
                sp.dma_start(be1[:, :, :], tok_b1.rearrange("(a p c) -> p a c", a=KP // C, c=C)).then_inc(s["tok_in"], 16)
                for i, v in enumerate((tok_bias, tok_g2, tok_b2)):
                    sp.dma_start(vec0[:, i, :], v.rearrange("(c p) -> p c", p=P)).then_inc(s["tok_in"], 16)
                for q in range(4):
                    b0, b9 = q * B // 4, (q + 1) * B // 4
                    sp.dma_start(tx[:, b0:b9, :], txt[b0:b9].rearrange("b t d -> t b d")).then_inc(s["txt_in"], 16)
                for i, v in enumerate((bo1, ln_gamma, ln_beta, b2)):
                    sp.dma_start(vec1[:, i, :], v.rearrange("(c p) -> p c", p=P)).then_inc(s["w_in"], 16)
                sp.dma_start(b1_sb[:, :], b1.rearrange("(c p) -> p c", p=P)).then_inc(s["w_in"], 16)
                for i, v in enumerate((q_beta, k_beta)):
                    for h in range(HC):
                        sp.dma_start(beta[h * DH:(h + 1) * DH, i:i + 1], v.rearrange("(p a) -> p a", a=1)).then_inc(s["w_in"], 16)
                sp.wait_ge(s["w_in"], 16 * (5 + 2 * HC))

            @block.gpsimd
            def _(p):
                p.memset(ident[:, :], 0.0).then_inc(s["cst"], 1)
                p.wait_ge(s["cst"], 1)
                p.affine_select(out=ident[:, :], in_=ident[:, :], compare_op=ALU.not_equal, fill=1.0, base=0,
                                pattern=[[-1, P]], channel_multiplier=1).then_inc(s["cst"], 1)
                p.wait_ge(s["cst"], 2)
                p.tensor_copy(ident16[:, :], ident[:, :]).then_inc(s["cst"], 1)
                p.memset(ones_d[:, :], 1.0 / D).then_inc(s["cst"], 1)
                p.memset(three_halves[:, :], 1.5).then_inc(s["cst"], 1)
                p.memset(eps_tok[:, :], EPS_TOK).then_inc(s["cst"], 1)
                for j in range(4):
                    p.memset(heads[j], 1.0).then_inc(s["cst"], 1)
                p.memset(head_mean[:, :, :], 1.0 / DH).then_inc(s["cst"], 1)
                p.wait_ge(s["cst"], 11)
                for j in range(4):
                    p.affine_select(out=heads[j], in_=heads[j], compare_op=ALU.is_ge, fill=0.0,
                                    base=32 * DH * j, pattern=[[HC * DH, 4], [1, P]], channel_multiplier=-DH).then_inc(s["cst"], 1)
                p.affine_select(out=head_mean[:, :, :], in_=head_mean[:, :, :], compare_op=ALU.is_ge, fill=0.0,
                                base=0, pattern=[[HC * DH, 4], [-DH, 32]], channel_multiplier=1).then_inc(s["cst"], 1)
                p.wait_ge(s["cst"], 16)
                for j in range(4):
                    p.affine_select(out=heads[j], in_=heads[j], compare_op=ALU.is_ge, fill=0.0,
                                    base=DH - 1 - 32 * DH * j, pattern=[[-HC * DH, 4], [-1, P]], channel_multiplier=DH).then_inc(s["cst"], 1)
                p.affine_select(out=head_mean[:, :, :], in_=head_mean[:, :, :], compare_op=ALU.is_ge, fill=0.0,
                                base=DH - 1, pattern=[[-HC * DH, 4], [DH, 32]], channel_multiplier=-1).then_inc(s["cst"], 1)
                for j in range(1, 4):
                    p.wait_ge(s["cst"], 20 + j)
                    p.tensor_tensor(head_back[:, :, :], heads[0] if j == 1 else head_back[:, :, :], heads[j], ALU.add).then_inc(s["cst"], 1)
                p.wait_ge(s["cst"], 24)
                p.wait_ge(s["gain"], 32)
                for k in range(4):
                    hb = head_back[:, k, :].rearrange("p (h d) -> p h d", d=DH)
                    p.tensor_tensor(hb, hb, gain[:, k // 2, :].unsqueeze(1).to_broadcast([P, HC, DH]), ALU.mult).then_inc(s["cst"], 1)
                p.wait_ge(s["cst"], 28)
                n = 0
                for par in range(2):
                    for buf, r0, r9 in ((qs[par][0], 32, 64), (qs[par][0], 64, P), (qs[par][1], 0, 64), (qs[par][1], 96, P),
                                        (ks[par], 32, 64)):
                        if n:
                            p.wait_ge(s["zero_q"], n)
                        p.memset(buf[r0:r9, :, :].bitcast(I32), 0).then_inc(s["zero_q"], 1)
                        n += 1
                    p.wait_ge(s["zero_q"], n)
                    p.memset(ks[par][96:P, :, :], 1.0).then_inc(s["zero_q"], 1)
                    n += 1
                p.wait_ge(s["zero_q"], n)
                p.memset(vp[1][:, :, :, :, :, :], 0.0).then_inc(s["zero_q"], 1)
                p.wait_ge(s["zero_q"], n + 1)

                for q in range(NT):
                    lns[q].pool_lo(p, tile_cols(q), q)

            @block.vector
            def _(v):
                v.memset(bcast[:, :], 1.0 / 32).then_inc(s["bcast"], 1)
                v.memset(spread_in[:, :, :], 0.0).then_inc(s["bcast"], 1)
                v.wait_ge(s["bcast"], 2)
                for k in range(4):
                    v.memset(spread_in[32 * k:32 * k + 32, k, :], 1.0).then_inc(s["bcast"], 1)
                v.memset(vp[0][:, :, :, :, :, :], 0.0).then_inc(s["zero"], 1)
                v.memset(onesv[:, :, :], 0.0).then_inc(s["bcast"], 1)
                v.wait_ge(s["bcast"], 7)
                for hh in range(2):
                    v.memset(onesv[:, hh, hh * DH:(hh + 1) * DH], 1.0).then_inc(s["bcast"], 1)
                for c in range(C):
                    v.wait_ge(s[f"x{c}"], 16)
                    for w in range(GW):
                        m = v.bn_stats(stats[:, w, c, :], xs[:, c, :, w, :])
                        if c == C - 1:
                            m.then_inc(s["stats"], 1)
                for w in range(GW):
                    v.wait_ge(s["stats"], w + 1)
                    v.bn_aggr(mv[:, w, :], stats[:, w, :, :]).then_inc(s["mv"], 1)
                v.wait_ge(s["sd"], 1)
                v.reciprocal(rs0[:, :], sd0[:, :]).then_inc(s["rstd"], 1)
                v.wait_ge(s["rstd"], 1)
                for w in range(GW):
                    for c in range(C):
                        m = v.tensor_scalar(xn0[:, w, c, :, :], xs[:, c, :, w, :], mv[:, w, 0:1], rs0[:, w:w + 1],
                                            ALU.subtract, ALU.mult)
                    m.then_inc(s["xn"], 1)
                v.wait_ge(s["tok_in"], 16 * 6)
                for k in range(KP):
                    for g in range(2):
                        v.wait_ge(s["tr"], 2 * k + g + 1)
                        c, a = k % C, k // C
                        v.tensor_scalar(xpT[:, k, g * 3:g * 3 + 3, :], pb[(2 * k + g) % 4][:, 0:3 * BH].rearrange("p (w n) -> p w n", w=3),
                                        g1[:, a, c:c + 1], be1[:, a, c:c + 1], ALU.mult, ALU.add).then_inc(s["xp"], 1)
                v.wait_ge(s["wq_in"], 32)
                w3 = raw_qkv[:, :, 0:2 * D].rearrange("p c (h d) -> p c h d", d=DH)
                for c in range(KD):
                    m = v.tensor_reduce(wmean[:, c, :], w3[:, c], AX.X, ALU.add)
                m.then_inc(s["wm"], 1)
                v.wait_ge(s["wm"], 1)
                v.tensor_scalar(wmean[:, :, :], wmean[:, :, :], 1 / DH, None, ALU.mult).then_inc(s["wm"], 1)
                v.wait_ge(s["wm"], 2)
                for c in range(KD):
                    m = v.tensor_tensor(w3[:, c], w3[:, c], wmean[:, c, :].unsqueeze(2).to_broadcast([P, 2 * H, DH]), ALU.subtract)
                m.then_inc(s["wc"], 1)
                tg = [tk[:, :, g * 3:g * 3 + 3, :].rearrange("p c w n -> p c (w n)") for g in range(2)]
                for g in range(2):
                    for c in range(KD):
                        v.wait_ge(s["mlp"], 2 * g + c + 1)
                        v.tensor_scalar(tg[g][:, c, :], pb[4 * g + c][:, 0:half], vec0[:, 0, c:c + 1], None, ALU.add).then_inc(s["tk"], 1)
                for g in range(2):
                    v.wait_ge(s["mean"], g + 1)
                    v.wait_ge(s["tk"], 2 * g + 2)
                    for c in range(KD):
                        m = v.tensor_tensor(tg[g][:, c, :], tg[g][:, c, :], pb[4 * g + 2][:, 0:half], ALU.subtract)
                    m.then_inc(s["txc"], 1)
                v.wait_ge(s["wcp"], 3)
                for c in range(KD):
                    for lo, hi, src in ((wqkv[1], wqkv[0], raw_qkv), (wpro[1], wpro[0], raw_proj)):
                        v.scalar_tensor_tensor(out=lo[:, c, :], in0=src[:, c, :], scalar=WS, in1=hi[:, c, :],
                                               op0=ALU.mult, op1=ALU.subtract).then_inc(s["wlo"], 1)
                for g in range(2):
                    v.wait_ge(s["tsd"], g + 1)
                    v.reciprocal(trs[:, g, :], tsd[g]).then_inc(s["trs"], 1)
                for g in range(2):
                    v.wait_ge(s["trs"], g + 1)
                    for c in range(KD):
                        m = v.tensor_tensor(tg[g][:, c, :], tg[g][:, c, :], trs[:, g, :], ALU.mult)
                    m.then_inc(s["tnx"], 1)
                for g in range(2):
                    v.wait_ge(s["tnx"], g + 1)
                    for c in range(KD):
                        for w in range(g * 3, g * 3 + 3):
                            dst = hT[:, c, :].rearrange("p (b s) -> p b s", b=B)[:, :, w:NI:GW]
                            m = v.tensor_scalar(dst, tk[:, c, w, :].rearrange("p (b h) -> p b h", b=B),
                                                vec0[:, 1, c:c + 1], vec0[:, 2, c:c + 1], ALU.mult, ALU.add)
                    m.then_inc(s["h_img"], 1)
                v.wait_ge(s["h_img"], 2)
                v.wait_ge(s["h_txt"], B)
                v.wait_ge(s["cst"], 24)

                for q in range(NT):
                    lns[q].dve_center(v, tile_cols(q), q, True)
                for q in range(NT):
                    lns[q].dve_ve(v, q, True)
                v.wait_ge(lns[0].s["ln_ve"], NT)
                ve, rstd = (x[:, :, :].rearrange("p q j -> p (q j)") for x in spread)
                root_guess(v, ve, rstd, lns[0].s["ln_root"], 0)
                root_steps(v, True, ve, rstd, places[NT + 3].rearrange("p c t -> p (c t)"), lns[0].s["ln_root"], 0)
                v.wait_ge(lns[0].s["ln_root"], ROOT_DVE - 1)
                for q in range(NT + 1):
                    if q < NT:
                        widen(v, lns[q].w["wide"][:, 0, :, :], lns[q].w["rstd"]).then_inc(lns[0].s["ln_root"], 1)
                    if q:
                        lns[q - 1].dve_scale(v, q - 1, True)

            @block.scalar
            def _(a):
                a.wait_ge(s["cst"], 6)
                a.wait_ge(s["mv"], GW)
                a.activation(sd0[:, :], mv[:, :, 1], ACT.Sqrt, bias=eps_tok[0:BH, 0:1]).then_inc(s["sd"], 1)
                a.wait_ge(s["wq_in"], 32)
                a.activation(wqkv[0][:, :, 2 * D:], raw_qkv[:, :, 2 * D:], ACT.Copy, scale=WS).then_inc(s["wcp"], 1)
                a.activation(wpro[0][:, :, :], raw_proj[:, :, :], ACT.Copy, scale=WS).then_inc(s["wcp"], 1)
                for b in range(B):
                    a.wait_ge(s["ttr"], b + 1)
                    a.activation(hT[:, :, b * S + NI:(b + 1) * S],
                                 pb[6 + b % 2][:, 0:KD * ST].rearrange("p (c t) -> p c t", c=KD), ACT.Copy).then_inc(s["h_txt"], 1)
                a.wait_ge(s["wc"], 1)
                a.activation(wqkv[0][:, :, 0:2 * D], raw_qkv[:, :, 0:2 * D], ACT.Copy, scale=WS).then_inc(s["wcp"], 1)
                for g in range(2):
                    a.wait_ge(s["txc"], g + 1)
                    a.activation(tsq[:, g, :, :], tk[:, :, g * 3:g * 3 + 3, :].rearrange("p c w n -> p c (w n)"), ACT.Square).then_inc(s["tsq"], 1)
                for g in range(2):
                    a.wait_ge(s["var"], g + 1)
                    a.activation(tsd[g], pb[4 * g + 2][:, 0:half], ACT.Sqrt, bias=eps_tok[:, 0:1]).then_inc(s["tsd"], 1)

                for q in range(NT):
                    if q >= 4:
                        a.wait_ge(lns[0].s["ln_var"], q - 3)
                    lns[q].act_square(a, q, True)
                for q in range(NT):
                    lns[q].act_hi(a, tile_cols(q), q)

            @block.tensor
            def _(pe):
                pe.wait_ge(s["cst"], 6)
                def text(b):
                    if b >= 2:
                        pe.wait_ge(s["h_txt"], b - 1)
                    for c in range(KD):
                        m = pe.transpose(pb[6 + b % 2][:, c * ST:(c + 1) * ST], tx[:, b, c * P:(c + 1) * P], ident[0:ST, 0:ST])
                    m.then_inc(s["ttr"], 1)
                pe.wait_ge(s["txt_in"], 16 * 4)
                for b in range(B // 2):
                    text(b)
                for k in range(KP):
                    c, a = k % C, k // C
                    for g in range(2):
                        j = 2 * k + g
                        pe.wait_ge(s["xn"], g * 3 + 3)
                        if j >= 4:
                            pe.wait_ge(s["xp"], j - 3)
                        for w in range(3):
                            m = pe.transpose(pb[j % 4][:, w * BH:(w + 1) * BH],
                                             xn0[:, g * 3 + w, c, a * 8:(a + 1) * 8, :].rearrange("n p q -> n (p q)"), ident[0:BH, 0:BH])
                        m.then_inc(s["tr"], 1)
                for b in range(B // 2, B):
                    text(b)
                pe.wait_ge(s["xp"], 2 * KP)
                for g in range(2):
                    for n in range(KD):
                        for k in range(KP):
                            c, a = k % C, k // C
                            m = pe.matmul(pb[4 * g + n][:, 0:half], wm[:, a, c, n * P:(n + 1) * P],
                                          xpT[:, k, g * 3:g * 3 + 3, :].rearrange("p w n -> p (w n)"), start=(k == 0), stop=(k == KP - 1))
                        m.then_inc(s["mlp"], 1)
                pe.wait_ge(s["h_txt"], B)
                for g in range(2):
                    pe.wait_ge(s["tk"], 2 * g + 2)
                    for c in range(KD):
                        m = pe.matmul(pb[4 * g + 2][:, 0:half], ones_d[:, :], tk[:, c, g * 3:g * 3 + 3, :].rearrange("p w n -> p (w n)"),
                                      start=(c == 0), stop=(c == KD - 1))
                    m.then_inc(s["mean"], 1)
                for g in range(2):
                    pe.wait_ge(s["tsq"], g + 1)
                    for c in range(KD):
                        m = pe.matmul(pb[4 * g + 2][:, 0:half], ones_d[:, :], tsq[:, g, c, :], start=(c == 0), stop=(c == KD - 1))
                    m.then_inc(s["var"], 1)
                pe.wait_ge(s["h_img"], 2)

                for q in range(NT):
                    lns[q].pe_mean(pe, tile_cols(q), q)
                    if q:
                        lns[q - 1].pe_var(pe, q - 1)
                lns[NT - 1].pe_var(pe, NT - 1)
                pe.wait_ge(s["bcast"], 1)
                for q in range(NT):
                    lns[q].pe_bcast(pe, q, ROOT_DVE + q)
        ph.close()
        weights0 = ctx.enter_context(ExitStack())
        raw_gate = sb("raw_gate", [P, K0, D], I32, scope=weights0)
        raw_up = sb("raw_up", [P, K0, D], I32, scope=weights0)
        raw_down = sb("raw_down", [P, KD, F0], I32, scope=weights0)
        attention(0)
        feed_forward(0)
        end_phase()
        weights0.close()
        raw_w1 = sb("raw_w1", [P, K1, D])
        raw_w2 = sb("raw_w2", [P, KD, F1])
        attention(1)
        feed_forward(1)


_INS = ['x', 'txt', 'L0_tok_g1', 'L0_tok_b1', 'L0_tok_W_mlp', 'L0_tok_b_mlp', 'L0_tok_g2', 'L0_tok_b2',
        'L0_attn_w_qkv', 'L0_attn_w_proj', 'L0_attn_q_gamma', 'L0_attn_q_beta', 'L0_attn_k_gamma', 'L0_attn_k_beta',
        'L0_ffn_w_gate', 'L0_ffn_w_up', 'L0_ffn_w_down', 'L1_attn_Wq', 'L1_attn_Wk', 'L1_attn_Wv', 'L1_attn_Wo',
        'L1_attn_bo', 'L1_attn_ln_gamma', 'L1_attn_ln_beta', 'L1_ffn_w1', 'L1_ffn_b1', 'L1_ffn_w2', 'L1_ffn_b2']


def kernel(**inputs):
    import numpy as _np
    import concourse.bacc as _bacc
    from concourse import mybir as _mybir
    from concourse.bass_utils import run_bass_kernel_spmd as _run

    nc = _bacc.Bacc("TRN2", target_bir_lowering=False, num_devices=1)
    arrays, args = {}, []
    for name in _INS:
        a = _np.ascontiguousarray(inputs[name])
        arrays[f"in_{name}"] = a
        args.append(nc.dram_tensor(f"in_{name}", a.shape, _mybir.dt.from_np(a.dtype), kind="ExternalInput").ap())
    shape = (inputs['x'].shape[0], (inputs['x'].shape[2] // 16) * (inputs['x'].shape[3] // 16) + inputs['txt'].shape[1],
             inputs['txt'].shape[2])
    args.append(nc.dram_tensor("out0", shape, _mybir.dt.float32, kind="ExternalOutput").ap())
    fused_block(nc, *args)
    r = _run(nc, [arrays], core_ids=[0])
    return r.results[0]["out0"]
```
